# Optimizing a Trainium2 kernel written in Bass

```python
import numpy as np
import jax
import jax.numpy as jnp

def _softmax(x, axis=-1):
    return jax.nn.softmax(x, axis=axis)

def _gelu(x):
    return jax.nn.gelu(x, approximate=True)

def _silu(x):
    return jax.nn.silu(x)

def _sigmoid(x):
    return jax.nn.sigmoid(x)

def _layernorm(x, axis=-1, eps=1e-05):
    m = jnp.mean(x, axis=axis, keepdims=True)
    v = jnp.var(x, axis=axis, keepdims=True)
    return (x - m) / jnp.sqrt(v + eps)

def _scatter_add(tgt, idx, src, axis=0):
    return tgt.at[idx].add(src)

def _segment_sum(src, seg, n):
    return jax.ops.segment_sum(src, seg, n)
kernel_name = 'mk_gnn_ffn_d1_gnn_r32_0c6442'

def setup_inputs(seed: int=0):
    np.random.seed(seed)
    _w = jnp.asarray

    def _rec_inputs():
        import jax
        import jax.numpy as jnp
        _gk = jax.random.key(seed)
        x = -0.0002117 + 1 * jax.random.normal(jax.random.fold_in(_gk, 1), (3125, 256), jnp.float32)
        _s = jax.random.randint(jax.random.fold_in(_gk, 2), (25000,), 0, 3125, jnp.int32)
        _d = jax.random.randint(jax.random.fold_in(_gk, 3), (25000,), 0, 3125, jnp.int32)
        _loop = jnp.arange(3125, dtype=jnp.int32)
        src = jnp.concatenate([_s, _d, _loop])
        dst = jnp.concatenate([_d, _s, _loop])
        _o = jnp.argsort(dst, stable=True)
        src = src[_o]
        dst = dst[_o]
        return (x, src, dst)
    x, src, dst = _rec_inputs()

    def _L0_gnn_setup():
        import jax, jax.numpy as jnp
        import numpy as np
        N = 3125
        E = 50000
        IN = 256
        H = 4
        C = 64
        key = jax.random.key(seed)
        k1, k2, k3, k4, k5, k6 = jax.random.split(key, 6)
        x = jax.random.normal(k1, (N, IN), dtype=jnp.float32)
        edge_index = jax.random.randint(k2, (2, E), 0, N, dtype=jnp.int64)
        W = jax.random.normal(k3, (IN, H * C), dtype=jnp.float32) * (1.0 / np.sqrt(IN))
        att_src = jax.random.normal(k4, (H, C), dtype=jnp.float32) * 0.1
        att_dst = jax.random.normal(k5, (H, C), dtype=jnp.float32) * 0.1
        bias = jax.random.normal(k6, (H * C,), dtype=jnp.float32) * 0.01
        return {'x': x, 'edge_index': edge_index, 'W': W, 'att_src': att_src, 'att_dst': att_dst, 'bias': bias}
    _L0_gnn_all = _L0_gnn_setup()
    _L0_gnn_in = {k: v for k, v in _L0_gnn_all.items() if k in ('W', 'att_src', 'att_dst', 'bias')}
    del _L0_gnn_all

    def _L0_ffn_setup():
        import jax, jax.numpy as jnp
        import numpy as np
        DIM = 256
        H = 8
        D = 64
        G = 64
        INNER = H * D
        SCALE = D ** (-0.5)
        key = jax.random.key(seed)
        ks = jax.random.split(key, 12)
        B, N = (4, 512)
        x = jax.random.normal(ks[0], (B, N, DIM), dtype=jnp.float32)
        s = lambda fan_in: 1.0 / np.sqrt(fan_in)
        W_fx = jax.random.normal(ks[1], (DIM, INNER), dtype=jnp.float32) * s(DIM)
        b_fx = jnp.zeros((INNER,), dtype=jnp.float32)
        W_x = jax.random.normal(ks[2], (DIM, INNER), dtype=jnp.float32) * s(DIM)
        b_x = jnp.zeros((INNER,), dtype=jnp.float32)
        A = jax.random.normal(ks[3], (G, D), dtype=jnp.float32)
        Q, _ = jnp.linalg.qr(A.T)
        W_slice = Q[:, :G].astype(jnp.float32)
        b_slice = jnp.zeros((G,), dtype=jnp.float32)
        W_q = jax.random.normal(ks[4], (D, D), dtype=jnp.float32) * s(D)
        W_k = jax.random.normal(ks[5], (D, D), dtype=jnp.float32) * s(D)
        W_v = jax.random.normal(ks[6], (D, D), dtype=jnp.float32) * s(D)
        W_out = jax.random.normal(ks[7], (INNER, DIM), dtype=jnp.float32) * s(INNER)
        b_out = jnp.zeros((DIM,), dtype=jnp.float32)
        temperature = jnp.ones((1, H, 1, 1), dtype=jnp.float32) * 0.5
        return {'x': x, 'W_fx': W_fx, 'b_fx': b_fx, 'W_x': W_x, 'b_x': b_x, 'W_slice': W_slice, 'b_slice': b_slice, 'W_q': W_q, 'W_k': W_k, 'W_v': W_v, 'W_out': W_out, 'b_out': b_out, 'temperature': temperature}
    _L0_ffn_all = _L0_ffn_setup()
    _L0_ffn_in = {k: v for k, v in _L0_ffn_all.items() if k in ('W_fx', 'b_fx', 'W_x', 'b_x', 'W_slice', 'b_slice', 'W_q', 'W_k', 'W_v', 'W_out', 'b_out', 'temperature')}
    del _L0_ffn_all
    return {'x': x, 'src': src, 'dst': dst, 'L0_gnn_W': _L0_gnn_in['W'], 'L0_gnn_att_src': _L0_gnn_in['att_src'], 'L0_gnn_att_dst': _L0_gnn_in['att_dst'], 'L0_gnn_bias': _L0_gnn_in['bias'], 'L0_ffn_W_fx': _L0_ffn_in['W_fx'], 'L0_ffn_b_fx': _L0_ffn_in['b_fx'], 'L0_ffn_W_x': _L0_ffn_in['W_x'], 'L0_ffn_b_x': _L0_ffn_in['b_x'], 'L0_ffn_W_slice': _L0_ffn_in['W_slice'], 'L0_ffn_b_slice': _L0_ffn_in['b_slice'], 'L0_ffn_W_q': _L0_ffn_in['W_q'], 'L0_ffn_W_k': _L0_ffn_in['W_k'], 'L0_ffn_W_v': _L0_ffn_in['W_v'], 'L0_ffn_W_out': _L0_ffn_in['W_out'], 'L0_ffn_b_out': _L0_ffn_in['b_out'], 'L0_ffn_temperature': _L0_ffn_in['temperature']}

def reference(x, src, dst, L0_gnn_W, L0_gnn_att_src, L0_gnn_att_dst, L0_gnn_bias, L0_ffn_W_fx, L0_ffn_b_fx, L0_ffn_W_x, L0_ffn_b_x, L0_ffn_W_slice, L0_ffn_b_slice, L0_ffn_W_q, L0_ffn_W_k, L0_ffn_W_v, L0_ffn_W_out, L0_ffn_b_out, L0_ffn_temperature):
    import jax
    import jax.numpy as jnp

    def _L0_gnn_ref(x, edge_index, W, att_src, att_dst, bias):
        import jax, jax.numpy as jnp
        import numpy as np
        N = 3125
        E = 50000
        IN = 256
        H = 4
        C = 64
        n = x.shape[0]
        loops = jnp.arange(n, dtype=edge_index.dtype)
        src = jnp.concatenate([edge_index[0], loops])
        dst = jnp.concatenate([edge_index[1], loops])
        xp = (x @ W).reshape(n, H, C)
        a_src = jnp.einsum('nhc,hc->nh', xp, att_src)
        a_dst = jnp.einsum('nhc,hc->nh', xp, att_dst)
        alpha = jax.nn.leaky_relu(a_src[src] + a_dst[dst], negative_slope=0.2)
        amax = jax.ops.segment_max(alpha, dst, num_segments=n)
        amax = jnp.where(jnp.isfinite(amax), amax, 0.0)
        ex = jnp.exp(alpha - amax[dst])
        denom = jax.ops.segment_sum(ex, dst, num_segments=n)
        w = ex / denom[dst]
        msg = xp[src] * w[..., None]
        agg = jax.ops.segment_sum(msg, dst, num_segments=n)
        out = agg.reshape(n, H * C) + bias
        return jax.nn.elu(out)

    def _L0_ffn_ref(x, W_fx, b_fx, W_x, b_x, W_slice, b_slice, W_q, W_k, W_v, W_out, b_out, temperature):
        import jax, jax.numpy as jnp
        import numpy as np
        DIM = 256
        H = 8
        D = 64
        G = 64
        INNER = H * D
        SCALE = D ** (-0.5)
        B, N, _ = x.shape
        fx_mid = (x @ W_fx + b_fx).reshape(B, N, H, D).transpose(0, 2, 1, 3)
        x_mid = (x @ W_x + b_x).reshape(B, N, H, D).transpose(0, 2, 1, 3)
        temp = jnp.clip(temperature, 0.1, 5.0)
        slice_weights = jax.nn.softmax((x_mid @ W_slice + b_slice) / temp, axis=-1)
        slice_norm = slice_weights.sum(axis=2)
        slice_token = jnp.einsum('bhnc,bhng->bhgc', fx_mid, slice_weights)
        slice_token = slice_token / (slice_norm[..., None] + 1e-05)
        q = slice_token @ W_q
        k = slice_token @ W_k
        v = slice_token @ W_v
        attn = jax.nn.softmax(jnp.einsum('bhgc,bhkc->bhgk', q, k) * SCALE, axis=-1)
        out_slice = jnp.einsum('bhgk,bhkc->bhgc', attn, v)
        out_x = jnp.einsum('bhgc,bhng->bhnc', out_slice, slice_weights)
        out_x = out_x.transpose(0, 2, 1, 3).reshape(B, N, INNER)
        return out_x @ W_out + b_out
    edge_index = jnp.stack([src, dst])
    x = x + _L0_gnn_ref(_layernorm(x, axis=-1), edge_index, L0_gnn_W, L0_gnn_att_src, L0_gnn_att_dst, L0_gnn_bias)
    x = x + _L0_ffn_ref(_layernorm(x, axis=-1)[None], L0_ffn_W_fx, L0_ffn_b_fx, L0_ffn_W_x, L0_ffn_b_x, L0_ffn_W_slice, L0_ffn_b_slice, L0_ffn_W_q, L0_ffn_W_k, L0_ffn_W_v, L0_ffn_W_out, L0_ffn_b_out, L0_ffn_temperature)[0]
    return x

_drawn_inputs = setup_inputs


def setup_inputs(seed=0):
    import zlib

    import numpy as np

    out = dict(_drawn_inputs(seed))
    spreads = {'L0_ffn_b_fx': (0.0, 0.1),
     'L0_ffn_b_x': (0.0, 0.8),
     'L0_ffn_b_slice': (0.0, 0.8),
     'L0_ffn_b_out': (0.0, 0.1),
     'L0_ffn_temperature': (0.5, 0.6)}
    factors = {'L0_gnn_bias': 4.791,
     'L0_ffn_W_x': 8.0,
     'L0_ffn_W_slice': 8.0,
     'L0_ffn_W_q': 8.0,
     'L0_ffn_W_k': 8.0}
    for name, (base, spread) in spreads.items():
        noise = np.random.default_rng([zlib.crc32(name.encode()), seed]).standard_normal(out[name].shape)
        drawn = base * np.exp(spread * noise) if base else spread * noise
        out[name] = jnp.asarray(drawn.astype(out[name].dtype))
    for name, factor in factors.items():
        out[name] = (out[name] * factor).astype(out[name].dtype)
    return out
```

```python
from contextlib import ExitStack

import concourse.bass as bass
from concourse import mybir

F32 = mybir.dt.float32
BF16 = mybir.dt.bfloat16
I32 = mybir.dt.int32
ALU = mybir.AluOpType
ACT = mybir.ActivationFunctionType
X = mybir.AxisListType.X

P = 128
ROW = 512
CPG = 8
GE = CPG * P
SPREAD = 60.0
EPS = 1e-5


class Own:

    def __init__(self, eng, sem, base):
        self.eng, self.sem, self.base, self.k = eng, sem, base, 0

    def add(self, ins):
        ins.then_inc(self.sem, 1)
        self.k += 1

    def wait(self):
        self.eng.wait_ge(self.sem, self.base + self.k)


class Chain:

    def __init__(self, eng, sem):
        self.eng, self.sem, self.base, self.k = eng, sem, 0, 0

    def add(self, ins):
        ins.then_inc(self.sem, 1)
        self.k += 1
        return ins

    def wait(self):
        self.eng.wait_ge(self.sem, self.base + self.k)


def build(nc, x, src, dst, W, att_src, att_dst, gbias, W_fx, b_fx, W_x, b_x, W_slice, b_slice,
          W_q, W_k, W_v, W_out, b_out, temperature, out):
    N, D = x.shape
    E = src.shape[0]
    H, C = att_src.shape
    FH = temperature.shape[1]
    G = W_slice.shape[1]
    HG = FH * G
    NT = -(-N // P)
    LAST = N - (NT - 1) * P
    NG = -(-E // GE)
    NG += NG % 2
    ROWS = NG * GE // ROW
    FULL = E // ROW
    REST = E - FULL * ROW
    TW = D + 3 * H
    AW = D + 2 * H
    RPG = GE // ROW
    NB = 4
    PAD_BASE = (ROWS // 32) * 32 if ROWS % 32 else ROWS - 32
    assert D == 256 and H * C == D and HG == 512 and G == 64 and NT % 2 == 1 and NG % NB == 0 and ROWS <= P
    assert FULL >= PAD_BASE and LAST < P

    table = nc.dram_tensor("table", [NT * P, TW], F32, kind="Internal").ap()
    slots_d = nc.dram_tensor("slots_d", [ROWS, ROW], BF16, kind="Internal").ap()

    ctx = ExitStack()
    with ctx:
        def sb(name, shape, dt=F32):
            return ctx.enter_context(nc.sbuf_tensor(name, shape, dt))

        def sem(name):
            return ctx.enter_context(nc.semaphore(name))

        bank = [ctx.enter_context(nc.psum_tensor(f"bank{i}", [P, 512], F32)) for i in range(8)]

        def carve(region, sizes):
            at, views = 0, {}
            for name, parts, shape, dt in sizes:
                n = 1
                for k in shape:
                    n *= k
                a = region[0:parts, at:at + n]
                if dt != F32:
                    a = a.bitcast(dt)
                if len(shape) == 2:
                    a = a.rearrange("p (a b) -> p a b", a=shape[0])
                if len(shape) == 3:
                    a = a.rearrange("p (a b c) -> p a b c", a=shape[0], b=shape[1])
                views[name] = a
                at += n
            assert at <= region.shape[1]
            return views

        swT_r = sb("swT_r", [P, 4 * NT * P])
        swT = swT_r[:, :].rearrange("p (j n) -> p j n", j=4)
        prep = carve(swT_r, [("es", ROWS, [ROW], I32), ("ed", ROWS, [ROW], I32), ("esf", ROWS, [ROW], F32),
                             ("edf", ROWS, [ROW], F32), ("emi", ROWS, [ROW], I32), ("emf", ROWS, [ROW], F32),
                             ("Wx", P, [2, HG], F32), ("WxT", P, [4, D], F32), ("attb", P, [2, D], F32), ("watt", P, [2, D], F32),
                             ("uv", P, [NT, 2 * H], F32), ("uu", P, [NT, H], F32), ("ab", P, [NT, 2 * H], F32), ("abr", P, [NT, 2 * H], F32)])
        es, ed, esf, edf, emi, emf, Wx, WxT, attb, watt, uv, uu, ab, abr = (prep[k] for k in prep)

        gt_r = sb("gt_r", [P, NB * CPG * TW])
        gt = gt_r[:, :].rearrange("p (b c e) -> p b c e", b=NB, c=CPG)
        late = carve(gt_r, [("tokn", P, [4, D + 1], F32), ("tokT", P, [2, HG], F32), ("nrow", 1, [HG], F32), ("stT", G, [HG], F32),
                            ("qkv", G, [3, HG], F32), ("at_s", G, [HG], F32), ("at_e", G, [HG], F32),
                            ("osT", G, [HG], F32), ("Z", P, [4, D], F32), ("swb", P, [2, 4, P], F32)])
        tokn, tokT, nrow, stT, qkv, at_s, at_e, osT, Z, swb = (late[k] for k in late)
        at_T = at_e
        amx = sb("amx", [G, 2, FH])
        nrm = sb("nrm", [P, 2, 4])

        ident = sb("ident", [P, P])
        lane_i = sb("lane_i", [P, 1], I32)
        lane = sb("lane", [P, 1])
        cols_i = sb("cols_i", [P, P], I32)
        cols = sb("cols", [P, P])
        ones = sb("ones", [P, P])
        Wg = sb("Wg", [P, 2, D + 2 * H])
        gb = sb("gb", [P, D])
        bo = sb("bo", [P, D])
        Ws2 = sb("Ws2", [P, G])
        bxT = sb("bxT", [G, FH])
        bsl = sb("bsl", [1, G])
        tmp8 = sb("tmp8", [P, FH])
        itemp = sb("itemp", [P, FH])
        Wl = sb("Wl", [P, 2, HG])
        bl = sb("bl", [1, HG])
        Wf = sb("Wf", [P, 2, HG])
        bf = sb("bf", [1, HG])
        Wq = sb("Wq", [G, 3, G])
        Wo = sb("Wo", [G, FH, D])

        emb = sb("emb", [ROWS, ROW], BF16)
        mm = sb("mm", [ROWS, 2])
        idx = sb("idx", [P, ROWS * 4], I32)
        idxg = sb("idxg", [P, NB, CPG], I32)
        slot = sb("slot", [P, ROWS * 4])
        gmm = sb("gmm", [1, 2, NG])
        gi = sb("gi", [1, NG], I32)
        gblk = sb("gblk", [1, NG], I32)
        gmi = sb("gmi", [1, NG], I32)
        gmf = sb("gmf", [1, NG])
        mhi = sb("mhi", [P, NG])
        mlo = sb("mlo", [P, NG])
        flagf = sb("flagf", [1, 4])
        spr = sb("spr", [1, H])
        flag = sb("flag", [1, 1], I32)

        xs = sb("xs", [P, NT, D])
        st = sb("st", [P, NT, 6])
        mv = sb("mv", [P, NT, 2])
        rstd = sb("rstd", [P, NT])
        xn = sb("xn", [P, 2, D + 1])
        xT = sb("xT", [P, 2, D])
        acc = sb("acc", [P, NT + 1, AW])
        r8 = sb("r8", [P, 2 * H])
        g8 = sb("g8", [2 * H, 1])
        dg8 = sb("dg8", [2 * H, 2 * H])
        Gb = sb("Gb", [P, 2 * H])
        ee = sb("ee", [P, NT, 3 * H])
        ab3 = sb("ab3", [P, NT + 1, 2 * H, 3], BF16)

        db = sb("db", [P, 2, GE], BF16)
        ot = sb("ot", [P, 2, GE], BF16)
        oh = sb("oh", [P, 2, CPG, P])
        tsa = sb("tsa", [P, 2, 2 * H * 3], BF16)
        tsl = sb("tsl", [P, 2, 2 * H * 3], BF16)
        abe = sb("abe", [P, 2, CPG, 2 * H])
        we = sb("we", [P, 2, CPG, 2 * H])

        rden = sb("rden", [P, 2, H])
        z = sb("z", [P, 2, D])
        zm = sb("zm", [P, 2, D])
        ze = zm
        nhalf = sb("nhalf", [P, 1])
        mx = sb("mx", [P, 2, FH])
        sm = sb("sm", [P, 2, FH])
        lg = sb("lg", [P, 2, HG])
        sw = sb("sw", [P, 2, HG])
        y = z

        s_w = sem("s_w"); s_w2 = sem("s_w2"); s_es = sem("s_es"); s_ed = sem("s_ed")
        s_x = [sem(f"s_x{i}") for i in range(5)]
        s_pool = sem("s_pool"); s_const = sem("s_const")
        s_ef = sem("s_ef"); s_sl_st = sem("s_sl_st"); s_eT = sem("s_eT"); s_eTc = sem("s_eTc")
        s_gm = sem("s_gm"); s_gmT = sem("s_gmT"); s_idx = sem("s_idx"); s_flag = sem("s_flag")
        s_wxT = sem("s_wxT"); s_wxTc = sem("s_wxTc"); s_wl = sem("s_wl"); s_wlc = sem("s_wlc")
        s_var = sem("s_var"); s_sd = sem("s_sd"); s_xn = sem("s_xn"); s_xnT = sem("s_xnT"); s_xTc = sem("s_xTc")
        s_xp = sem("s_xp"); s_xpc = sem("s_xpc"); s_tab = sem("s_tab"); s_r8 = sem("s_r8"); s_r8T = sem("s_r8T")
        s_dg = sem("s_dg"); s_G = sem("s_G"); s_ea = sem("s_ea"); s_ex = sem("s_ex"); s_tab2 = sem("s_tab2")
        s_gat = [sem(f"s_gat{i}") for i in range(NB)]
        s_db = [sem(f"s_db{i}") for i in range(2)]
        s_ot = sem("s_ot"); s_ts = sem("s_ts"); s_oh = sem("s_oh"); s_lk = sem("s_lk"); s_ab = sem("s_ab")
        s_sc = sem("s_sc"); s_mm = sem("s_mm"); s_mg = sem("s_mg")
        s_min = sem("s_min"); s_exm = sem("s_exm"); s_n2 = sem("s_n2"); s_n2T = sem("s_n2T"); s_n2c = sem("s_n2c")
        s_lg = sem("s_lg"); s_sub = sem("s_sub"); s_exl = sem("s_exl"); s_sw = sem("s_sw"); s_tok = sem("s_tok")
        s_swT = sem("s_swT"); s_swc = sem("s_swc")
        s_f = sem("s_f"); s_fp = sem("s_fp"); s_fa = sem("s_fa")
        s_cp = sem("s_cp"); s_y = sem("s_y"); s_yo = sem("s_yo")
        s_st = [sem(f"s_st{i}") for i in range(2)]
        s_dv = sem("s_dv"); s_ix = sem("s_ix"); s_pad = sem("s_pad"); s_turn = sem("s_turn"); s_turn_v = sem("s_turn_v"); s_var2 = sem("s_var2"); s_rs = sem("s_rs"); s_own = sem("s_own"); s_bn = sem("s_bn"); s_ta = sem("s_ta"); s_we = sem("s_we"); s_wp = sem("s_wp")
        s_res = sem("s_res"); s_kc = sem("s_kc"); s_os = sem("s_os")

        pT = bank[4]
        TOK = [bank[j][:, 0:D + 1] for j in range(4)]

        XB = 6
        XL = -(-(NT - 1) // XB) + 1

        def flat(a):
            return a.rearrange("p a b -> p (a b)")

        def by_head(a):
            return a.rearrange("p (h g) -> p h g", g=G)

        def over_slices(a):
            return a.unsqueeze(2).broadcast_to((a.shape[0], FH, G))

        def abs3(blk):
            return ab3[:, bass.ds(blk, 1), :, :].rearrange("p t e c -> p (t e c)")

        block = ctx.enter_context(nc.Block())

        @block.sync
        def _(sp):
            for i in range(XL - 1):
                a, b = i * XB, min((i + 1) * XB, NT - 1)
                if b > a:
                    sp.dma_start(xs[:, a:b, :], x[a * P:b * P, :].rearrange("(t p) d -> p t d", p=P)).then_inc(s_x[i], 16)
            sp.wait_ge(s_pool, 1)
            sp.dma_start(xs[0:LAST, NT - 1, :], x[(NT - 1) * P:N, :]).then_inc(s_x[XL - 1], 16)
            sp.dma_start(Wx[:, :, :], W_x.rearrange("(k p) n -> p k n", p=P)).then_inc(s_w2, 16)
            sp.dma_start(Ws2[0:G, :], W_slice).then_inc(s_w2, 16)
            sp.dma_start(Ws2[G:P, :], W_slice).then_inc(s_w2, 16)
            sp.dma_start(bxT[:, :], b_x.rearrange("(h c) -> c h", c=G), allow_slow_non_contiguous=True).then_inc(s_w2, 16)
            sp.dma_start(bsl[:, :], b_slice.rearrange("(a n) -> a n", a=1)).then_inc(s_w2, 16)
            sp.dma_start(tmp8[:, :], temperature.rearrange("a h b c -> (a b c) h").broadcast_to((P, FH))).then_inc(s_w2, 16)
            sp.dma_start(Wf[:, :, :], W_fx.rearrange("(k p) n -> p k n", p=P)).then_inc(s_w2, 16)
            sp.dma_start(bf[:, :], b_fx.rearrange("(a n) -> a n", a=1)).then_inc(s_w2, 16)
            for i, w in enumerate((W_q, W_k, W_v)):
                sp.dma_start(Wq[:, i, :], w).then_inc(s_w2, 16)
            sp.dma_start(Wo[:, :, :], W_out.rearrange("(h c) n -> c h n", c=G)).then_inc(s_w2, 16)
            sp.wait_ge(s_ef, 3)
            sp.dma_start(slots_d, emb[:, :]).then_inc(s_sl_st, 16)

            def put(t):
                sp.wait_ge(s_xpc, t + 1)
                sp.dma_start(table[bass.ds(t * P, P), 0:D], acc[:, bass.ds(t, 1), 0:D]).then_inc(s_tab, 16)
            with sp.Fori(0, NT) as t:
                put(t)
            sp.wait_ge(s_ea, 1)
            sp.wait_ge(s_ex, 2)
            sp.dma_start(table[:, D:TW].rearrange("(t p) e -> p t e", p=P), ee[:, :, :]).then_inc(s_tab2, 16)

            def spread_slots(g, b):
                if not isinstance(g, int) or g >= 2:
                    sp.wait_ge(s_ot, g - 1)
                sp.dma_start(db[:, b, :], slots_d.rearrange("(g r) c -> g (r c)", r=RPG)[bass.ds(g, 1), :]
                             .broadcast_to((P, GE))).then_inc(s_db[b], 16)
            sp.wait_ge(s_sl_st, 16)
            for g in range(NB):
                spread_slots(g, g % 2)
            with sp.Fori(1, NG // NB) as i:
                for u in range(NB):
                    spread_slots(NB * i + u, u % 2)

            def store(t, b, n):
                sp.wait_ge(s_yo, t + 1)
                sp.dma_start(out[bass.ds(t * P, n), :], y[0:n, b, :]).then_inc(s_st[b], 16)
            with sp.Fori(0, NT // 2) as i:
                for u in range(2):
                    store(2 * i + u, u, P)
            store(NT - 1, 0, LAST)
            sp.wait_ge(s_st[0], 16 * ((NT + 1) // 2))
            sp.wait_ge(s_st[1], 16 * (NT // 2))

        @block.gpsimd
        def _(pool):
            pool.memset(xs[:, NT - 1, :], 0.0).then_inc(s_pool, 1)
            pool.memset(ident[:, :], 0.0).then_inc(s_pool, 1)
            pool.iota(lane_i[:, :], pattern=[[0, 1]], base=0, channel_multiplier=1).then_inc(s_pool, 1)
            pool.iota(cols_i[:, :], pattern=[[1, P]], base=0, channel_multiplier=0).then_inc(s_pool, 1)
            pool.wait_ge(s_pool, 4)
            pool.affine_select(out=ident[:, :], in_=ident[:, :], compare_op=ALU.not_equal, fill=1.0, base=0,
                               pattern=[[-1, P]], channel_multiplier=1).then_inc(s_const, 1)
            pool.tensor_copy(lane[:, :], lane_i[:, :]).then_inc(s_const, 1)
            pool.tensor_copy(cols[:, :], cols_i[:, :]).then_inc(s_const, 1)
            pool.memset(ones[:, :], 1.0).then_inc(s_const, 1)
            pool.memset(nhalf[:, :], -0.5).then_inc(s_const, 1)
            pool.memset(acc[:, NT, :], 0.0).then_inc(s_const, 1)
            pool.memset(ab3[:, NT, :, :], 0.0).then_inc(s_const, 1)
            pool.memset(xn[:, :, D:D + 1], 1.0).then_inc(s_const, 1)
            pool.wait_ge(s_tab, 16 * NT)
            pool.wait_ge(s_tab2, 16)

            def gather(g, b):
                if not isinstance(g, int) or g >= NB:
                    pool.wait_ge(s_mm, g - NB + 1)
                pool.wait_ge(s_ix, g + 1)
                pool.sem_inc(s_turn, 1)
                for c in range(CPG):
                    pool.indirect_dma_start(
                        gt[:, b, c, :], None, table,
                        bass.IndirectOffsetOnAxis(idxg[:, b, c:c + 1], 0)).then_inc(s_gat[b], 16)
            for g in range(NB):
                gather(g, g)
            with pool.Fori(1, NG // NB) as i:
                for u in range(NB):
                    gather(NB * i + u, u)

            pool.wait_ge(s_const, 5)
            with pool.Fori(0, NT) as t:
                pool.wait_ge(s_var2, t + 1)
                pool.tensor_tensor(rstd[:, 0:1], mv[:, 0, 1:2], nhalf[:, :], ALU.pow).then_inc(s_rs, 1)

        @block.scalar
        def _(act):
            act.wait_ge(s_pad, 2)
            act.dma_start(ed[0:FULL, :], dst[0:FULL * ROW].rearrange("(r c) -> r c", c=ROW)).then_inc(s_ed, 16)
            act.dma_start(ed[FULL:FULL + 1, 0:REST], dst[FULL * ROW:E].rearrange("(r c) -> r c", r=1)).then_inc(s_ed, 16)
            act.dma_start(es[0:FULL, :], src[0:FULL * ROW].rearrange("(r c) -> r c", c=ROW)).then_inc(s_es, 16)
            act.dma_start(es[FULL:FULL + 1, 0:REST], src[FULL * ROW:E].rearrange("(r c) -> r c", r=1)).then_inc(s_es, 16)
            act.dma_start(Wg[:, :, 0:D], W.rearrange("(k p) n -> p k n", p=P)).then_inc(s_w, 16)
            for i, a in enumerate((att_src, att_dst)):
                act.dma_start(attb[:, i, :], a.rearrange("(a h) c -> a (h c)", a=1).broadcast_to((P, D))).then_inc(s_w, 16)
            act.dma_start(gb[:, :], gbias.rearrange("(a n) -> a n", a=1).broadcast_to((P, D))).then_inc(s_w, 16)
            act.dma_start(bo[:, :], b_out.rearrange("(a n) -> a n", a=1).broadcast_to((P, D))).then_inc(s_w, 16)
            for k in range(2):
                act.wait_ge(s_wxT, k + 1)
                act.copy(WxT[:, :, k * P:(k + 1) * P], bank[k][:, :].rearrange("p (j n) -> p j n", j=4)).then_inc(s_wxTc, 1)
            act.wait_ge(s_var, 1)
            act.activation(rstd[:, :], mv[:, :, 1], ACT.Sqrt).then_inc(s_sd, 1)

            def evac_xT(t, b):
                act.wait_ge(s_xnT, t + 1)
                act.copy(xT[:, b, :], pT[:, b * D:(b + 1) * D]).then_inc(s_xTc, 1)
            with act.Fori(0, NT // 2) as i:
                for u in range(2):
                    evac_xT(2 * i + u, u)
            evac_xT(NT - 1, 0)
            act.wait_ge(s_idx, 1)
            act.wait_ge(s_ea, 2)
            act.activation(ee[:, :, H:2 * H], ee[:, :, 0:H], ACT.Exp, scale=0.2).then_inc(s_ex, 1)
            act.wait_ge(s_ex, 1)
            act.activation(ee[:, :, 0:H], ee[:, :, 0:H], ACT.Exp).then_inc(s_ex, 1)
            act.wait_ge(s_ea, 3)
            act.activation(ab[:, :, :], uv[:, :, :], ACT.Exp).then_inc(s_ex, 1)

            def pick(g, u):
                if not isinstance(g, int) or g >= NB:
                    act.wait_ge(s_we, g - NB + 1)
                act.copy(idxg[:, u, :], idx[:, bass.ds(g * CPG, CPG)]).then_inc(s_ix, 1)
            for g in range(NB):
                pick(g, g)
            with act.Fori(1, NG // NB) as i:
                for u in range(NB):
                    pick(NB * i + u, u)

            def ffn1(t, b):
                act.wait_ge(s_min, t + 1)
                act.activation(ze[:, b, :], zm[:, b, :], ACT.Exp).then_inc(s_exm, 1)
                act.wait_ge(s_n2T, t + 1)
                act.copy(xT[:, b, :], pT[:, b * D:(b + 1) * D]).then_inc(s_n2c, 1)
                act.wait_ge(s_sub, t + 1)
                act.activation(bank[5 + b][:, :], lg[:, b, :], ACT.Exp).then_inc(s_exl, 1)
                act.wait_ge(s_swT, t + 1)
                act.copy(swT[:, :, bass.ds(t * P, P)], bank[7][:, :].rearrange("p (j n) -> p j n", j=4)).then_inc(s_swc, 1)
            with act.Fori(0, NT // 2) as i:
                for u in range(2):
                    ffn1(2 * i + u, u)
            ffn1(NT - 1, 0)

            for k in range(2):
                act.wait_ge(s_fp, 2 + k)
                act.copy(tokT[:, k, :], bank[4 + k][:, :]).then_inc(s_fa, 1)
            act.wait_ge(s_fp, 5)
            act.copy(qkv[:, 0, :], bank[1][0:G, :]).then_inc(s_fa, 1)
            act.wait_ge(s_f, 4)
            act.activation(at_e[:, :], at_s[:, :], ACT.Exp, scale=float(G) ** -0.5).then_inc(s_fa, 1)
            for k in range(2):
                act.wait_ge(s_fp, 9)
                act.copy(Z[:, 2 * k:2 * k + 2, :], bank[5 + k][:, :].rearrange("p (j n) -> p j n", j=2)).then_inc(s_fa, 1)

            def ffn2(t, b):
                if not isinstance(t, int) or t >= 2:
                    act.wait_ge(s_y, t - 1)
                act.copy(swb[:, b, :, :], swT[:, :, bass.ds(t * P, P)]).then_inc(s_cp, 1)
            for t in range(2):
                ffn2(t, t)
            with act.Fori(1, NT // 2) as i:
                for u in range(2):
                    ffn2(2 * i + u, u)
            ffn2(NT - 1, 0)

        @block.tensor
        def _(pe):
            mm_ = nc.tensor.matmul
            pe.wait_ge(s_const, 1)
            pe.wait_ge(s_w2, 16 * 12)
            for k in range(2):
                for j in range(4):
                    last = nc.tensor.transpose(bank[k][:, j * P:(j + 1) * P], Wx[:, k, j * P:(j + 1) * P], ident[:, :])
                last.then_inc(s_wxT, 1)
            pe.wait_ge(s_wxTc, 2)
            for k in range(2):
                for h in range(FH):
                    o = G * (h % 2)
                    j = h // 2
                    last = mm_(bank[2 + k + 2 * (h % 2)][:, j * G:(j + 1) * G], WxT[o:o + G, h // 2, k * P:(k + 1) * P], Ws2[o:o + G, :],
                               start=True, stop=True)
                last.then_inc(s_wl, 1)
            for h in range(FH):
                last = mm_(bank[0][0:1, h * G:(h + 1) * G], bxT[:, h:h + 1], Ws2[0:G, :], start=True, stop=True)
            last.then_inc(s_wl, 1)

            pe.wait_ge(s_ef, 5)
            pe.wait_ge(s_wlc, 3)
            for i in range(4):
                nc.tensor.transpose(bank[0][:, i * ROWS:(i + 1) * ROWS], esf[:, i * P:(i + 1) * P], ident[0:ROWS, 0:ROWS])
                last = nc.tensor.transpose(bank[1][:, i * ROWS:(i + 1) * ROWS], emf[:, i * P:(i + 1) * P], ident[0:ROWS, 0:ROWS])
            last.then_inc(s_eT, 1)
            for i in range(2):
                last = nc.tensor.transpose(bank[2][0:1, i * ROWS:(i + 1) * ROWS], mm[:, i:i + 1], ident[0:ROWS, 0:ROWS])
            last.then_inc(s_eT, 1)
            pe.wait_ge(s_gm, 1)
            pe.wait_ge(s_const, 4)
            mm_(bank[3][:, 0:NG], ones[0:1, :], gmf[:, :], start=True, stop=True).then_inc(s_gmT, 1)

            def proj(t, b):
                pe.wait_ge(s_xn, t + 1)
                if not isinstance(t, int) or t >= 2:
                    pe.wait_ge(s_xTc, t - 1)
                for k in range(2):
                    last = nc.tensor.transpose(pT[:, b * D + k * P:b * D + (k + 1) * P], xn[:, b, k * P:(k + 1) * P], ident[:, :])
                last.then_inc(s_xnT, 1)
                pe.wait_ge(s_xTc, t + 1)
                if not isinstance(t, int) or t >= 2:
                    pe.wait_ge(s_xpc, t - 1)
                for k in range(2):
                    last = mm_(bank[5 + b][:, 0:AW], xT[:, b, k * P:(k + 1) * P], Wg[:, k, :], start=(k == 0), stop=(k == 1))
                last.then_inc(s_xp, 1)
            for t in range(2):
                proj(t, t)
            with pe.Fori(1, NT // 2) as i:
                for u in range(2):
                    proj(2 * i + u, u)
            proj(NT - 1, 0)

            pe.wait_ge(s_r8, 1)
            nc.tensor.transpose(bank[0][0:2 * H, 0:P], r8[:, :], ident[:, :]).then_inc(s_r8T, 1)
            pe.wait_ge(s_dg, 1)
            mm_(bank[1][:, 0:2 * H], ones[0:2 * H, :], dg8[:, :], start=True, stop=True).then_inc(s_G, 1)

            def lookup(g, b):
                pe.wait_ge(s_ot, g + 1)
                pe.wait_ge(s_ts, g + 1)
                if not isinstance(g, int) or g >= 2:
                    pe.wait_ge(s_ab, g - 1)
                for c in range(CPG):
                    last = mm_(bank[b][:, c * 24:(c + 1) * 24], ot[:, b, c * P:(c + 1) * P], tsl[:, b, :], start=True, stop=True)
                last.then_inc(s_lk, 1)

            def sums(g, b, b4):
                pe.wait_ge(s_oh, g + 1)
                pe.wait_ge(s_sc, g + 1)
                if not isinstance(g, int) or g >= 2:
                    pe.wait_ge(s_mg, g - 1)
                for c in range(CPG):
                    last = mm_(bank[2 + b][:, 0:D + H], oh[:, b, c, :], gt[:, b4, c, 0:D + H], start=(c == 0), stop=(c == CPG - 1))
                last.then_inc(s_mm, 1)

            lookup(0, 0)
            for g in range(NB):
                lookup(g + 1, (g + 1) % 2)
                sums(g, g % 2, g)
            with pe.Fori(1, NG // NB - 1) as i:
                for u in range(NB):
                    lookup(NB * i + u + 1, (u + 1) % 2)
                    sums(NB * i + u, u % 2, u)
            for g in range(NG - NB, NG):
                if g + 1 < NG:
                    lookup(g + 1, (g + 1) % 2)
                sums(g, g % 2, g % NB)

            def ffn1(t, b, n):
                first = isinstance(t, int) and t == 0
                pe.wait_ge(s_n2, t + 1)
                if not isinstance(t, int) or t >= 2:
                    pe.wait_ge(s_n2c, t - 1)
                for k in range(2):
                    last = nc.tensor.transpose(pT[:, b * D + k * P:b * D + (k + 1) * P], xn[:, b, k * P:(k + 1) * P], ident[:, :])
                last.then_inc(s_n2T, 1)
                pe.wait_ge(s_n2c, t + 1)
                if not isinstance(t, int) or t >= 2:
                    pe.wait_ge(s_sw, t - 1)
                mm_(bank[5 + b][:, :], ones[0:1, :], bl[:, :], start=True, stop=False)
                for k in range(2):
                    last = mm_(bank[5 + b][:, :], xT[:, b, k * P:(k + 1) * P], Wl[:, k, :], start=False, stop=(k == 1))
                last.then_inc(s_lg, 1)
                pe.wait_ge(s_sw, t + 1)
                if not first:
                    pe.wait_ge(s_swc, t)
                for j in range(4):
                    last = nc.tensor.transpose(bank[7][:, j * P:(j + 1) * P], sw[:, b, j * P:(j + 1) * P], ident[:, :])
                last.then_inc(s_swT, 1)
                fin = isinstance(t, int) and t == NT - 1
                for j in range(4):
                    last = mm_(TOK[j], sw[0:n, b, j * P:(j + 1) * P], xn[0:n, b, :], start=first, stop=fin)
                last.then_inc(s_tok, 1)
            for t in range(2):
                ffn1(t, t, P)
            with pe.Fori(1, NT // 2) as i:
                for u in range(2):
                    ffn1(2 * i + u, u, P)
            ffn1(NT - 1, 0, LAST)

            pe.wait_ge(s_f, 1)
            pe.wait_ge(s_swc, NT)
            for j in range(4):
                last = nc.tensor.transpose(bank[7][0:1, j * P:(j + 1) * P], tokn[:, j, D:D + 1], ident[:, :])
            last.then_inc(s_fp, 1)
            for k in range(2):
                for j in range(4):
                    last = nc.tensor.transpose(bank[4 + k][:, j * P:(j + 1) * P], tokn[:, j, k * P:(k + 1) * P], ident[:, :])
                last.then_inc(s_fp, 1)
            pe.wait_ge(s_fa, 2)
            pe.wait_ge(s_f, 2)
            nrow_ = nrow
            stT_ = stT
            for h in range(FH):
                s = slice(h * G, (h + 1) * G)
                for k in range(2):
                    mm_(bank[0][0:G, s], Wf[:, k, s], tokT[:, k, s], start=(k == 0), stop=False)
                last = mm_(bank[0][0:G, s], bf[:, s], nrow_[:, s], start=False, stop=True)
            last.then_inc(s_fp, 1)
            pe.wait_ge(s_f, 3)
            mm_(bank[1][0:G, :], Wq[:, 0, :], stT_, start=True, stop=True).then_inc(s_fp, 1)
            mm_(bank[2][0:G, :], Wq[:, 1, :], stT_, start=True, stop=True)
            for h in range(FH):
                s = slice(h * G, (h + 1) * G)
                last = mm_(bank[3][0:G, s], stT_[:, s], Wq[:, 2, :], start=True, stop=True)
            last.then_inc(s_fp, 1)
            pe.wait_ge(s_fa, 3)
            pe.wait_ge(s_kc, 1)
            for h in range(FH):
                s = slice(h * G, (h + 1) * G)
                last = mm_(bank[0][0:G, s], qkv[:, 0, s], qkv[:, 1, s], start=True, stop=True)
            last.then_inc(s_fp, 1)
            pe.wait_ge(s_f, 5)
            for h in range(FH):
                s = slice(h * G, (h + 1) * G)
                last = nc.tensor.transpose(bank[1][0:G, s], at_s[:, s], ident[0:G, 0:G])
            last.then_inc(s_fp, 1)
            pe.wait_ge(s_f, 6)
            pe.wait_ge(s_kc, 2)
            for h in range(FH):
                s = slice(h * G, (h + 1) * G)
                last = mm_(bank[2][0:G, s], qkv[:, 2, s], at_T[:, s], start=True, stop=True)
            last.then_inc(s_os, 1)
            pe.wait_ge(s_f, 7)
            for h in range(FH):
                o = G * (h % 2)
                j = h // 2
                last = mm_(bank[5 + j // 2][o:o + G, (j % 2) * D:(j % 2 + 1) * D], osT[:, h * G:(h + 1) * G], Wo[:, h, :],
                           start=True, stop=True)
            last.then_inc(s_fp, 1)

            def ffn2(t, b):
                pe.wait_ge(s_cp, t + 1)
                if not isinstance(t, int) or t >= 2:
                    pe.wait_ge(s_yo, t - 1)
                for j in range(4):
                    last = mm_(bank[b][:, 0:D], swb[:, b, j, :], Z[:, j, :], start=(j == 0), stop=(j == 3))
                last.then_inc(s_y, 1)
            pe.wait_ge(s_fa, 6)
            for t in range(2):
                ffn2(t, t)
            with pe.Fori(1, NT // 2) as i:
                for u in range(2):
                    ffn2(2 * i + u, u)
            ffn2(NT - 1, 0)

        @block.vector
        def _(v):
            own = Chain(v, s_dv)
            v.memset(ed[PAD_BASE:ROWS, :], N).then_inc(s_pad, 1)
            v.memset(es[PAD_BASE:ROWS, :], 0).then_inc(s_pad, 1)
            v.wait_ge(s_ed, 32)
            own.add(v.tensor_scalar(emi[:, :], ed[:, :], P - 1, None, ALU.bitwise_and))
            own.add(v.tensor_copy(edf[:, :], ed[:, :]))
            v.wait_ge(s_es, 32)
            v.tensor_copy(esf[:, :], es[:, :]).then_inc(s_ef, 1)
            own.wait()
            v.tensor_copy(emf[:, :], emi[:, :]).then_inc(s_ef, 1)
            v.tensor_copy(emb[:, :], emi[:, :]).then_inc(s_ef, 1)
            v.tensor_reduce(mm[:, 0:1], edf[:, :], X, ALU.min).then_inc(s_ef, 1)
            v.tensor_reduce(mm[:, 1:2], edf[:, :], X, ALU.max).then_inc(s_ef, 1)
            v.wait_ge(s_w, 16 * 5)
            for i in range(2):
                for k in range(2):
                    own.add(v.tensor_tensor(watt[:, k, :], Wg[:, k, 0:D], attb[:, i, :], ALU.mult))
                own.wait()
                own.add(v.tensor_reduce(Wg[:, :, D + i * H:D + (i + 1) * H],
                                        watt[:, :, :].rearrange("p k (h c) -> p k h c", c=C), X, ALU.add))
                own.wait()
            for i in range(XL):
                v.wait_ge(s_x[i], 16)
            with v.Fori(0, NT) as t:
                v.bn_stats(st[:, bass.ds(t, 1), :], xs[:, bass.ds(t, 1), :]).then_inc(s_bn, 1)
            v.wait_ge(s_bn, NT)
            own.add(v.tensor_tensor(mv[:, :, 0], st[:, :, 1], st[:, :, 4], ALU.subtract))
            own.add(v.tensor_tensor(mv[:, :, 1], st[:, :, 2], st[:, :, 5], ALU.add))
            own.wait()
            own.add(v.tensor_tensor(mv[:, :, 0], mv[:, :, 0], mv[:, :, 0], ALU.mult))
            own.add(v.tensor_scalar(mv[:, :, 1], mv[:, :, 1], 1.0 / D, EPS, ALU.mult, ALU.add))
            own.wait()
            v.scalar_tensor_tensor(mv[:, :, 1], mv[:, :, 0], 0.25, mv[:, :, 1], ALU.mult, ALU.add).then_inc(s_var, 1)
            own.wait()
            v.wait_ge(s_var, 1)
            own.add(v.tensor_tensor(mv[:, :, 0], st[:, :, 1], st[:, :, 4], ALU.add))
            own.wait()
            own.add(v.tensor_scalar(mv[:, :, 0], mv[:, :, 0], 0.5, None, ALU.mult))
            v.wait_ge(s_w2, 16 * 12)
            own.add(v.tensor_scalar(tmp8[:, :], tmp8[:, :], 0.1, 5.0, ALU.max, ALU.min))
            own.wait()
            own.add(v.reciprocal(itemp[:, :], tmp8[:, :]))
            own.wait()
            v.wait_ge(s_wl, 2)
            it2 = itemp[:, :].rearrange("p (j o) -> p o j", o=2)
            for k in range(2):
                for o in range(2):
                    last = v.tensor_tensor(Wl[:, k, :].rearrange("p (j o g) -> p o j g", o=2, g=G)[:, o],
                                           bank[2 + k + 2 * o][:, 0:HG // 2].rearrange("p (j g) -> p j g", g=G),
                                           it2[:, o].unsqueeze(2).broadcast_to((P, FH // 2, G)), ALU.mult)
                last.then_inc(s_wlc, 1)
            v.wait_ge(s_wl, 3)
            own.add(v.tensor_tensor(by_head(bl[:, :]), by_head(bank[0][0:1, :]), bsl[:, :].unsqueeze(1).broadcast_to((1, FH, G)), ALU.add))
            own.wait()
            v.tensor_tensor(by_head(bl[:, :]), by_head(bl[:, :]), over_slices(itemp[0:1, :]), ALU.mult).then_inc(s_wlc, 1)
            v.wait_ge(s_eT, 1)
            v.tensor_copy(idx[:, :].rearrange("p (q i) -> p q i", i=4), bank[0][:, 0:4 * ROWS].rearrange("p (i q) -> p q i", i=4)).then_inc(s_idx, 1)
            own.add(v.tensor_copy(slot[:, :].rearrange("p (q i) -> p q i", i=4), bank[1][:, 0:4 * ROWS].rearrange("p (i q) -> p q i", i=4)))
            v.wait_ge(s_eT, 2)
            own.add(v.tensor_reduce(gmm[:, 0, :], bank[2][0:1, 0:ROWS].rearrange("p (g r) -> p g r", r=RPG), X, ALU.min))
            own.add(v.tensor_reduce(gmm[:, 1, :], bank[2][0:1, ROWS:2 * ROWS].rearrange("p (g r) -> p g r", r=RPG), X, ALU.max))
            own.wait()
            own.add(v.tensor_copy(gi[:, :], gmm[:, 0, :]))
            own.add(v.tensor_tensor(gmm[:, 1, :], gmm[:, 1, :], gmm[:, 0, :], ALU.subtract))
            own.wait()
            own.add(v.tensor_reduce(flagf[:, 0:1], gmm[:, 1, :], X, ALU.max))
            own.add(v.tensor_scalar(gblk[:, :], gi[:, :], 7, None, ALU.arith_shift_right))
            own.add(v.tensor_scalar(gmi[:, :], gi[:, :], P - 1, None, ALU.bitwise_and))
            own.wait()
            v.tensor_copy(gmf[:, :], gmi[:, :]).then_inc(s_gm, 1)
            v.wait_ge(s_gmT, 1)
            v.wait_ge(s_const, 8)
            own.add(v.tensor_scalar(mhi[:, :], bank[3][:, 0:NG], lane[:, :], None, ALU.is_le))
            own.add(v.tensor_scalar(mlo[:, :], bank[3][:, 0:NG], lane[:, :], None, ALU.is_gt))

            v.wait_ge(s_sd, 1)
            own.add(v.reciprocal(rstd[:, :], rstd[:, :]))
            own.wait()

            def norm(t, b):
                if not isinstance(t, int) or t >= 2:
                    v.wait_ge(s_xnT, t - 1)
                v.tensor_scalar(xn[:, b, 0:D], flat(xs[:, bass.ds(t, 1), :]), mv[:, bass.ds(t, 1), 0], rstd[:, bass.ds(t, 1)],
                                ALU.subtract, ALU.mult).then_inc(s_xn, 1)

            def take(t, b):
                v.wait_ge(s_xp, t + 1)
                v.tensor_copy(flat(acc[:, bass.ds(t, 1), :]), bank[5 + b][:, 0:AW]).then_inc(s_xpc, 1)
            norm(0, 0)
            norm(1, 1)
            take(0, 0)
            norm(2, 0)
            with v.Fori(0, (NT - 3) // 2) as i:
                for u in range(2):
                    t0 = 2 * i + 1
                    take(t0 + u, (u + 1) % 2)
                    norm(t0 + u + 2, (u + 1) % 2)
            take(NT - 2, 1)
            take(NT - 1, 0)
            v.wait_ge(s_xpc, NT)
            a_src = acc[:, 0:NT, D:D + H]
            a_dst = acc[:, 0:NT, D + H:D + 2 * H]
            v.tensor_copy(ee[:, :, 2 * H:3 * H], a_src).then_inc(s_ea, 1)
            own.add(v.tensor_reduce(r8[:, 0:H], a_src.rearrange("p t h -> p h t"), X, ALU.max))
            own.add(v.tensor_reduce(r8[:, H:2 * H], a_src.rearrange("p t h -> p h t"), X, ALU.min))
            own.wait()
            v.tensor_scalar(r8[:, H:2 * H], r8[:, H:2 * H], -1.0, None, ALU.mult).then_inc(s_r8, 1)
            v.wait_ge(s_r8T, 1)
            own.add(v.tensor_reduce(g8[:, :], bank[0][0:2 * H, 0:P], X, ALU.max))
            own.wait()
            v.tensor_scalar(dg8[:, :], ident[0:2 * H, 0:2 * H], g8[:, :], None, ALU.mult).then_inc(s_dg, 1)
            v.wait_ge(s_G, 1)
            own.add(v.tensor_copy(Gb[:, :], bank[1][:, 0:2 * H]))
            own.wait()
            Gx = Gb[:, 0:H].unsqueeze(1).broadcast_to((P, NT, H))
            v.tensor_tensor(ee[:, :, 0:H], a_src, Gx, ALU.subtract).then_inc(s_ea, 1)
            own.add(v.tensor_tensor(uv[:, :, 0:H], a_dst, Gx, ALU.add))
            own.add(v.tensor_tensor(spr[:, :], Gb[0:1, 0:H], Gb[0:1, H:2 * H], ALU.add))
            own.wait()
            own.add(v.tensor_scalar(uv[:, :, H:2 * H], uv[:, :, 0:H], 0.2, None, ALU.mult))
            own.add(v.tensor_reduce(flagf[:, 1:2], spr[:, :], X, ALU.max))
            own.wait()
            own.add(v.tensor_tensor(uu[:, :, :], uv[:, :, 0:H], uv[:, :, H:2 * H], ALU.max))
            own.add(v.tensor_scalar(flagf[:, 0:1], flagf[:, 0:1], P - 0.5, None, ALU.is_gt))
            own.add(v.tensor_scalar(flagf[:, 1:2], flagf[:, 1:2], SPREAD, None, ALU.is_gt))
            own.wait()
            own.add(v.tensor_tensor(uv[:, :, 0:H], uv[:, :, 0:H], uu[:, :, :], ALU.subtract))
            v.tensor_tensor(uv[:, :, H:2 * H], uv[:, :, H:2 * H], uu[:, :, :], ALU.subtract).then_inc(s_ea, 1)
            own.add(v.tensor_tensor(flagf[:, 2:3], flagf[:, 0:1], flagf[:, 1:2], ALU.max))
            own.wait()
            v.tensor_copy(flag[:, :], flagf[:, 2:3]).then_inc(s_flag, 1)

            def quick():
                v.wait_ge(s_ex, 3)
                own.add(v.tensor_copy(ab3[:, 0:NT, :, 0], ab[:, :, :]))
                own.add(v.tensor_tensor(uv[:, :, :], ab[:, :, :], ee[:, :, 0:2 * H], ALU.mult))
                own.wait()
                own.add(v.tensor_tensor(abr[:, :, :], ab[:, :, :], ab3[:, 0:NT, :, 0], ALU.subtract))
                wself = bank[7][:, 0:NT * H].rearrange("p (t h) -> p t h", h=H)
                own.add(v.tensor_tensor(wself, uv[:, :, 0:H], uv[:, :, H:2 * H], ALU.max))
                own.add(v.tensor_tensor(a_src, uv[:, :, 0:H], uv[:, :, H:2 * H], ALU.max))
                own.wait()
                own.add(v.tensor_copy(ab3[:, 0:NT, :, 1], abr[:, :, :]))
                own.wait()
                own.add(v.tensor_tensor(abr[:, :, :], abr[:, :, :], ab3[:, 0:NT, :, 1], ALU.subtract))
                own.wait()
                own.add(v.tensor_copy(ab3[:, 0:NT, :, 2], abr[:, :, :]))
                v.wait_ge(s_tab, 16 * NT)
                xp4 = acc[:, 0:NT, 0:D].rearrange("p t (h c) -> p t h c", c=C)
                for t in range(NT):
                    own.add(v.tensor_tensor(xp4[:, t], xp4[:, t], wself[:, t].unsqueeze(2).broadcast_to((P, H, C)), ALU.mult))
                own.wait()

                def hot(i, u):
                    g, b = NB * i + u, u % 2
                    first = isinstance(i, int) and g < 2
                    blk = v.value_load(gblk[0:1, bass.ds(g, 1)], min_val=0, max_val=NT - 1)
                    v.wait_ge(s_db[b], 16 * (NB // 2 * i + u // 2 + 1))
                    if not first:
                        v.wait_ge(s_lk, g - 1)
                        v.wait_ge(s_mm, g - 1)
                    v.tensor_scalar(tsa[:, b, :], abs3(blk), mhi[:, bass.ds(g, 1)], None, ALU.mult).then_inc(s_ta, 1)
                    v.tensor_scalar(ot[:, b, :], db[:, b, :], lane[:, :], None, ALU.is_equal).then_inc(s_ot, 1)
                    v.wait_ge(s_ta, g + 1)
                    v.scalar_tensor_tensor(tsl[:, b, :], abs3(blk + 1), mlo[:, bass.ds(g, 1)], tsa[:, b, :],
                                           ALU.mult, ALU.add).then_inc(s_ts, 1)
                    for c in range(CPG):
                        last = v.tensor_scalar(oh[:, b, c, :], cols[:, :], slot[:, bass.ds(g * CPG + c, 1)], None, ALU.is_equal)
                    last.then_inc(s_oh, 1)

                def weigh(i, u):
                    g, b = NB * i + u, u % 2
                    v.wait_ge(s_lk, g + 1)
                    v.tensor_reduce(abe[:, b, :, :], bank[b][:, 0:CPG * 24].rearrange("p (c e k) -> p c e k", c=CPG, k=3), X, ALU.add).then_inc(s_ab, 1)
                    v.wait_ge(s_gat[u], 16 * CPG * (i + 1))
                    v.wait_ge(s_ab, g + 1)
                    v.tensor_tensor(we[:, b, :, :], abe[:, b, :, :], gt[:, u, :, D:D + 2 * H], ALU.mult).then_inc(s_we, 1)
                    v.wait_ge(s_we, g + 1)
                    wp = bank[4][:, b * 32:b * 32 + CPG * H].rearrange("p (c h) -> p c h", h=H)
                    v.tensor_tensor(wp, we[:, b, :, 0:H], we[:, b, :, H:2 * H], ALU.max).then_inc(s_wp, 1)
                    v.tensor_tensor(gt[:, u, :, D:D + H], we[:, b, :, 0:H], we[:, b, :, H:2 * H], ALU.max)
                    v.wait_ge(s_wp, g + 1)
                    for c in range(CPG):
                        r = gt[:, u, c, 0:D].rearrange("p (h k) -> p h k", k=C)
                        last = v.tensor_tensor(r, r, wp[:, c, :].unsqueeze(2).broadcast_to((P, H, C)), ALU.mult)
                    last.then_inc(s_sc, 1)

                def merge(i, u):
                    g, b = NB * i + u, u % 2
                    blk = v.value_load(gblk[0:1, bass.ds(g, 1)], min_val=0, max_val=NT - 1)
                    v.wait_ge(s_mm, g + 1)
                    if not (isinstance(i, int) and g == 0):
                        v.wait_ge(s_mg, g)
                    for m, k in ((mhi, 0), (mlo, 1)):
                        a = flat(acc[:, bass.ds(blk + k, 1), 0:D + H])
                        last = v.scalar_tensor_tensor(a, bank[2 + b][:, 0:D + H], m[:, bass.ds(g, 1)], a, ALU.mult, ALU.add)
                    last.then_inc(s_mg, 1)

                def step(i, u, more=True):
                    if more:
                        hot(i + (u + 1) // NB, (u + 1) % NB)
                    weigh(i, u)
                    if u > 0 or not (isinstance(i, int) and i == 0):
                        merge(i - (u == 0), (u - 1) % NB)
                hot(0, 0)
                for u in range(NB):
                    step(0, u)
                with v.Fori(1, NG // NB - 1) as i:
                    for u in range(NB):
                        step(i, u)
                for u in range(NB):
                    step(NG // NB - 1, u, more=(u < NB - 1))
                merge(NG // NB - 1, NB - 1)
                v.wait_ge(s_mg, NG)

            quick()

            def ffn1(t, b):
                at = flat(acc[:, bass.ds(t, 1), :])
                xt = flat(xs[:, bass.ds(t, 1), :])
                o = Own(v, s_own, t * 10)
                o.add(v.reciprocal(rden[:, b, :], at[:, D:D + H]))
                o.wait()
                for h in range(H):
                    s = slice(h * C, (h + 1) * C)
                    ins = v.scalar_tensor_tensor(z[:, b, s], at[:, s], rden[:, b, h:h + 1], gb[:, s], ALU.mult, ALU.add)
                o.add(ins)
                o.wait()
                v.tensor_scalar(zm[:, b, :], z[:, b, :], 0.0, None, ALU.min).then_inc(s_min, 1)
                o.add(v.tensor_scalar(z[:, b, :], z[:, b, :], 0.0, -1.0, ALU.max, ALU.add))
                o.wait()
                o.add(v.tensor_tensor(z[:, b, :], z[:, b, :], xt, ALU.add))
                o.wait()
                v.wait_ge(s_exm, t + 1)
                o.add(v.tensor_tensor(z[:, b, :], z[:, b, :], ze[:, b, :], ALU.add))
                o.wait()
                o.add(v.bn_stats(st[:, 0, :], z[:, b, :]))
                o.wait()
                v.sem_inc(s_turn_v, 1)
                o.add(v.bn_aggr(mv[:, 0, :], st[:, 0, :]))
                o.wait()
                v.tensor_scalar(mv[:, 0, 1:2], mv[:, 0, 1:2], EPS, None, ALU.add).then_inc(s_var2, 1)
                v.wait_ge(s_rs, t + 1)
                if not isinstance(t, int) or t >= 2:
                    v.wait_ge(s_tok, t - 1)
                v.tensor_scalar(xn[:, b, 0:D], z[:, b, :], mv[:, 0, 0:1], rstd[:, 0:1], ALU.subtract, ALU.mult).then_inc(s_n2, 1)
                v.tensor_tensor(xt, z[:, b, :], bo[:, :], ALU.add).then_inc(s_res, 1)
                v.wait_ge(s_lg, t + 1)
                o.add(v.tensor_reduce(mx[:, b, :], by_head(bank[5 + b][:, :]), X, ALU.max))
                o.wait()
                v.tensor_tensor(by_head(lg[:, b, :]), by_head(bank[5 + b][:, :]), over_slices(mx[:, b, :]), ALU.subtract).then_inc(s_sub, 1)
                v.wait_ge(s_exl, t + 1)
                o.add(v.tensor_reduce(sm[:, b, :], by_head(bank[5 + b][:, :]), X, ALU.add))
                o.wait()
                o.add(v.reciprocal(sm[:, b, :], sm[:, b, :]))
                o.wait()
                v.tensor_tensor(by_head(sw[:, b, :]), by_head(bank[5 + b][:, :]), over_slices(sm[:, b, :]), ALU.mult).then_inc(s_sw, 1)
                assert o.k == 10
            for t in range(2):
                ffn1(t, t)
            with v.Fori(1, NT // 2) as i:
                for u in range(2):
                    ffn1(2 * i + u, u)
            ffn1(NT - 1, 0)

            v.wait_ge(s_tok, NT)
            for j in range(4):
                last = v.tensor_scalar(nrm[:, 0, j:j + 1], TOK[j][:, D:D + 1], 1e-5, None, ALU.add)
            own.add(last)
            own.wait()
            own.add(v.reciprocal(nrm[:, 1, :], nrm[:, 0, :]))
            own.wait()
            for j in range(4):
                last = v.tensor_scalar(tokn[:, j, :], TOK[j], nrm[:, 1, j:j + 1], None, ALU.mult)
            last.then_inc(s_f, 1)
            v.wait_ge(s_fp, 1)
            v.tensor_copy(nrow, bank[7][0:1, :]).then_inc(s_f, 1)
            v.wait_ge(s_fp, 4)
            v.tensor_copy(stT, bank[0][0:G, :]).then_inc(s_f, 1)
            v.wait_ge(s_fp, 6)
            v.tensor_copy(qkv[:, 1, :], bank[2][0:G, :]).then_inc(s_kc, 1)
            v.tensor_copy(qkv[:, 2, :], bank[3][0:G, :]).then_inc(s_kc, 1)
            v.wait_ge(s_fp, 7)
            own.add(v.tensor_reduce(amx[:, 0, :], by_head(bank[0][0:G, :]), X, ALU.max))
            own.wait()
            v.tensor_tensor(by_head(at_s[:, :]), by_head(bank[0][0:G, :]), over_slices(amx[:, 0, :]), ALU.subtract).then_inc(s_f, 1)
            v.wait_ge(s_fa, 4)
            own.add(v.tensor_reduce(amx[:, 0, :], by_head(at_e[:, :]), X, ALU.add))
            own.wait()
            own.add(v.reciprocal(amx[:, 1, :], amx[:, 0, :]))
            own.wait()
            v.tensor_tensor(by_head(at_s[:, :]), by_head(at_e[:, :]), over_slices(amx[:, 1, :]), ALU.mult).then_inc(s_f, 1)
            v.wait_ge(s_fp, 8)
            v.tensor_copy(at_T[:, :], bank[1][0:G, :]).then_inc(s_f, 1)
            v.wait_ge(s_os, 1)
            v.tensor_copy(osT[:, :], bank[2][0:G, :]).then_inc(s_f, 1)

            def ffn2(t, b):
                v.wait_ge(s_y, t + 1)
                if not isinstance(t, int) or t >= 2:
                    v.wait_ge(s_st[b], 16 * half(t))
                v.tensor_tensor(y[:, b, :], bank[b][:, 0:D], flat(xs[:, bass.ds(t, 1), :]), ALU.add).then_inc(s_yo, 1)

            def half(t):
                return t // 2 if isinstance(t, int) else t
            for t in range(2):
                ffn2(t, t)
            with v.Fori(1, NT // 2) as i:
                for u in range(2):
                    t = 2 * i + u
                    v.wait_ge(s_y, t + 1)
                    v.wait_ge(s_st[u], 16 * i)
                    v.tensor_tensor(y[:, u, :], bank[u][:, 0:D], flat(xs[:, bass.ds(t, 1), :]), ALU.add).then_inc(s_yo, 1)
            ffn2(NT - 1, 0)


_INS = ['x', 'src', 'dst', 'L0_gnn_W', 'L0_gnn_att_src', 'L0_gnn_att_dst', 'L0_gnn_bias', 'L0_ffn_W_fx', 'L0_ffn_b_fx',
        'L0_ffn_W_x', 'L0_ffn_b_x', 'L0_ffn_W_slice', 'L0_ffn_b_slice', 'L0_ffn_W_q', 'L0_ffn_W_k', 'L0_ffn_W_v',
        'L0_ffn_W_out', 'L0_ffn_b_out', 'L0_ffn_temperature']


def kernel(**inputs):
    import numpy as _np
    import concourse.bacc as _bacc
    from concourse import mybir as _mybir
    from concourse.bass_utils import run_bass_kernel_spmd as _run

    nc = _bacc.Bacc("TRN2", target_bir_lowering=False, num_devices=1)
    arrays, args = {}, []
    for name in _INS:
        a = _np.ascontiguousarray(inputs[name])
        arrays[f"in_{name}_dram"] = a
        args.append(nc.dram_tensor(f"in_{name}_dram", a.shape, _mybir.dt.from_np(a.dtype), kind="ExternalInput").ap())
    x = inputs['x']
    args.append(nc.dram_tensor("out_0_dram", tuple(x.shape), _mybir.dt.float32, kind="ExternalOutput").ap())
    build(nc, *args)
    r = _run(nc, [arrays], core_ids=[0])
    return r.results[0]["out_0_dram"]
```

```python
from contextlib import ExitStack

import concourse.bass as bass
from concourse import mybir

F32 = mybir.dt.float32
BF16 = mybir.dt.bfloat16
I32 = mybir.dt.int32
ALU = mybir.AluOpType
ACT = mybir.ActivationFunctionType
X = mybir.AxisListType.X

P = 128
ROW = 512
CPG = 8
GE = CPG * P
SPREAD = 60.0
EPS = 1e-5


class Own:

    def __init__(self, eng, sem, base):
        self.eng, self.sem, self.base, self.k = eng, sem, base, 0

    def add(self, ins):
        ins.then_inc(self.sem, 1)
        self.k += 1

    def wait(self):
        self.eng.wait_ge(self.sem, self.base + self.k)


class Chain:

    def __init__(self, eng, sem):
        self.eng, self.sem, self.base, self.k = eng, sem, 0, 0

    def add(self, ins):
        ins.then_inc(self.sem, 1)
        self.k += 1
        return ins

    def wait(self):
        self.eng.wait_ge(self.sem, self.base + self.k)


def build(nc, x, src, dst, W, att_src, att_dst, gbias, W_fx, b_fx, W_x, b_x, W_slice, b_slice,
          W_q, W_k, W_v, W_out, b_out, temperature, out):
    N, D = x.shape
    E = src.shape[0]
    H, C = att_src.shape
    FH = temperature.shape[1]
    G = W_slice.shape[1]
    HG = FH * G
    NT = -(-N // P)
    LAST = N - (NT - 1) * P
    NG = -(-E // GE)
    NG += NG % 2
    ROWS = NG * GE // ROW
    FULL = E // ROW
    REST = E - FULL * ROW
    TW = D + 3 * H
    AW = D + 2 * H
    RPG = GE // ROW
    NB = 4
    PAD_BASE = (ROWS // 32) * 32 if ROWS % 32 else ROWS - 32
    assert D == 256 and H * C == D and HG == 512 and G == 64 and NT % 2 == 1 and NG % NB == 0 and ROWS <= P
    assert FULL >= PAD_BASE and LAST < P

    table = nc.dram_tensor("table", [NT * P, TW], F32, kind="Internal").ap()
    slots_d = nc.dram_tensor("slots_d", [ROWS, ROW], BF16, kind="Internal").ap()

    ctx = ExitStack()
    with ctx:
        def sb(name, shape, dt=F32):
            return ctx.enter_context(nc.sbuf_tensor(name, shape, dt))

        def sem(name):
            return ctx.enter_context(nc.semaphore(name))

        bank = [ctx.enter_context(nc.psum_tensor(f"bank{i}", [P, 512], F32)) for i in range(8)]

        def carve(region, sizes):
            at, views = 0, {}
            for name, parts, shape, dt in sizes:
                n = 1
                for k in shape:
                    n *= k
                a = region[0:parts, at:at + n]
                if dt != F32:
                    a = a.bitcast(dt)
                if len(shape) == 2:
                    a = a.rearrange("p (a b) -> p a b", a=shape[0])
                if len(shape) == 3:
                    a = a.rearrange("p (a b c) -> p a b c", a=shape[0], b=shape[1])
                views[name] = a
                at += n
            assert at <= region.shape[1]
            return views

        swT_r = sb("swT_r", [P, max(4 * NT * P, 7424)])
        swT = swT_r[:, 0:4 * NT * P].rearrange("p (j n) -> p j n", j=4)
        prep = carve(swT_r, [("es", ROWS, [ROW], I32), ("ed", ROWS, [ROW], I32), ("esf", ROWS, [ROW], F32),
                             ("edf", ROWS, [ROW], F32), ("emi", ROWS, [ROW], I32), ("emf", ROWS, [ROW], F32),
                             ("Wx", P, [2, HG], F32), ("WxT", P, [4, D], F32), ("attb", P, [2, D], F32), ("watt", P, [2, D], F32),
                             ("uv", P, [NT, 2 * H], F32), ("uu", P, [NT, H], F32), ("ab", P, [NT, 2 * H], F32), ("abr", P, [NT, 2 * H], F32)])
        es, ed, esf, edf, emi, emf, Wx, WxT, attb, watt, uv, uu, ab, abr = (prep[k] for k in prep)

        gt_r = sb("gt_r", [P, NB * CPG * TW])
        gt = gt_r[:, :].rearrange("p (b c e) -> p b c e", b=NB, c=CPG)
        late = carve(gt_r, [("tokn", P, [4, D + 1], F32), ("tokT", P, [2, HG], F32), ("nrow", 1, [HG], F32), ("stT", G, [HG], F32),
                            ("qkv", G, [3, HG], F32), ("at_s", G, [HG], F32), ("at_e", G, [HG], F32),
                            ("osT", G, [HG], F32), ("Z", P, [4, D], F32), ("swb", P, [2, 4, P], F32)])
        tokn, tokT, nrow, stT, qkv, at_s, at_e, osT, Z, swb = (late[k] for k in late)
        at_T = at_e
        amx = sb("amx", [G, 2, FH])
        nrm = sb("nrm", [P, 2, 4])

        ident = sb("ident", [P, P])
        lane_i = sb("lane_i", [P, 1], I32)
        lane = sb("lane", [P, 1])
        cols_i = sb("cols_i", [P, P], I32)
        cols = sb("cols", [P, P])
        ones = sb("ones", [P, P])
        Wg = sb("Wg", [P, 2, D + 2 * H])
        gb = sb("gb", [P, D])
        bo = sb("bo", [P, D])
        Ws2 = sb("Ws2", [P, G])
        bxT = sb("bxT", [G, FH])
        bsl = sb("bsl", [1, G])
        tmp8 = sb("tmp8", [P, FH])
        itemp = sb("itemp", [P, FH])
        Wl = sb("Wl", [P, 2, HG])
        bl = sb("bl", [1, HG])
        Wf = sb("Wf", [P, 2, HG])
        bf = sb("bf", [1, HG])
        Wq = sb("Wq", [G, 3, G])
        Wo = sb("Wo", [G, FH, D])

        emb = sb("emb", [ROWS, ROW], BF16)
        mm = sb("mm", [ROWS, 2])
        idx = sb("idx", [P, ROWS * 4], I32)
        idxg = sb("idxg", [P, NB, CPG], I32)
        slot = sb("slot", [P, ROWS * 4])
        gmm = sb("gmm", [1, 2, NG])
        gi = sb("gi", [1, NG], I32)
        gblk = sb("gblk", [1, NG], I32)
        gmi = sb("gmi", [1, NG], I32)
        gmf = sb("gmf", [1, NG])
        mhi = sb("mhi", [P, NG])
        mlo = sb("mlo", [P, NG])
        flagf = sb("flagf", [1, 4])
        spr = sb("spr", [1, H])
        flag = sb("flag", [1, 1], I32)

        xs = sb("xs", [P, NT, D])
        st = sb("st", [P, NT, 6])
        mv = sb("mv", [P, NT, 2])
        rstd = sb("rstd", [P, NT])
        xn = sb("xn", [P, 2, D])
        xT = sb("xT", [P, 2, D])
        acc = sb("acc", [P, NT + 1, AW])
        r8 = sb("r8", [P, 2 * H])
        g8 = sb("g8", [2 * H, 1])
        dg8 = sb("dg8", [2 * H, 2 * H])
        Gb = sb("Gb", [P, 2 * H])
        ee = sb("ee", [P, NT, 3 * H])
        ab3 = sb("ab3", [P, NT + 1, 2 * H, 3], BF16)

        db = sb("db", [P, 2, GE], BF16)
        ot = sb("ot", [P, 2, GE], BF16)
        oh = sb("oh", [P, 2, CPG, P])
        tsa = sb("tsa", [P, 2, 2 * H * 3], BF16)
        tsl = sb("tsl", [P, 2, 2 * H * 3], BF16)
        abe = sb("abe", [P, 2, CPG, 2 * H])
        we = sb("we", [P, 2, CPG, 2 * H])

        NCH = ROWS * 4
        dst_d = nc.dram_tensor("dst_d", [NCH, P], F32, kind="Internal").ap()
        BIG = 1e30
        xrow = gt[:, 0, 0, :]
        xdst = db[:, 0, 0:2 * P].bitcast(F32)
        xhot, xpen, xhotT = oh[:, 0, 0, :], oh[:, 0, 1, :], oh[:, 0, 2, :]
        xdiag, xtmp = oh[:, 1, 0:H, :], oh[:, 1, H:2 * H, :]
        xnode = sb("xnode", [P, 1])
        xmax = sb("xmax", [P, H])
        xred = sb("xred", [P, H])
        xtbl = sb("xtbl", [P, 2 * H])
        xs1 = sb("xs1", [P, H])
        xs2 = sb("xs2", [P, H])
        xw = sb("xw", [P, H])
        idx_of = lambda k: idx[:, bass.ds(k, 1)]

        rden = sb("rden", [P, H])
        z = sb("z", [P, D])
        zr = sb("zr", [P, D])
        stf = sb("stf", [P, 6])
        mvf = sb("mvf", [P, 2, 2])
        sdf = sb("sdf", [P, 2, 1])
        xTf = sb("xTf", [P, D])
        mx = sb("mx", [P, FH])
        sm = sb("sm", [P, FH])
        sw = sb("sw", [P, HG])
        nrt = sb("nrt", [P, NT, 4])
        blb = sb("blb", [P, HG], BF16)
        blr = sb("blr", [1, HG])
        onesb = sb("onesb", [P, P], BF16)
        y = sb("y", [P, 2, D])
        thr_i = sb("thr_i", [1, NG + NB], I32)
        thr = sb("thr", [1, NG + NB])

        s_w = sem("s_w"); s_w2 = sem("s_w2"); s_es = sem("s_es"); s_ed = sem("s_ed")
        s_x = [sem(f"s_x{i}") for i in range(5)]
        s_pool = sem("s_pool"); s_const = sem("s_const")
        s_ef = sem("s_ef"); s_sl_st = sem("s_sl_st"); s_eT = sem("s_eT"); s_eTc = sem("s_eTc")
        s_gm = sem("s_gm"); s_gmT = sem("s_gmT"); s_idx = sem("s_idx"); s_flag = sem("s_flag")
        s_wxT = sem("s_wxT"); s_wxTc = sem("s_wxTc"); s_wl = sem("s_wl"); s_wlc = sem("s_wlc")
        s_var = sem("s_var"); s_sd = sem("s_sd"); s_xn = sem("s_xn"); s_xnT = sem("s_xnT"); s_xTc = sem("s_xTc")
        s_xp = sem("s_xp"); s_xpc = sem("s_xpc"); s_tab = sem("s_tab"); s_r8 = sem("s_r8"); s_r8T = sem("s_r8T")
        s_dg = sem("s_dg"); s_G = sem("s_G"); s_ea = sem("s_ea"); s_ex = sem("s_ex"); s_tab2 = sem("s_tab2")
        s_gat = [sem(f"s_gat{i}") for i in range(NB)]
        s_db = [sem(f"s_db{i}") for i in range(2)]
        s_ot = sem("s_ot"); s_ts = sem("s_ts"); s_oh = sem("s_oh"); s_lk = sem("s_lk"); s_ab = sem("s_ab")
        s_sc = sem("s_sc"); s_mm = sem("s_mm"); s_mg = sem("s_mg")
        x_dst = sem("x_dst"); x_go = sem("x_go"); x_ix = sem("x_ix"); x_gat = sem("x_gat"); x_db = sem("x_db")
        x_diag = sem("x_diag"); x_bc = sem("x_bc"); x_self = sem("x_self"); x_selfe = sem("x_selfe")
        x_hot = sem("x_hot"); x_lk = sem("x_lk"); x_arg = sem("x_arg"); x_exp = sem("x_exp"); x_rows = sem("x_rows")
        x_sum = sem("x_sum"); x_own = sem("x_own"); x_turn = sem("x_turn"); x_turn_v = sem("x_turn_v"); x_turn_p = sem("x_turn_p")
        s_rd = sem("s_rd"); s_zz = sem("s_zz"); s_z = sem("s_z"); s_r = sem("s_r"); s_e = sem("s_e"); s_sd2 = sem("s_sd2")
        s_nm = sem("s_nm"); s_ownA = sem("s_ownA"); s_ownB = sem("s_ownB"); s_thr = sem("s_thr"); s_xT1 = sem("s_xT1")
        s_n2 = sem("s_n2"); s_n2T = sem("s_n2T"); s_n2c = sem("s_n2c")
        s_lg = sem("s_lg"); s_exl = sem("s_exl"); s_sw = sem("s_sw"); s_tok = sem("s_tok")
        s_swT = sem("s_swT"); s_swc = sem("s_swc")
        s_f = sem("s_f"); s_fp = sem("s_fp"); s_fa = sem("s_fa")
        s_cp = sem("s_cp"); s_y = sem("s_y"); s_yo = sem("s_yo")
        s_st = [sem(f"s_st{i}") for i in range(2)]
        s_dv = sem("s_dv"); s_ix = sem("s_ix"); s_quick = sem("s_quick"); s_pad = sem("s_pad"); s_turn = sem("s_turn"); s_turn_v = sem("s_turn_v"); s_var2 = sem("s_var2"); s_rs = sem("s_rs"); s_own = sem("s_own"); s_bn = sem("s_bn"); s_ta = sem("s_ta"); s_we = sem("s_we"); s_wp = sem("s_wp")
        s_res = sem("s_res"); s_kc = sem("s_kc"); s_os = sem("s_os")

        pT = bank[4]
        TOK = [bank[j // 2][:, (j % 2) * D:(j % 2 + 1) * D] for j in range(4)]
        SUMS, LOOK, WP, LOGIT, ELU, TR = (bank[i] for i in (2, 3, 4, 5, 6, 7))

        TL = 3
        NI = NG // NB
        TPI = NB // 2
        IN_LOOP = TPI * (NI - TL)
        XB = 6
        XL = -(-(NT - 1) // XB) + 1

        def flat(a):
            return a.rearrange("p a b -> p (a b)")

        def by_head(a):
            return a.rearrange("p (h g) -> p h g", g=G)

        def over_slices(a):
            return a.unsqueeze(2).broadcast_to((a.shape[0], FH, G))

        def abs3(blk):
            return ab3[:, bass.ds(blk, 1), :, :].rearrange("p t e c -> p (t e c)")

        block = ctx.enter_context(nc.Block())

        @block.sync
        def _(sp):
            for i in range(XL - 1):
                a, b = i * XB, min((i + 1) * XB, NT - 1)
                if b > a:
                    sp.dma_start(xs[:, a:b, :], x[a * P:b * P, :].rearrange("(t p) d -> p t d", p=P)).then_inc(s_x[i], 16)
            sp.wait_ge(s_pool, 1)
            sp.dma_start(xs[0:LAST, NT - 1, :], x[(NT - 1) * P:N, :]).then_inc(s_x[XL - 1], 16)
            sp.dma_start(Wx[:, :, :], W_x.rearrange("(k p) n -> p k n", p=P)).then_inc(s_w2, 16)
            sp.dma_start(Ws2[0:G, :], W_slice).then_inc(s_w2, 16)
            sp.dma_start(Ws2[G:P, :], W_slice).then_inc(s_w2, 16)
            sp.dma_start(bxT[:, :], b_x.rearrange("(h c) -> c h", c=G), allow_slow_non_contiguous=True).then_inc(s_w2, 16)
            sp.dma_start(bsl[:, :], b_slice.rearrange("(a n) -> a n", a=1)).then_inc(s_w2, 16)
            sp.dma_start(tmp8[:, :], temperature.rearrange("a h b c -> (a b c) h").broadcast_to((P, FH))).then_inc(s_w2, 16)
            sp.dma_start(Wf[:, :, :], W_fx.rearrange("(k p) n -> p k n", p=P)).then_inc(s_w2, 16)
            sp.dma_start(bf[:, :], b_fx.rearrange("(a n) -> a n", a=1)).then_inc(s_w2, 16)
            for i, w in enumerate((W_q, W_k, W_v)):
                sp.dma_start(Wq[:, i, :], w).then_inc(s_w2, 16)
            sp.dma_start(Wo[:, :, :], W_out.rearrange("(h c) n -> c h n", c=G)).then_inc(s_w2, 16)
            sp.wait_ge(s_ef, 3)
            sp.dma_start(slots_d, emb[:, :]).then_inc(s_sl_st, 16)

            def put(t):
                sp.wait_ge(s_xpc, t + 1)
                sp.dma_start(table[bass.ds(t * P, P), 0:D], acc[:, bass.ds(t, 1), 0:D]).then_inc(s_tab, 16)
            with sp.Fori(0, NT) as t:
                put(t)
            sp.wait_ge(s_ea, 1)
            sp.wait_ge(s_ex, 2)
            sp.dma_start(table[:, D:TW].rearrange("(t p) e -> p t e", p=P), ee[:, :, :]).then_inc(s_tab2, 16)

            def spread_slots(g, b):
                if not isinstance(g, int) or g >= 2:
                    sp.wait_ge(s_ot, g - 1)
                sp.dma_start(db[:, b, :], slots_d.rearrange("(g r) c -> g (r c)", r=RPG)[bass.ds(g, 1), :]
                             .broadcast_to((P, GE))).then_inc(s_db[b], 16)
            sp.wait_ge(s_flag, 1)
            general = sp.value_load(flag[0:1, 0:1], min_val=0, max_val=1)
            sp.wait_ge(s_sl_st, 16)
            with sp.If(general == 0):
                for g in range(NB):
                    spread_slots(g, g % 2)
                with sp.Fori(1, NG // NB) as i:
                    for u in range(NB):
                        spread_slots(NB * i + u, u % 2)
            with sp.Else():
                sp.dma_start(dst_d.rearrange("(r i) c -> r (i c)", i=4), edf[:, :]).then_inc(x_dst, 16)
                sp.wait_ge(x_dst, 16)
                with sp.Fori(0, 2 * NT) as n:
                    with sp.Fori(0, NCH) as k:
                        sp.wait_ge(x_go, n * NCH + k + 1)
                        sp.dma_start(xdst, dst_d[bass.ds(k, 1), :].broadcast_to((P, P))).then_inc(x_db, 16)

            def store(t, b, n):
                sp.wait_ge(s_yo, t + 1)
                sp.dma_start(out[bass.ds(t * P, n), :], y[0:n, b, :]).then_inc(s_st[b], 16)
            with sp.Fori(0, NT // 2) as i:
                for u in range(2):
                    store(2 * i + u, u, P)
            store(NT - 1, 0, LAST)
            sp.wait_ge(s_st[0], 16 * ((NT + 1) // 2))
            sp.wait_ge(s_st[1], 16 * (NT // 2))

        @block.gpsimd
        def _(pool):
            pool.memset(xs[:, NT - 1, :], 0.0).then_inc(s_pool, 1)
            pool.memset(ident[:, :], 0.0).then_inc(s_pool, 1)
            pool.iota(lane_i[:, :], pattern=[[0, 1]], base=0, channel_multiplier=1).then_inc(s_pool, 1)
            pool.iota(cols_i[:, :], pattern=[[1, P]], base=0, channel_multiplier=0).then_inc(s_pool, 1)
            pool.iota(thr_i[:, :], pattern=[[P * TPI, NI + 1], [0, NB]], base=P * TPI * (1 - TL), channel_multiplier=0).then_inc(s_thr, 1)
            pool.wait_ge(s_pool, 4)
            pool.wait_ge(s_thr, 1)
            pool.affine_select(out=ident[:, :], in_=ident[:, :], compare_op=ALU.not_equal, fill=1.0, base=0,
                               pattern=[[-1, P]], channel_multiplier=1).then_inc(s_const, 1)
            pool.tensor_copy(lane[:, :], lane_i[:, :]).then_inc(s_const, 1)
            pool.tensor_copy(cols[:, :], cols_i[:, :]).then_inc(s_const, 1)
            pool.memset(ones[:, :], 1.0).then_inc(s_const, 1)
            pool.memset(onesb[:, :], 1.0).then_inc(s_const, 1)
            pool.memset(acc[:, NT, :], 0.0).then_inc(s_const, 1)
            pool.memset(ab3[:, NT, :, :], 0.0).then_inc(s_const, 1)
            pool.memset(blb[:, :], 0.0).then_inc(s_const, 1)
            pool.wait_ge(s_tab, 16 * NT)
            pool.wait_ge(s_tab2, 16)

            def gather(g, b):
                if not isinstance(g, int) or g >= NB:
                    pool.wait_ge(s_mm, g - NB + 1)
                pool.wait_ge(s_ix, g + 1)
                pool.sem_inc(s_turn, 1)
                for c in range(CPG):
                    pool.indirect_dma_start(
                        gt[:, b, c, :], None, table,
                        bass.IndirectOffsetOnAxis(idxg[:, b, c:c + 1], 0)).then_inc(s_gat[b], 16)
            pool.wait_ge(s_flag, 1)
            general = pool.value_load(flag[0:1, 0:1], min_val=0, max_val=1)
            with pool.If(general == 0):
                for g in range(NB):
                    gather(g, g)
                with pool.Fori(1, NG // NB) as i:
                    for u in range(NB):
                        gather(NB * i + u, u)
            with pool.Else():
                with pool.Fori(0, 2 * NT) as n:
                    with pool.Fori(0, NCH) as k:
                        pool.wait_ge(x_ix, n * NCH + k + 1)
                        pool.sem_inc(x_turn, 1)
                        pool.indirect_dma_start(xrow, None, table, bass.IndirectOffsetOnAxis(idxg[:, 0, 0:1], 0)).then_inc(x_gat, 16)

        @block.scalar
        def _(act):
            act.wait_ge(s_pad, 2)
            act.dma_start(ed[0:FULL, :], dst[0:FULL * ROW].rearrange("(r c) -> r c", c=ROW)).then_inc(s_ed, 16)
            act.dma_start(ed[FULL:FULL + 1, 0:REST], dst[FULL * ROW:E].rearrange("(r c) -> r c", r=1)).then_inc(s_ed, 16)
            act.dma_start(es[0:FULL, :], src[0:FULL * ROW].rearrange("(r c) -> r c", c=ROW)).then_inc(s_es, 16)
            act.dma_start(es[FULL:FULL + 1, 0:REST], src[FULL * ROW:E].rearrange("(r c) -> r c", r=1)).then_inc(s_es, 16)
            act.dma_start(Wg[:, :, 0:D], W.rearrange("(k p) n -> p k n", p=P)).then_inc(s_w, 16)
            for i, a in enumerate((att_src, att_dst)):
                act.dma_start(attb[:, i, :], a.rearrange("(a h) c -> a (h c)", a=1).broadcast_to((P, D))).then_inc(s_w, 16)
            act.dma_start(gb[:, :], gbias.rearrange("(a n) -> a n", a=1).broadcast_to((P, D))).then_inc(s_w, 16)
            act.dma_start(bo[:, :], b_out.rearrange("(a n) -> a n", a=1).broadcast_to((P, D))).then_inc(s_w, 16)
            for k in range(2):
                act.wait_ge(s_wxT, k + 1)
                act.copy(WxT[:, :, k * P:(k + 1) * P], bank[k][:, :].rearrange("p (j n) -> p j n", j=4)).then_inc(s_wxTc, 1)
            act.wait_ge(s_var, 1)
            act.activation(rstd[:, :], mv[:, :, 1], ACT.Sqrt).then_inc(s_sd, 1)

            def evac_xT(t, b):
                act.wait_ge(s_xnT, t + 1)
                act.copy(xT[:, b, :], pT[:, b * D:(b + 1) * D]).then_inc(s_xTc, 1)
            with act.Fori(0, NT // 2) as i:
                for u in range(2):
                    evac_xT(2 * i + u, u)
            evac_xT(NT - 1, 0)
            act.wait_ge(s_idx, 1)
            act.wait_ge(s_ea, 2)
            act.activation(ee[:, :, H:2 * H], ee[:, :, 0:H], ACT.Exp, scale=0.2).then_inc(s_ex, 1)
            act.wait_ge(s_ex, 1)
            act.activation(ee[:, :, 0:H], ee[:, :, 0:H], ACT.Exp).then_inc(s_ex, 1)
            act.wait_ge(s_ea, 3)
            act.activation(ab[:, :, :], uv[:, :, :], ACT.Exp).then_inc(s_ex, 1)

            def half_a(t):
                act.wait_ge(s_rd, t + 1)
                for h in range(H):
                    last = act.activation(ELU[:, h * C:(h + 1) * C], flat(acc[:, bass.ds(t, 1), h * C:(h + 1) * C]), ACT.Copy, scale=rden[:, h:h + 1])
                last.then_inc(s_zz, 1)
                act.wait_ge(s_z, t + 1)
                act.activation(zr[:, :], z[:, :], ACT.Relu, scale=-1.0).then_inc(s_r, 1)
                act.wait_ge(s_r, t + 1)
                act.activation(ELU[:, 0:D], zr[:, :], ACT.Exp, scale=-1.0).then_inc(s_e, 1)

            def root(t, b):
                act.wait_ge(s_var2, t + 1)
                act.activation(sdf[:, b, :], mvf[:, b, 1:2], ACT.Sqrt).then_inc(s_sd2, 1)

            def turn(t):
                act.wait_ge(s_n2T, t + 1)
                act.copy(xTf[:, :], TR[:, 0:D]).then_inc(s_n2c, 1)

            def exps(t):
                act.wait_ge(s_nm, t + 1)
                for h in range(FH):
                    s = slice(h * G, (h + 1) * G)
                    last = act.activation(LOGIT[:, s], LOGIT[:, s], ACT.Exp, bias=mx[:, h:h + 1], accum_out=sm[:, h:h + 1])
                last.then_inc(s_exl, 1)

            def close(t, n=P):
                act.wait_ge(s_swT, t + 1)
                for j in range(4):
                    last = act.activation(swT[:, j, bass.ds(t * P, n)], TR[:, j * P:j * P + n], ACT.Copy,
                                          accum_out=flat(nrt[:, bass.ds(t, 1), j:j + 1]))
                last.then_inc(s_swc, 1)

            def pick(i, u):
                g = NB * i + u
                if not isinstance(i, int) or i >= 1:
                    act.wait_ge(s_we, g - NB + 1)
                act.copy(idxg[:, u, :], idx[:, bass.ds(g * CPG, CPG)]).then_inc(s_ix, 1)

            def iteration(i):
                tiles = not isinstance(i, int) or i >= TL
                for u in range(NB):
                    t = TPI * (i - TL) + u // 2 if tiles else None
                    if tiles and u % 2 == 0:
                        if not (isinstance(i, int) and t == 0):
                            close(t - 1)
                        half_a(t)
                    if tiles and u % 2 == 1:
                        turn(t)
                        exps(t)
                    if not isinstance(i, int) or i < NI - 1:
                        pick(i + 1, u)
                    if tiles and u % 2 == 0:
                        root(t, u // 2)

            act.wait_ge(s_flag, 1)
            general = act.value_load(flag[0:1, 0:1], min_val=0, max_val=1)
            with act.If(general == 0):
                for u in range(NB):
                    pick(0, u)
                iteration(0)
                with act.Fori(1, TL) as i:
                    for u in range(NB):
                        pick(i + 1, u)
                iteration(TL)
                with act.Fori(TL + 1, NI - 1) as i:
                    iteration(i)
                iteration(NI - 1)
                close(IN_LOOP - 1)
                half_a(IN_LOOP)
                root(IN_LOOP, 0)
                for t in range(IN_LOOP, NT):
                    turn(t)
                    if t + 1 < NT:
                        half_a(t + 1)
                    exps(t)
                    if t + 1 < NT:
                        root(t + 1, (t + 1) % 2)
                    close(t, P if t < NT - 1 else LAST)
            with act.Else():
                def pick1(q, k):
                    act.wait_ge(x_go, q + 1)
                    act.copy(idxg[:, 0, 0:1], idx_of(k)).then_inc(x_ix, 1)
                with act.Fori(0, NT) as j:
                    with act.Fori(0, NCH) as k:
                        pick1(2 * NCH * j + k, k)
                    act.wait_ge(x_self, j + 1)
                    act.activation(xw[:, :], xs1[:, :], ACT.Exp).then_inc(x_selfe, 1)
                    with act.Fori(0, NCH) as k:
                        pick1(2 * NCH * j + NCH + k, k)
                        act.wait_ge(x_arg, NCH * j + k + 1)
                        act.activation(xw[:, :], xs1[:, :], ACT.Exp).then_inc(x_exp, 1)

                def tile(t, b, n=P):
                    half_a(t)
                    root(t, b)
                    turn(t)
                    exps(t)
                    close(t, n)
                for t in range(2):
                    tile(t, t)
                with act.Fori(1, NT // 2) as i:
                    for u in range(2):
                        tile(2 * i + u, u)
                tile(NT - 1, 0, LAST)

            for k in range(2):
                act.wait_ge(s_fp, 2 + k)
                act.copy(tokT[:, k, :], bank[4 + k][:, :]).then_inc(s_fa, 1)
            act.wait_ge(s_fp, 5)
            act.copy(qkv[:, 0, :], bank[1][0:G, :]).then_inc(s_fa, 1)
            act.wait_ge(s_f, 4)
            act.activation(at_e[:, :], at_s[:, :], ACT.Exp, scale=float(G) ** -0.5).then_inc(s_fa, 1)
            for k in range(2):
                act.wait_ge(s_fp, 9)
                act.copy(Z[:, 2 * k:2 * k + 2, :], bank[5 + k][:, :].rearrange("p (j n) -> p j n", j=2)).then_inc(s_fa, 1)

            def ffn2(t, b, n=P):
                if not isinstance(t, int) or t >= 2:
                    act.wait_ge(s_y, t - 1)
                act.copy(swb[:, b, :, 0:n], swT[:, :, bass.ds(t * P, n)]).then_inc(s_cp, 1)
            for t in range(2):
                ffn2(t, t)
            with act.Fori(1, NT // 2) as i:
                for u in range(2):
                    ffn2(2 * i + u, u)
            ffn2(NT - 1, 0, LAST)

        @block.tensor
        def _(pe):
            mm_ = nc.tensor.matmul
            pe.wait_ge(s_const, 1)
            pe.wait_ge(s_w2, 16 * 12)
            for k in range(2):
                for j in range(4):
                    last = nc.tensor.transpose(bank[k][:, j * P:(j + 1) * P], Wx[:, k, j * P:(j + 1) * P], ident[:, :])
                last.then_inc(s_wxT, 1)
            pe.wait_ge(s_wxTc, 2)
            for k in range(2):
                for h in range(FH):
                    o = G * (h % 2)
                    j = h // 2
                    last = mm_(bank[2 + k + 2 * (h % 2)][:, j * G:(j + 1) * G], WxT[o:o + G, h // 2, k * P:(k + 1) * P], Ws2[o:o + G, :],
                               start=True, stop=True)
                last.then_inc(s_wl, 1)
            for h in range(FH):
                last = mm_(bank[0][0:1, h * G:(h + 1) * G], bxT[:, h:h + 1], Ws2[0:G, :], start=True, stop=True)
            last.then_inc(s_wl, 1)

            pe.wait_ge(s_ef, 5)
            pe.wait_ge(s_wlc, 3)
            for i in range(4):
                nc.tensor.transpose(bank[0][:, i * ROWS:(i + 1) * ROWS], esf[:, i * P:(i + 1) * P], ident[0:ROWS, 0:ROWS])
                last = nc.tensor.transpose(bank[1][:, i * ROWS:(i + 1) * ROWS], emf[:, i * P:(i + 1) * P], ident[0:ROWS, 0:ROWS])
            last.then_inc(s_eT, 1)
            for i in range(2):
                last = nc.tensor.transpose(bank[2][0:1, i * ROWS:(i + 1) * ROWS], mm[:, i:i + 1], ident[0:ROWS, 0:ROWS])
            last.then_inc(s_eT, 1)
            pe.wait_ge(s_gm, 1)
            pe.wait_ge(s_const, 4)
            mm_(bank[3][:, 0:NG], ones[0:1, :], gmf[:, :], start=True, stop=True).then_inc(s_gmT, 1)

            def proj(t, b):
                pe.wait_ge(s_xn, t + 1)
                if not isinstance(t, int) or t >= 2:
                    pe.wait_ge(s_xTc, t - 1)
                for k in range(2):
                    last = nc.tensor.transpose(pT[:, b * D + k * P:b * D + (k + 1) * P], xn[:, b, k * P:(k + 1) * P], ident[:, :])
                last.then_inc(s_xnT, 1)
                pe.wait_ge(s_xTc, t + 1)
                if not isinstance(t, int) or t >= 2:
                    pe.wait_ge(s_xpc, t - 1)
                for k in range(2):
                    last = mm_(bank[5 + b][:, 0:AW], xT[:, b, k * P:(k + 1) * P], Wg[:, k, :], start=(k == 0), stop=(k == 1))
                last.then_inc(s_xp, 1)
            for t in range(2):
                proj(t, t)
            with pe.Fori(1, NT // 2) as i:
                for u in range(2):
                    proj(2 * i + u, u)
            proj(NT - 1, 0)

            pe.wait_ge(s_r8, 1)
            nc.tensor.transpose(bank[0][0:2 * H, 0:P], r8[:, :], ident[:, :]).then_inc(s_r8T, 1)
            pe.wait_ge(s_dg, 1)
            mm_(bank[1][:, 0:2 * H], ones[0:2 * H, :], dg8[:, :], start=True, stop=True).then_inc(s_G, 1)

            def lookup(i, u):
                g, b = NB * i + u, u % 2
                pe.wait_ge(s_ot, g + 1)
                pe.wait_ge(s_ts, g + 1)
                if not (isinstance(i, int) and g == 0):
                    pe.wait_ge(s_ab, g)
                for c in range(CPG):
                    last = mm_(LOOK[:, c * 24:(c + 1) * 24], ot[:, b, c * P:(c + 1) * P], tsl[:, b, :], start=True, stop=True)
                last.then_inc(s_lk, 1)

            def sums(i, u):
                g, b = NB * i + u, u % 2
                pe.wait_ge(s_oh, g + 1)
                pe.wait_ge(s_sc, g + 1)
                if not (isinstance(i, int) and g == 0):
                    pe.wait_ge(s_mg, g)
                for c in range(CPG):
                    last = mm_(SUMS[:, 0:D + H], oh[:, b, c, :], gt[:, u, c, 0:D + H], start=(c == 0), stop=(c == CPG - 1))
                last.then_inc(s_mm, 1)

            def half_b(t, b):
                pe.wait_ge(s_n2, t + 1)
                if not (isinstance(t, int) and t == 0):
                    pe.wait_ge(s_swc, t)
                for k in range(2):
                    last = nc.tensor.transpose(TR[:, k * P:(k + 1) * P], xn[:, b, k * P:(k + 1) * P], ident[:, :])
                last.then_inc(s_n2T, 1)
                mm_(LOGIT[:, :], onesb[:, :], blb[:, :], start=True, stop=False)
                pe.wait_ge(s_n2c, t + 1)
                for k in range(2):
                    last = mm_(LOGIT[:, :], xTf[:, k * P:(k + 1) * P], Wl[:, k, :], start=False, stop=(k == 1))
                last.then_inc(s_lg, 1)

            def close(t, b, n=P):
                pe.wait_ge(s_sw, t + 1)
                for j in range(4):
                    last = nc.tensor.transpose(TR[:, j * P:(j + 1) * P], sw[:, j * P:(j + 1) * P], ident[:, :])
                last.then_inc(s_swT, 1)
                for j in range(4):
                    last = mm_(TOK[j], sw[0:n, j * P:(j + 1) * P], xn[0:n, b, :], start=(isinstance(t, int) and t == 0 and j % 2 == 0),
                               stop=(isinstance(t, int) and t == NT - 1), skip_group_check=True)
                last.then_inc(s_tok, 1)

            def iteration(i):
                tiles = not isinstance(i, int) or i >= TL
                for u in range(NB):
                    if not (isinstance(i, int) and i == NI - 1 and u == NB - 1):
                        lookup(i + (u + 1) // NB, (u + 1) % NB)
                    t = TPI * (i - TL) + u // 2 if tiles else None
                    if tiles and u % 2 == 0 and not (isinstance(i, int) and t == 0):
                        close(t - 1, (u // 2 + 1) % 2)
                    if tiles and u % 2 == 1:
                        half_b(t, u // 2)
                    sums(i, u)

            pe.wait_ge(s_flag, 1)
            general = pe.value_load(flag[0:1, 0:1], min_val=0, max_val=1)
            with pe.If(general == 0):
                lookup(0, 0)
                iteration(0)
                with pe.Fori(1, TL) as i:
                    for u in range(NB):
                        lookup(i + (u + 1) // NB, (u + 1) % NB)
                        sums(i, u)
                iteration(TL)
                with pe.Fori(TL + 1, NI - 1) as i:
                    iteration(i)
                iteration(NI - 1)
                close(IN_LOOP - 1, (IN_LOOP - 1) % 2)
                for t in range(IN_LOOP, NT):
                    half_b(t, t % 2)
                    close(t, t % 2, P if t < NT - 1 else LAST)
            with pe.Else():
                with pe.Fori(0, NT) as j:
                    with pe.Fori(0, NCH) as k:
                        pe.wait_ge(x_diag, NCH * j + k + 1)
                        mm_(bank[0][:, 0:H * P], ones[:, :], xdiag, start=True, stop=True).then_inc(x_bc, 1)
                    pe.wait_ge(x_self, j + 1)
                    pe.sem_inc(x_turn_p, 1)
                    with pe.Fori(0, NCH) as k:
                        pe.wait_ge(x_hot, NCH * j + k + 1)
                        mm_(bank[1][:, 0:2 * H], xhot, xtbl[:, :], start=True, stop=True)
                        nc.tensor.transpose(bank[2][:, 0:P], xhot, ident[:, :]).then_inc(x_lk, 1)
                        pe.wait_ge(x_rows, NCH * j + k + 1)
                        mm_(bank[3][:, 0:D + H], xhotT, xrow[:, 0:D + H], start=True, stop=True).then_inc(x_sum, 1)

                def tile(t, b, n=P):
                    half_b(t, b)
                    close(t, b, n)
                for t in range(2):
                    tile(t, t)
                with pe.Fori(1, NT // 2) as i:
                    for u in range(2):
                        tile(2 * i + u, u)
                tile(NT - 1, 0, LAST)

            pe.wait_ge(s_f, 1)
            pe.wait_ge(s_swc, NT)
            for j in range(4):
                last = nc.tensor.transpose(bank[7][0:1, j * P:(j + 1) * P], tokn[:, j, D:D + 1], ident[:, :])
            last.then_inc(s_fp, 1)
            for k in range(2):
                for j in range(4):
                    last = nc.tensor.transpose(bank[4 + k][:, j * P:(j + 1) * P], tokn[:, j, k * P:(k + 1) * P], ident[:, :])
                last.then_inc(s_fp, 1)
            pe.wait_ge(s_fa, 2)
            pe.wait_ge(s_f, 2)
            nrow_ = nrow
            stT_ = stT
            for h in range(FH):
                s = slice(h * G, (h + 1) * G)
                for k in range(2):
                    mm_(bank[0][0:G, s], Wf[:, k, s], tokT[:, k, s], start=(k == 0), stop=False)
                last = mm_(bank[0][0:G, s], bf[:, s], nrow_[:, s], start=False, stop=True)
            last.then_inc(s_fp, 1)
            pe.wait_ge(s_f, 3)
            mm_(bank[1][0:G, :], Wq[:, 0, :], stT_, start=True, stop=True).then_inc(s_fp, 1)
            mm_(bank[2][0:G, :], Wq[:, 1, :], stT_, start=True, stop=True)
            for h in range(FH):
                s = slice(h * G, (h + 1) * G)
                last = mm_(bank[3][0:G, s], stT_[:, s], Wq[:, 2, :], start=True, stop=True)
            last.then_inc(s_fp, 1)
            pe.wait_ge(s_fa, 3)
            pe.wait_ge(s_kc, 1)
            for h in range(FH):
                s = slice(h * G, (h + 1) * G)
                last = mm_(bank[0][0:G, s], qkv[:, 0, s], qkv[:, 1, s], start=True, stop=True)
            last.then_inc(s_fp, 1)
            pe.wait_ge(s_f, 5)
            for h in range(FH):
                s = slice(h * G, (h + 1) * G)
                last = nc.tensor.transpose(bank[1][0:G, s], at_s[:, s], ident[0:G, 0:G])
            last.then_inc(s_fp, 1)
            pe.wait_ge(s_f, 6)
            pe.wait_ge(s_kc, 2)
            for h in range(FH):
                s = slice(h * G, (h + 1) * G)
                last = mm_(bank[2][0:G, s], qkv[:, 2, s], at_T[:, s], start=True, stop=True)
            last.then_inc(s_os, 1)
            pe.wait_ge(s_f, 7)
            for h in range(FH):
                o = G * (h % 2)
                j = h // 2
                last = mm_(bank[5 + j // 2][o:o + G, (j % 2) * D:(j % 2 + 1) * D], osT[:, h * G:(h + 1) * G], Wo[:, h, :],
                           start=True, stop=True)
            last.then_inc(s_fp, 1)

            def ffn2(t, b, n=P):
                pe.wait_ge(s_cp, t + 1)
                if not isinstance(t, int) or t >= 2:
                    pe.wait_ge(s_yo, t - 1)
                for j in range(4):
                    last = mm_(bank[b][0:n, 0:D], swb[:, b, j, 0:n], Z[:, j, :], start=(j == 0), stop=(j == 3))
                last.then_inc(s_y, 1)
            pe.wait_ge(s_f, 8)
            for t in range(2):
                ffn2(t, t)
            with pe.Fori(1, NT // 2) as i:
                for u in range(2):
                    ffn2(2 * i + u, u)
            ffn2(NT - 1, 0, LAST)

        @block.vector
        def _(v):
            own = Chain(v, s_dv)
            v.memset(ed[PAD_BASE:ROWS, :], N).then_inc(s_pad, 1)
            v.memset(es[PAD_BASE:ROWS, :], 0).then_inc(s_pad, 1)
            v.wait_ge(s_ed, 32)
            own.add(v.tensor_scalar(emi[:, :], ed[:, :], P - 1, None, ALU.bitwise_and))
            own.add(v.tensor_copy(edf[:, :], ed[:, :]))
            v.wait_ge(s_es, 32)
            v.tensor_copy(esf[:, :], es[:, :]).then_inc(s_ef, 1)
            own.wait()
            v.tensor_copy(emf[:, :], emi[:, :]).then_inc(s_ef, 1)
            v.tensor_copy(emb[:, :], emi[:, :]).then_inc(s_ef, 1)
            v.tensor_reduce(mm[:, 0:1], edf[:, :], X, ALU.min).then_inc(s_ef, 1)
            v.tensor_reduce(mm[:, 1:2], edf[:, :], X, ALU.max).then_inc(s_ef, 1)
            v.wait_ge(s_w, 16 * 5)
            for i in range(2):
                for k in range(2):
                    own.add(v.tensor_tensor(watt[:, k, :], Wg[:, k, 0:D], attb[:, i, :], ALU.mult))
                own.wait()
                own.add(v.tensor_reduce(Wg[:, :, D + i * H:D + (i + 1) * H],
                                        watt[:, :, :].rearrange("p k (h c) -> p k h c", c=C), X, ALU.add))
                own.wait()
            for i in range(XL):
                v.wait_ge(s_x[i], 16)
            with v.Fori(0, NT) as t:
                v.bn_stats(st[:, bass.ds(t, 1), :], xs[:, bass.ds(t, 1), :]).then_inc(s_bn, 1)
            v.wait_ge(s_bn, NT)
            own.add(v.tensor_tensor(mv[:, :, 0], st[:, :, 1], st[:, :, 4], ALU.subtract))
            own.add(v.tensor_tensor(mv[:, :, 1], st[:, :, 2], st[:, :, 5], ALU.add))
            own.wait()
            own.add(v.tensor_tensor(mv[:, :, 0], mv[:, :, 0], mv[:, :, 0], ALU.mult))
            own.add(v.tensor_scalar(mv[:, :, 1], mv[:, :, 1], 1.0 / D, EPS, ALU.mult, ALU.add))
            own.wait()
            v.scalar_tensor_tensor(mv[:, :, 1], mv[:, :, 0], 0.25, mv[:, :, 1], ALU.mult, ALU.add).then_inc(s_var, 1)
            own.wait()
            v.wait_ge(s_var, 1)
            own.add(v.tensor_tensor(mv[:, :, 0], st[:, :, 1], st[:, :, 4], ALU.add))
            own.wait()
            own.add(v.tensor_scalar(mv[:, :, 0], mv[:, :, 0], 0.5, None, ALU.mult))
            v.wait_ge(s_w2, 16 * 12)
            own.add(v.tensor_scalar(tmp8[:, :], tmp8[:, :], 0.1, 5.0, ALU.max, ALU.min))
            own.wait()
            own.add(v.reciprocal(itemp[:, :], tmp8[:, :]))
            own.wait()
            v.wait_ge(s_wl, 2)
            it2 = itemp[:, :].rearrange("p (j o) -> p o j", o=2)
            for k in range(2):
                for o in range(2):
                    last = v.tensor_tensor(Wl[:, k, :].rearrange("p (j o g) -> p o j g", o=2, g=G)[:, o],
                                           bank[2 + k + 2 * o][:, 0:HG // 2].rearrange("p (j g) -> p j g", g=G),
                                           it2[:, o].unsqueeze(2).broadcast_to((P, FH // 2, G)), ALU.mult)
                last.then_inc(s_wlc, 1)
            v.wait_ge(s_wl, 3)
            own.add(v.tensor_tensor(by_head(bl[:, :]), by_head(bank[0][0:1, :]), bsl[:, :].unsqueeze(1).broadcast_to((1, FH, G)), ALU.add))
            own.wait()
            own.add(v.tensor_tensor(by_head(bl[:, :]), by_head(bl[:, :]), over_slices(itemp[0:1, :]), ALU.mult))
            own.wait()
            v.wait_ge(s_const, 8)
            for i in range(3):
                r = 32 * i
                own.add(v.tensor_copy(blb[r:r + 1, :], bl[:, :]))
                own.wait()
                if i < 2:
                    own.add(v.tensor_copy(blr[:, :], blb[r:r + 1, :]))
                    own.wait()
                    own.add(v.tensor_tensor(bl[:, :], bl[:, :], blr[:, :], ALU.subtract))
                    own.wait()
            v.tensor_copy(thr[:, :], thr_i[:, :]).then_inc(s_wlc, 1)
            v.wait_ge(s_eT, 1)
            v.tensor_copy(idx[:, :].rearrange("p (q i) -> p q i", i=4), bank[0][:, 0:4 * ROWS].rearrange("p (i q) -> p q i", i=4)).then_inc(s_idx, 1)
            own.add(v.tensor_copy(slot[:, :].rearrange("p (q i) -> p q i", i=4), bank[1][:, 0:4 * ROWS].rearrange("p (i q) -> p q i", i=4)))
            v.wait_ge(s_eT, 2)
            own.add(v.tensor_reduce(gmm[:, 0, :], bank[2][0:1, 0:ROWS].rearrange("p (g r) -> p g r", r=RPG), X, ALU.min))
            own.add(v.tensor_reduce(gmm[:, 1, :], bank[2][0:1, ROWS:2 * ROWS].rearrange("p (g r) -> p g r", r=RPG), X, ALU.max))
            own.wait()
            own.add(v.tensor_copy(gi[:, :], gmm[:, 0, :]))
            own.add(v.tensor_tensor(gmf[:, :], thr[:, 1:NG + 1], gmm[:, 0, :], ALU.subtract))
            own.add(v.tensor_tensor(gmm[:, 1, :], gmm[:, 1, :], gmm[:, 0, :], ALU.subtract))
            own.wait()
            own.add(v.tensor_reduce(flagf[:, 0:1], gmm[:, 1, :], X, ALU.max))
            own.add(v.tensor_reduce(flagf[:, 3:4], gmf[:, :], X, ALU.max))
            own.add(v.tensor_scalar(gblk[:, :], gi[:, :], 7, None, ALU.arith_shift_right))
            own.add(v.tensor_scalar(gmi[:, :], gi[:, :], P - 1, None, ALU.bitwise_and))
            own.wait()
            v.tensor_copy(gmf[:, :], gmi[:, :]).then_inc(s_gm, 1)
            v.wait_ge(s_gmT, 1)
            v.wait_ge(s_const, 8)
            own.add(v.tensor_scalar(mhi[:, :], bank[3][:, 0:NG], lane[:, :], None, ALU.is_le))
            own.add(v.tensor_scalar(mlo[:, :], bank[3][:, 0:NG], lane[:, :], None, ALU.is_gt))

            v.wait_ge(s_sd, 1)
            own.add(v.reciprocal(rstd[:, :], rstd[:, :]))
            own.wait()

            def norm(t, b):
                if not isinstance(t, int) or t >= 2:
                    v.wait_ge(s_xnT, t - 1)
                v.tensor_scalar(xn[:, b, 0:D], flat(xs[:, bass.ds(t, 1), :]), mv[:, bass.ds(t, 1), 0], rstd[:, bass.ds(t, 1)],
                                ALU.subtract, ALU.mult).then_inc(s_xn, 1)

            def take(t, b):
                v.wait_ge(s_xp, t + 1)
                v.tensor_copy(flat(acc[:, bass.ds(t, 1), :]), bank[5 + b][:, 0:AW]).then_inc(s_xpc, 1)
            norm(0, 0)
            norm(1, 1)
            take(0, 0)
            norm(2, 0)
            with v.Fori(0, (NT - 3) // 2) as i:
                for u in range(2):
                    t0 = 2 * i + 1
                    take(t0 + u, (u + 1) % 2)
                    norm(t0 + u + 2, (u + 1) % 2)
            take(NT - 2, 1)
            take(NT - 1, 0)
            v.wait_ge(s_xpc, NT)
            a_src = acc[:, 0:NT, D:D + H]
            a_dst = acc[:, 0:NT, D + H:D + 2 * H]
            v.tensor_copy(ee[:, :, 2 * H:3 * H], a_src).then_inc(s_ea, 1)
            own.add(v.tensor_reduce(r8[:, 0:H], a_src.rearrange("p t h -> p h t"), X, ALU.max))
            own.add(v.tensor_reduce(r8[:, H:2 * H], a_src.rearrange("p t h -> p h t"), X, ALU.min))
            own.wait()
            v.tensor_scalar(r8[:, H:2 * H], r8[:, H:2 * H], -1.0, None, ALU.mult).then_inc(s_r8, 1)
            v.wait_ge(s_r8T, 1)
            own.add(v.tensor_reduce(g8[:, :], bank[0][0:2 * H, 0:P], X, ALU.max))
            own.wait()
            v.tensor_scalar(dg8[:, :], ident[0:2 * H, 0:2 * H], g8[:, :], None, ALU.mult).then_inc(s_dg, 1)
            v.wait_ge(s_G, 1)
            own.add(v.tensor_copy(Gb[:, :], bank[1][:, 0:2 * H]))
            own.wait()
            Gx = Gb[:, 0:H].unsqueeze(1).broadcast_to((P, NT, H))
            v.tensor_tensor(ee[:, :, 0:H], a_src, Gx, ALU.subtract).then_inc(s_ea, 1)
            own.add(v.tensor_tensor(uv[:, :, 0:H], a_dst, Gx, ALU.add))
            own.add(v.tensor_tensor(spr[:, :], Gb[0:1, 0:H], Gb[0:1, H:2 * H], ALU.add))
            own.wait()
            own.add(v.tensor_scalar(uv[:, :, H:2 * H], uv[:, :, 0:H], 0.2, None, ALU.mult))
            own.add(v.tensor_reduce(flagf[:, 1:2], spr[:, :], X, ALU.max))
            own.wait()
            own.add(v.tensor_tensor(uu[:, :, :], uv[:, :, 0:H], uv[:, :, H:2 * H], ALU.max))
            own.add(v.tensor_scalar(flagf[:, 0:1], flagf[:, 0:1], P - 0.5, None, ALU.is_gt))
            own.add(v.tensor_scalar(flagf[:, 1:2], flagf[:, 1:2], SPREAD, None, ALU.is_gt))
            own.add(v.tensor_scalar(flagf[:, 3:4], flagf[:, 3:4], 0.0, None, ALU.is_gt))
            own.wait()
            own.add(v.tensor_tensor(uv[:, :, 0:H], uv[:, :, 0:H], uu[:, :, :], ALU.subtract))
            v.tensor_tensor(uv[:, :, H:2 * H], uv[:, :, H:2 * H], uu[:, :, :], ALU.subtract).then_inc(s_ea, 1)
            own.add(v.tensor_tensor(flagf[:, 2:3], flagf[:, 0:1], flagf[:, 1:2], ALU.max))
            own.wait()
            own.add(v.tensor_tensor(flagf[:, 2:3], flagf[:, 2:3], flagf[:, 3:4], ALU.max))
            own.wait()
            v.tensor_copy(flag[:, :], flagf[:, 2:3]).then_inc(s_flag, 1)

            def a1(t):
                v.reciprocal(rden[:, :], flat(acc[:, bass.ds(t, 1), D:D + H])).then_inc(s_rd, 1)

            def a2(t):
                v.wait_ge(s_zz, t + 1)
                v.tensor_tensor(z[:, :], ELU[:, 0:D], gb[:, :], ALU.add).then_inc(s_z, 1)

            def a3(t, b):
                o = Own(v, s_ownA, t * 4)
                xt = flat(xs[:, bass.ds(t, 1), :])
                v.wait_ge(s_e, t + 1)
                o.add(v.scalar_tensor_tensor(ELU[:, 0:D], z[:, :], 0.0, ELU[:, 0:D], ALU.max, ALU.add))
                o.wait()
                o.add(v.scalar_tensor_tensor(xt, ELU[:, 0:D], -1.0, xt, ALU.add, ALU.add))
                o.wait()
                v.sem_inc(s_turn_v, 1)
                o.add(v.bn_stats(stf[:, :], xt))
                o.wait()
                v.sem_inc(s_turn_v, 1)
                o.add(v.bn_aggr(mvf[:, b, :], stf[:, :]))
                o.wait()
                v.tensor_scalar(mvf[:, b, 1:2], mvf[:, b, 1:2], EPS, None, ALU.add).then_inc(s_var2, 1)
                assert o.k == 4

            def b1(t, b):
                o = Own(v, s_ownB, t * 2)
                v.wait_ge(s_sd2, t + 1)
                o.add(v.reciprocal(sdf[:, b, :], sdf[:, b, :]))
                o.wait()
                if not isinstance(t, int) or t >= 2:
                    v.wait_ge(s_tok, t - 1)
                v.tensor_scalar(xn[:, b, :], flat(xs[:, bass.ds(t, 1), :]), mvf[:, b, 0:1], sdf[:, b, :],
                                ALU.subtract, ALU.mult).then_inc(s_n2, 1)

            def b2(t):
                v.wait_ge(s_lg, t + 1)
                v.tensor_reduce(mx[:, :], by_head(LOGIT[:, :]), X, ALU.max, negate=True).then_inc(s_nm, 1)

            def b3(t):
                o = Own(v, s_ownB, t * 2 + 1)
                v.wait_ge(s_exl, t + 1)
                o.add(v.reciprocal(sm[:, :], sm[:, :]))
                o.wait()
                if not (isinstance(t, int) and t == 0):
                    v.wait_ge(s_tok, t)
                v.tensor_tensor(by_head(sw[:, :]), by_head(LOGIT[:, :]), over_slices(sm[:, :]), ALU.mult).then_inc(s_sw, 1)

            def quick():
                mine = Chain(v, s_quick)
                v.wait_ge(s_ex, 3)
                mine.add(v.tensor_copy(ab3[:, 0:NT, :, 0], ab[:, :, :]))
                mine.add(v.tensor_tensor(uv[:, :, :], ab[:, :, :], ee[:, :, 0:2 * H], ALU.mult))
                mine.wait()
                mine.add(v.tensor_tensor(abr[:, :, :], ab[:, :, :], ab3[:, 0:NT, :, 0], ALU.subtract))
                wself = bank[7][:, 0:NT * H].rearrange("p (t h) -> p t h", h=H)
                mine.add(v.tensor_tensor(wself, uv[:, :, 0:H], uv[:, :, H:2 * H], ALU.max))
                mine.add(v.tensor_tensor(a_src, uv[:, :, 0:H], uv[:, :, H:2 * H], ALU.max))
                mine.wait()
                mine.add(v.tensor_copy(ab3[:, 0:NT, :, 1], abr[:, :, :]))
                mine.wait()
                mine.add(v.tensor_tensor(abr[:, :, :], abr[:, :, :], ab3[:, 0:NT, :, 1], ALU.subtract))
                mine.wait()
                mine.add(v.tensor_copy(ab3[:, 0:NT, :, 2], abr[:, :, :]))
                v.wait_ge(s_tab, 16 * NT)
                xp4 = acc[:, 0:NT, 0:D].rearrange("p t (h c) -> p t h c", c=C)
                for t in range(NT):
                    mine.add(v.tensor_tensor(xp4[:, t], xp4[:, t], wself[:, t].unsqueeze(2).broadcast_to((P, H, C)), ALU.mult))
                mine.wait()

                def hot(i, u):
                    g, b = NB * i + u, u % 2
                    first = isinstance(i, int) and g < 2
                    blk = v.value_load(gblk[0:1, bass.ds(g, 1)], min_val=0, max_val=NT - 1)
                    v.wait_ge(s_db[b], 16 * (NB // 2 * i + u // 2 + 1))
                    if not first:
                        v.wait_ge(s_lk, g - 1)
                    v.tensor_scalar(tsa[:, b, :], abs3(blk), mhi[:, bass.ds(g, 1)], None, ALU.mult).then_inc(s_ta, 1)
                    v.tensor_scalar(ot[:, b, :], db[:, b, :], lane[:, :], None, ALU.is_equal).then_inc(s_ot, 1)
                    v.wait_ge(s_ta, g + 1)
                    v.scalar_tensor_tensor(tsl[:, b, :], abs3(blk + 1), mlo[:, bass.ds(g, 1)], tsa[:, b, :],
                                           ALU.mult, ALU.add).then_inc(s_ts, 1)

                def hot2(i, u):
                    g, b = NB * i + u, u % 2
                    if not (isinstance(i, int) and g < 2):
                        v.wait_ge(s_mm, g - 1)
                    for c in range(CPG):
                        last = v.tensor_scalar(oh[:, b, c, :], cols[:, :], slot[:, bass.ds(g * CPG + c, 1)], None, ALU.is_equal)
                    last.then_inc(s_oh, 1)

                def weigh(i, u):
                    g, b = NB * i + u, u % 2
                    v.wait_ge(s_lk, g + 1)
                    v.tensor_reduce(abe[:, b, :, :], LOOK[:, 0:CPG * 24].rearrange("p (c e k) -> p c e k", c=CPG, k=3), X, ALU.add).then_inc(s_ab, 1)
                    v.wait_ge(s_gat[u], 16 * CPG * (i + 1))
                    v.wait_ge(s_ab, g + 1)
                    v.tensor_tensor(we[:, b, :, :], abe[:, b, :, :], gt[:, u, :, D:D + 2 * H], ALU.mult).then_inc(s_we, 1)
                    v.wait_ge(s_we, g + 1)
                    wp = WP[:, b * 32:b * 32 + CPG * H].rearrange("p (c h) -> p c h", h=H)
                    v.tensor_tensor(wp, we[:, b, :, 0:H], we[:, b, :, H:2 * H], ALU.max).then_inc(s_wp, 1)
                    v.tensor_tensor(gt[:, u, :, D:D + H], we[:, b, :, 0:H], we[:, b, :, H:2 * H], ALU.max)
                    v.wait_ge(s_wp, g + 1)
                    for c in range(CPG):
                        r = gt[:, u, c, 0:D].rearrange("p (h k) -> p h k", k=C)
                        last = v.tensor_tensor(r, r, wp[:, c, :].unsqueeze(2).broadcast_to((P, H, C)), ALU.mult)
                    last.then_inc(s_sc, 1)

                def merge(i, u):
                    g, b = NB * i + u, u % 2
                    blk = v.value_load(gblk[0:1, bass.ds(g, 1)], min_val=0, max_val=NT - 1)
                    v.wait_ge(s_mm, g + 1)
                    if not (isinstance(i, int) and g == 0):
                        v.wait_ge(s_mg, g)
                    for m, k in ((mhi, 0), (mlo, 1)):
                        a = flat(acc[:, bass.ds(blk + k, 1), 0:D + H])
                        last = v.scalar_tensor_tensor(a, SUMS[:, 0:D + H], m[:, bass.ds(g, 1)], a, ALU.mult, ALU.add)
                    last.then_inc(s_mg, 1)

                def iteration(i, tiles):
                    for u in range(NB):
                        more = not (isinstance(i, int) and i == NI - 1 and u == NB - 1)
                        t = TPI * (i - TL) + u // 2 if tiles else None
                        b = u // 2
                        if tiles:
                            a1(t) if u % 2 == 0 else b1(t, b)
                        if more:
                            hot(i + (u + 1) // NB, (u + 1) % NB)
                        weigh(i, u)
                        if tiles:
                            a2(t) if u % 2 == 0 else b2(t)
                        if u > 0 or not (isinstance(i, int) and i == 0):
                            merge(i - (u == 0), (u - 1) % NB)
                        if more:
                            hot2(i + (u + 1) // NB, (u + 1) % NB)
                        if tiles:
                            a3(t, b) if u % 2 == 0 else b3(t)
                hot(0, 0)
                hot2(0, 0)
                iteration(0, False)
                with v.Fori(1, TL) as i:
                    iteration(i, False)
                iteration(TL, True)
                with v.Fori(TL + 1, NI - 1) as i:
                    iteration(i, True)
                iteration(NI - 1, True)
                merge(NI - 1, NB - 1)
                v.wait_ge(s_mg, NG)
                a1(IN_LOOP)
                a2(IN_LOOP)
                a3(IN_LOOP, 0)
                for t in range(IN_LOOP, NT):
                    b1(t, t % 2)
                    if t + 1 < NT:
                        a1(t + 1)
                        a2(t + 1)
                    b2(t)
                    if t + 1 < NT:
                        a3(t + 1, (t + 1) % 2)
                    b3(t)

            def general_path():
                K1, K2, KB = 4, 9, 11
                PB = (K1 + K2) * NCH + KB
                xown = Own(v, x_own, 0)

                def at(base, n):
                    xown.base, xown.k = base, 0

                v.wait_ge(s_tab, 16 * NT)
                v.tensor_copy(xnode[:, :], lane[:, :]).then_inc(x_own, 1)
                v.sem_inc(x_go, 1)

                def arrive(q):
                    v.wait_ge(x_gat, 16 * (q + 1))
                    v.wait_ge(x_db, 16 * (q + 1))
                    return v.tensor_scalar(xhot, xdst, xnode[:, :], None, ALU.is_equal)

                def leaky(a):
                    xown.add(v.tensor_scalar(xs2[:, :], a, 0.2, None, ALU.mult))
                    xown.wait()
                    xown.add(v.tensor_tensor(a, a, xs2[:, :], ALU.max))
                    xown.wait()

                with v.Fori(0, NT) as j:
                    a_s = flat(ee[:, bass.ds(j, 1), 2 * H:3 * H])
                    acc_j = flat(acc[:, bass.ds(j, 1), :])
                    B0 = j * PB + 1
                    at(B0, 2)
                    xown.wait()
                    xown.add(v.tensor_copy(xmax[:, :], a_s))
                    xown.add(v.tensor_copy(xtbl[:, 0:H], acc_j[:, D + H:D + 2 * H]))
                    xown.wait()
                    v.sem_inc(x_turn_v, 1)
                    with v.Fori(0, NCH) as k:
                        q = 2 * NCH * j + k
                        at(B0 + 2 + K1 * k, K1)
                        v.wait_ge(x_go, q + 1)
                        xown.add(arrive(q))
                        for h in range(H):
                            last = v.tensor_scalar(xdiag[:, h, :], ident[:, :], xrow[:, D + 2 * H + h:D + 2 * H + h + 1], None, ALU.mult)
                        last.then_inc(x_diag, 1)
                        xown.wait()
                        xown.add(v.tensor_scalar(xpen, xhot, -1.0, BIG, ALU.add, ALU.mult))
                        xown.wait()
                        v.wait_ge(x_bc, NCH * j + k + 1)
                        xown.add(v.tensor_tensor(xtmp, bank[0][:, 0:H * P].rearrange("p (h e) -> p h e", h=H),
                                                 xpen.unsqueeze(1).broadcast_to((P, H, P)), ALU.add))
                        xown.wait()
                        xown.add(v.tensor_reduce(xred[:, :], xtmp, X, ALU.max))
                        xown.wait()
                        v.tensor_tensor(xmax[:, :], xmax[:, :], xred[:, :], ALU.max).then_inc(x_go, 1)
                        assert xown.k == K1
                    v.wait_ge(x_go, 2 * NCH * j + NCH + 1)
                    at(B0 + 2 + K1 * NCH, KB - 2)
                    xown.add(v.tensor_tensor(xtbl[:, H:2 * H], xmax[:, :], xtbl[:, 0:H], ALU.add))
                    xown.add(v.tensor_tensor(xs1[:, :], a_s, xtbl[:, 0:H], ALU.add))
                    xown.wait()
                    leaky(xtbl[:, H:2 * H])
                    leaky(xs1[:, :])
                    v.tensor_tensor(xs1[:, :], xs1[:, :], xtbl[:, H:2 * H], ALU.subtract).then_inc(x_self, 1)
                    v.wait_ge(x_selfe, j + 1)
                    for h in range(H):
                        last = v.tensor_scalar(acc_j[:, h * C:(h + 1) * C], acc_j[:, h * C:(h + 1) * C], xw[:, h:h + 1], None, ALU.mult)
                    xown.add(last)
                    xown.add(v.tensor_copy(acc_j[:, D:D + H], xw[:, :]))
                    xown.wait()
                    v.sem_inc(x_turn_v, 1)
                    with v.Fori(0, NCH) as k:
                        q = 2 * NCH * j + NCH + k
                        at(B0 + 2 + K1 * NCH + 8 + K2 * k, K2)
                        v.wait_ge(x_go, q + 1)
                        arrive(q).then_inc(x_hot, 1)
                        v.wait_ge(x_lk, NCH * j + k + 1)
                        xown.add(v.tensor_copy(xhotT, bank[2][:, 0:P]))
                        xown.add(v.tensor_tensor(xs1[:, :], xrow[:, D + 2 * H:D + 3 * H], bank[1][:, 0:H], ALU.add))
                        xown.wait()
                        leaky(xs1[:, :])
                        xown.add(v.tensor_tensor(xs1[:, :], xs1[:, :], bank[1][:, H:2 * H], ALU.subtract))
                        xown.wait()
                        v.tensor_scalar(xs1[:, :], xs1[:, :], 0.0, None, ALU.min).then_inc(x_arg, 1)
                        v.wait_ge(x_exp, NCH * j + k + 1)
                        for h in range(H):
                            xown.add(v.tensor_scalar(xrow[:, h * C:(h + 1) * C], xrow[:, h * C:(h + 1) * C], xw[:, h:h + 1], None, ALU.mult))
                        v.tensor_copy(xrow[:, D:D + H], xw[:, :]).then_inc(x_rows, 1)
                        v.wait_ge(x_sum, NCH * j + k + 1)
                        v.tensor_tensor(acc_j[:, 0:D + H], acc_j[:, 0:D + H], bank[3][:, 0:D + H], ALU.add).then_inc(x_go, 1)
                        assert xown.k == K2
                    v.wait_ge(x_go, 2 * NCH * (j + 1) + 1)
                    at(B0 + 2 + K1 * NCH + 8 + K2 * NCH, 1)
                    xown.add(v.tensor_scalar(xnode[:, :], xnode[:, :], float(P), None, ALU.add))

            v.wait_ge(s_flag, 1)
            general = v.value_load(flag[0:1, 0:1], min_val=0, max_val=1)
            with v.If(general == 0):
                quick()
            with v.Else():
                general_path()

                def tile(t, b):
                    a1(t)
                    a2(t)
                    a3(t, b)
                    b1(t, b)
                    b2(t)
                    b3(t)
                for t in range(2):
                    tile(t, t)
                with v.Fori(1, NT // 2) as i:
                    for u in range(2):
                        tile(2 * i + u, u)
                tile(NT - 1, 0)

            v.wait_ge(s_tok, NT)
            v.wait_ge(s_swc, NT)
            own.add(v.tensor_reduce(nrm[:, 0, :], nrt[:, :, :].rearrange("p t j -> p j t"), X, ALU.add))
            own.wait()
            own.add(v.tensor_scalar(nrm[:, 1, :], nrm[:, 0, :], 1e-5, None, ALU.add))
            own.wait()
            own.add(v.reciprocal(nrm[:, 1, :], nrm[:, 1, :]))
            own.wait()
            for j in range(4):
                v.tensor_scalar(tokn[:, j, 0:D], TOK[j], nrm[:, 1, j:j + 1], None, ALU.mult)
            last = v.tensor_tensor(tokn[:, :, D], nrm[:, 0, :], nrm[:, 1, :], ALU.mult)
            last.then_inc(s_f, 1)
            v.wait_ge(s_fp, 1)
            v.tensor_copy(nrow, bank[7][0:1, :]).then_inc(s_f, 1)
            v.wait_ge(s_fp, 4)
            v.tensor_copy(stT, bank[0][0:G, :]).then_inc(s_f, 1)
            v.wait_ge(s_fp, 6)
            v.tensor_copy(qkv[:, 1, :], bank[2][0:G, :]).then_inc(s_kc, 1)
            v.tensor_copy(qkv[:, 2, :], bank[3][0:G, :]).then_inc(s_kc, 1)
            v.wait_ge(s_fp, 7)
            own.add(v.tensor_reduce(amx[:, 0, :], by_head(bank[0][0:G, :]), X, ALU.max))
            own.wait()
            v.tensor_tensor(by_head(at_s[:, :]), by_head(bank[0][0:G, :]), over_slices(amx[:, 0, :]), ALU.subtract).then_inc(s_f, 1)
            v.wait_ge(s_fa, 4)
            own.add(v.tensor_reduce(amx[:, 0, :], by_head(at_e[:, :]), X, ALU.add))
            own.wait()
            own.add(v.reciprocal(amx[:, 1, :], amx[:, 0, :]))
            own.wait()
            v.tensor_tensor(by_head(at_s[:, :]), by_head(at_e[:, :]), over_slices(amx[:, 1, :]), ALU.mult).then_inc(s_f, 1)
            v.wait_ge(s_fp, 8)
            v.tensor_copy(at_T[:, :], bank[1][0:G, :]).then_inc(s_f, 1)
            v.wait_ge(s_os, 1)
            v.tensor_copy(osT[:, :], bank[2][0:G, :]).then_inc(s_f, 1)

            v.wait_ge(s_fa, 6)
            v.tensor_tensor(Z[0:G, 0, :], Z[0:G, 0, :], bo[0:G, :], ALU.add).then_inc(s_f, 1)

            def ffn2(t, b, n=P):
                v.wait_ge(s_y, t + 1)
                if not isinstance(t, int) or t >= 2:
                    v.wait_ge(s_st[b], 16 * half(t))
                v.tensor_tensor(y[0:n, b, :], bank[b][0:n, 0:D], flat(xs[0:n, bass.ds(t, 1), :]), ALU.add).then_inc(s_yo, 1)

            def half(t):
                return t // 2 if isinstance(t, int) else t
            for t in range(2):
                ffn2(t, t)
            with v.Fori(1, NT // 2) as i:
                for u in range(2):
                    t = 2 * i + u
                    v.wait_ge(s_y, t + 1)
                    v.wait_ge(s_st[u], 16 * i)
                    v.tensor_tensor(y[:, u, :], bank[u][:, 0:D], flat(xs[:, bass.ds(t, 1), :]), ALU.add).then_inc(s_yo, 1)
            ffn2(NT - 1, 0, LAST)


_INS = ['x', 'src', 'dst', 'L0_gnn_W', 'L0_gnn_att_src', 'L0_gnn_att_dst', 'L0_gnn_bias', 'L0_ffn_W_fx', 'L0_ffn_b_fx',
        'L0_ffn_W_x', 'L0_ffn_b_x', 'L0_ffn_W_slice', 'L0_ffn_b_slice', 'L0_ffn_W_q', 'L0_ffn_W_k', 'L0_ffn_W_v',
        'L0_ffn_W_out', 'L0_ffn_b_out', 'L0_ffn_temperature']


def kernel(**inputs):
    import numpy as _np
    import concourse.bacc as _bacc
    from concourse import mybir as _mybir
    from concourse.bass_utils import run_bass_kernel_spmd as _run

    nc = _bacc.Bacc("TRN2", target_bir_lowering=False, num_devices=1)
    arrays, args = {}, []
    for name in _INS:
        a = _np.ascontiguousarray(inputs[name])
        arrays[f"in_{name}_dram"] = a
        args.append(nc.dram_tensor(f"in_{name}_dram", a.shape, _mybir.dt.from_np(a.dtype), kind="ExternalInput").ap())
    x = inputs['x']
    args.append(nc.dram_tensor("out_0_dram", tuple(x.shape), _mybir.dt.float32, kind="ExternalOutput").ap())
    build(nc, *args)
    r = _run(nc, [arrays], core_ids=[0])
    return r.results[0]["out_0_dram"]
```

```python
from contextlib import ExitStack

import concourse.bass as bass
from concourse import mybir

F32 = mybir.dt.float32
BF16 = mybir.dt.bfloat16
I32 = mybir.dt.int32
ALU = mybir.AluOpType
ACT = mybir.ActivationFunctionType
X = mybir.AxisListType.X
XY = mybir.AxisListType.XY

P = 128
ROW = 512
CPG = 8
GE = CPG * P
SPREAD = 60.0
EPS = 1e-5


class Own:

    def __init__(self, eng, sem, base):
        self.eng, self.sem, self.base, self.k = eng, sem, base, 0

    def add(self, ins):
        ins.then_inc(self.sem, 1)
        self.k += 1

    def wait(self):
        self.eng.wait_ge(self.sem, self.base + self.k)


class Chain:

    def __init__(self, eng, sem):
        self.eng, self.sem, self.base, self.k = eng, sem, 0, 0

    def add(self, ins):
        ins.then_inc(self.sem, 1)
        self.k += 1
        return ins

    def wait(self):
        self.eng.wait_ge(self.sem, self.base + self.k)


def build(nc, x, src, dst, W, att_src, att_dst, gbias, W_fx, b_fx, W_x, b_x, W_slice, b_slice,
          W_q, W_k, W_v, W_out, b_out, temperature, out):
    N, D = x.shape
    E = src.shape[0]
    H, C = att_src.shape
    FH = temperature.shape[1]
    G = W_slice.shape[1]
    HG = FH * G
    NT = -(-N // P)
    LAST = N - (NT - 1) * P
    NG = -(-E // GE)
    NG += NG % 2
    ROWS = NG * GE // ROW
    FULL = E // ROW
    REST = E - FULL * ROW
    TW = D + H
    AW = D + 2 * H
    RPG = GE // ROW
    NB = 4
    PAD_BASE = (ROWS // 32) * 32 if ROWS % 32 else ROWS - 32
    assert D == 256 and H * C == D and HG == 512 and G == 64 and NT % 2 == 1 and NG % NB == 0 and ROWS <= P
    assert FULL >= PAD_BASE and LAST < P

    table = nc.dram_tensor("table", [NT * P, TW], F32, kind="Internal").ap()
    slots_d = nc.dram_tensor("slots_d", [ROWS, ROW], BF16, kind="Internal").ap()

    ctx = ExitStack()
    with ctx:
        def sb(name, shape, dt=F32):
            return ctx.enter_context(nc.sbuf_tensor(name, shape, dt))

        def sem(name):
            return ctx.enter_context(nc.semaphore(name))

        bank = [ctx.enter_context(nc.psum_tensor(f"bank{i}", [P, 512], F32)) for i in range(8)]

        def carve(region, sizes):
            at, views = 0, {}
            for name, parts, shape, dt in sizes:
                n = 1
                for k in shape:
                    n *= k
                a = region[0:parts, at:at + n]
                if dt != F32:
                    a = a.bitcast(dt)
                if len(shape) == 2:
                    a = a.rearrange("p (a b) -> p a b", a=shape[0])
                if len(shape) == 3:
                    a = a.rearrange("p (a b c) -> p a b c", a=shape[0], b=shape[1])
                views[name] = a
                at += n
            assert at <= region.shape[1]
            return views

        swT_r = sb("swT_r", [P, max(4 * NT * P, 7424)])
        swT = swT_r[:, 0:4 * NT * P].rearrange("p (j n) -> p j n", j=4)
        prep = carve(swT_r, [("es", ROWS, [ROW], I32), ("ed", ROWS, [ROW], I32), ("esf", ROWS, [ROW], F32),
                             ("edf", ROWS, [ROW], F32), ("emi", ROWS, [ROW], I32), ("emf", ROWS, [ROW], F32),
                             ("Wx", P, [2, HG], F32), ("WxT", P, [4, D], F32), ("attb", P, [2, D], F32), ("watt", P, [2, D], F32),
                             ("uv", P, [NT, 2 * H], F32), ("uu", P, [NT, H], F32), ("su", P, [NT, H], F32), ("ab", P, [NT, 2 * H], F32), ("abr", P, [NT, 2 * H], F32)])
        es, ed, esf, edf, emi, emf, Wx, WxT, attb, watt, uv, uu, su, ab, abr = (prep[k] for k in prep)

        gt_r = sb("gt_r", [P, NB * CPG * TW])
        gt = gt_r[:, :].rearrange("p (b c e) -> p b c e", b=NB, c=CPG)
        late = carve(gt_r, [("tokn", P, [4, D + 1], F32), ("tokT", P, [2, HG], F32), ("nrow", 1, [HG], F32), ("stT", G, [HG], F32),
                            ("qkv", G, [3, HG], F32), ("at_s", G, [HG], F32), ("at_e", G, [HG], F32),
                            ("Z", P, [4, D], F32), ("swb", P, [2, 4, P], F32)])
        tokn, tokT, nrow, stT, qkv, at_s, at_e, Z, swb = (late[k] for k in late)
        at_T = at_s
        vwo = gt_r[0:G, 0:FH * D].rearrange("p (h n) -> p h n", h=FH)
        amx = sb("amx", [G, FH])
        rz = sb("rz", [P, 4])
        nrm = sb("nrm", [P, 2, 4])

        ident = sb("ident", [P, P])
        lane_i = sb("lane_i", [P, 1], I32)
        lane = sb("lane", [P, 1])
        cols_i = sb("cols_i", [P, P], I32)
        cols = sb("cols", [P, P], BF16)
        ones = sb("ones", [P, P])
        Wg = sb("Wg", [P, 2, D + 2 * H])
        gb = sb("gb", [P, D])
        bo = sb("bo", [P, D])
        Ws2 = sb("Ws2", [P, G])
        bxT = sb("bxT", [G, FH])
        bsl = sb("bsl", [1, G])
        tmp8 = sb("tmp8", [P, FH])
        itemp = sb("itemp", [P, FH])
        Wl = sb("Wl", [P, 2, HG])
        bl = sb("bl", [1, HG])
        Wf = sb("Wf", [P, 2, HG])
        bf = sb("bf", [1, HG])
        Wq = sb("Wq", [G, 3, G])
        Wo = sb("Wo", [G, FH, D])

        emb = sb("emb", [ROWS, ROW], BF16)
        mm = sb("mm", [ROWS, 2])
        idx = sb("idx", [P, ROWS * 4], I32)
        idxg = sb("idxg", [P, NB, CPG], I32)
        slot = sb("slot", [P, ROWS * 4], BF16)
        gmm = sb("gmm", [1, 2, NG])
        gi = sb("gi", [1, NG], I32)
        gblk = sb("gblk", [1, NG], I32)
        gmi = sb("gmi", [1, NG], I32)
        gmf = sb("gmf", [1, NG])
        mhi = sb("mhi", [P, NG])
        mlo = sb("mlo", [P, NG])
        flagf = sb("flagf", [1, 4])
        spr = sb("spr", [1, 1])
        flag = sb("flag", [1, 1], I32)

        xs = sb("xs", [P, NT, D])
        st = sb("st", [P, NT, 6])
        mv = sb("mv", [P, NT, 2])
        rstd = sb("rstd", [P, NT])
        xn = sb("xn", [P, 2, D])
        xT = sb("xT", [P, 2, D])
        acc = sb("acc", [P, NT + 1, AW])
        r2 = sb("r2", [P, 2])
        g2 = sb("g2", [2, 1])
        dg2 = sb("dg2", [2, 2])
        Gb = sb("Gb", [P, 2])
        nG = sb("nG", [P, 2])
        ab3 = sb("ab3", [P, NT + 1, 2 * H, 3], BF16)

        db = sb("db", [P, 2, GE], BF16)
        ot = sb("ot", [P, 2, GE], BF16)
        oh = sb("oh", [P, 2, CPG, P])
        tsa = sb("tsa", [P, 2, 2 * H * 3], BF16)
        tsl = sb("tsl", [P, 2, 2 * H * 3], BF16)
        abe = sb("abe", [P, 2, CPG, 2 * H])
        ee = sb("ee", [P, 2, CPG, 2 * H])
        we = sb("we", [P, 2, CPG, 2 * H])
        ACH = 3

        NCH = ROWS * 4
        dst_d = nc.dram_tensor("dst_d", [NCH, P], F32, kind="Internal").ap()
        BIG = 1e30
        xrow = gt[:, 0, 0, :]
        xdst = db[:, 0, 0:2 * P].bitcast(F32)
        xhot, xpen, xhotT = oh[:, 0, 0, :], oh[:, 0, 1, :], oh[:, 0, 2, :]
        xdiag, xtmp = oh[:, 1, 0:H, :], oh[:, 1, H:2 * H, :]
        xnode = sb("xnode", [P, 1])
        xmax = sb("xmax", [P, H])
        xred = sb("xred", [P, H])
        xtbl = sb("xtbl", [P, 2 * H])
        xs1 = sb("xs1", [P, H])
        xs2 = sb("xs2", [P, H])
        xw = sb("xw", [P, H])
        idx_of = lambda k: idx[:, bass.ds(k, 1)]

        rden = sb("rden", [P, H])
        z = sb("z", [P, D])
        zr = sb("zr", [P, D])
        stf = sb("stf", [P, 6])
        mvf = sb("mvf", [P, 3, 2])
        sdf = sb("sdf", [P, 3])
        xTf = sb("xTf", [P, D])
        mx = sb("mx", [P, FH])
        sm = sb("sm", [P, FH])
        sw = sb("sw", [P, HG])
        nrt = sb("nrt", [P, NT, 4])
        blb = sb("blb", [P, HG], BF16)
        blr = sb("blr", [1, HG])
        onesb = sb("onesb", [P, P], BF16)
        y = sb("y", [P, 2, D])
        thr_i = sb("thr_i", [1, NG + 2], I32)
        thr = sb("thr", [1, NG + 2])

        s_gat_load = sem("s_gat_load"); s_ffn_load = sem("s_ffn_load"); s_src_load = sem("s_src_load")
        s_dst_load = sem("s_dst_load")
        s_x_load = [sem(f"s_x_load{i}") for i in range(5)]
        s_pool = sem("s_pool"); s_const = sem("s_const")
        s_ef = sem("s_ef"); s_sl_st = sem("s_sl_st"); s_eT = sem("s_eT")
        s_gm = sem("s_gm"); s_gmT = sem("s_gmT"); s_idx = sem("s_idx"); s_flag = sem("s_flag")
        s_wxT = sem("s_wxT"); s_wxTc = sem("s_wxTc"); s_wl = sem("s_wl"); s_wlc = sem("s_wlc")
        s_var = sem("s_var"); s_sd = sem("s_sd"); s_normed = sem("s_normed"); s_xnT = sem("s_xnT")
        s_xTc = sem("s_xTc")
        s_xp = sem("s_xp"); s_xpc = sem("s_xpc"); s_table = sem("s_table"); s_r2 = sem("s_r2"); s_r2T = sem("s_r2T")
        s_dg = sem("s_dg"); s_G = sem("s_G"); s_ea = sem("s_ea"); s_ex = sem("s_ex"); s_edge = sem("s_edge")
        s_gathered = [sem(f"s_gathered{i}") for i in range(NB)]
        s_slots = [sem(f"s_slots{i}") for i in range(2)]
        s_onehot = sem("s_onehot"); s_tsl = sem("s_tsl"); s_onehot_e = sem("s_onehot_e"); s_lookup = sem("s_lookup")
        s_abe = sem("s_abe")
        s_scaled = sem("s_scaled"); s_rates = sem("s_rates"); s_weights = sem("s_weights")
        s_scaled_act = sem("s_scaled_act"); s_sums = sem("s_sums")
        s_merged = sem("s_merged")
        x_dst = sem("x_dst"); x_prep = sem("x_prep"); x_go = sem("x_go"); x_ix = sem("x_ix")
        x_gat = [sem(f"x_gat{u}") for u in range(CPG)]; x_got = sem("x_got"); x_db = sem("x_db")
        x_diag = sem("x_diag"); x_bc = sem("x_bc"); x_self = sem("x_self"); x_selfe = sem("x_selfe")
        x_hot = sem("x_hot"); x_lk = sem("x_lk"); x_arg = sem("x_arg"); x_exp = sem("x_exp"); x_rows = sem("x_rows")
        x_sum = sem("x_sum"); x_own = sem("x_own"); x_turn = sem("x_turn"); x_turn_v = sem("x_turn_v")
        x_turn_p = sem("x_turn_p")
        s_rd = sem("s_rd"); s_zz = sem("s_zz"); s_z = sem("s_z"); s_r = sem("s_r"); s_e = sem("s_e")
        s_sd2 = sem("s_sd2")
        s_logit_max = sem("s_logit_max"); s_ownA = sem("s_ownA"); s_ownB = sem("s_ownB"); s_thr = sem("s_thr")
        s_n2 = sem("s_n2"); s_n2T = sem("s_n2T"); s_n2c = sem("s_n2c")
        s_logits = sem("s_logits"); s_logit_exp = sem("s_logit_exp"); s_slice_w = sem("s_slice_w")
        s_tokens = sem("s_tokens")
        s_swT = sem("s_swT"); s_swc = sem("s_swc")
        s_tokn = sem("s_tokn"); s_att_pe = sem("s_att_pe"); s_att_act = sem("s_att_act"); s_att_dve = sem("s_att_dve")
        s_swb = sem("s_swb"); s_product = sem("s_product"); s_result = sem("s_result")
        s_stored = [sem(f"s_stored{i}") for i in range(2)]
        s_dv = sem("s_dv"); s_picked = sem("s_picked"); s_quick = sem("s_quick"); s_pad = sem("s_pad")
        s_turn = sem("s_turn")
        s_turn_v = sem("s_turn_v"); s_var2 = sem("s_var2"); s_rs = sem("s_rs")
        s_ta = sem("s_ta"); s_we = sem("s_we"); s_wp = sem("s_wp"); s_wb = sem("s_wb")
        s_watt = sem("s_watt")

        pT = (bank[4], bank[7])
        TOK = [bank[j // 2][:, (j % 2) * D:(j % 2 + 1) * D] for j in range(4)]
        SUMS, LOOK, WP, LOGIT, ELU, TR = (bank[i] for i in (2, 3, 4, 5, 6, 7))

        TL = 2
        NI = NG // NB
        TPI = NB // 2
        IN_LOOP = TPI * (NI - TL)
        assert NT - IN_LOOP == 3 and IN_LOOP % 2 == 0
        XB = 6
        XL = -(-(NT - 1) // XB) + 1
        EDGE_AT = 4 * (NT // 8)
        assert NT % 4 == 1
        xns = (xn[:, 0, :], xn[:, 1, :], y[:, 0, :], y[:, 1, :])

        wself = bank[7][:, 0:NT * H].rearrange("p (t h) -> p t h", h=H)

        first_of = [i * XB for i in range(XL - 1)] + [NT - 1, NT]

        def tiles_of(i):
            return slice(first_of[i], first_of[i + 1])

        def flat(a):
            return a.rearrange("p a b -> p (a b)")

        VWO = (4, 5, 3, 7)

        def logits_of(t):
            return LOGIT if t % 2 == 0 else SUMS

        def runs(t):
            return not isinstance(t, int) or t >= 0

        def by_head(a):
            return a.rearrange("p (h g) -> p h g", g=G)

        def over_slices(a):
            return a.unsqueeze(2).broadcast_to((a.shape[0], FH, G))

        def abs3(blk):
            return ab3[:, bass.ds(blk, 1), :, :].rearrange("p t e c -> p (t e c)")

        block = ctx.enter_context(nc.Block())

        @block.sync
        def _(sp):
            for i in range(XL - 1):
                a, b = first_of[i], first_of[i + 1]
                sp.dma_start(xs[:, a:b, :], x[a * P:b * P, :].rearrange("(t p) d -> p t d", p=P)).then_inc(s_x_load[i], 16)
                if i == 0:
                    sp.dma_start(attb[:, 1, :], att_dst.rearrange("(a h) c -> a (h c)", a=1).broadcast_to((P, D))).then_inc(s_gat_load, 16)
            sp.wait_ge(s_pool, 1)
            sp.dma_start(xs[0:LAST, NT - 1, :], x[(NT - 1) * P:N, :]).then_inc(s_x_load[XL - 1], 16)
            sp.dma_start(Wx[:, :, :], W_x.rearrange("(k p) n -> p k n", p=P)).then_inc(s_ffn_load, 16)
            sp.dma_start(Ws2[0:G, :], W_slice).then_inc(s_ffn_load, 16)
            sp.dma_start(Ws2[G:P, :], W_slice).then_inc(s_ffn_load, 16)
            sp.dma_start(bxT[:, :], b_x.rearrange("(h c) -> c h", c=G), allow_slow_non_contiguous=True).then_inc(s_ffn_load, 16)
            sp.dma_start(bsl[:, :], b_slice.rearrange("(a n) -> a n", a=1)).then_inc(s_ffn_load, 16)
            sp.dma_start(tmp8[:, :], temperature.rearrange("a h b c -> (a b c) h").broadcast_to((P, FH))).then_inc(s_ffn_load, 16)
            sp.dma_start(Wf[:, :, :], W_fx.rearrange("(k p) n -> p k n", p=P)).then_inc(s_ffn_load, 16)
            sp.dma_start(bf[:, :], b_fx.rearrange("(a n) -> a n", a=1)).then_inc(s_ffn_load, 16)
            for i, w in enumerate((W_q, W_k, W_v)):
                sp.dma_start(Wq[:, i, :], w).then_inc(s_ffn_load, 16)
            sp.dma_start(Wo[:, :, :], W_out.rearrange("(h c) n -> c h n", c=G)).then_inc(s_ffn_load, 16)

            def put(t):
                sp.wait_ge(s_xpc, t + 1)
                sp.dma_start(table[bass.ds(t * P, P), :], acc[:, bass.ds(t, 1), 0:TW]).then_inc(s_table, 16)
            with sp.Fori(0, EDGE_AT) as t:
                put(t)
            sp.wait_ge(s_ef, 3)
            sp.dma_start(slots_d, emb[:, :]).then_inc(s_sl_st, 16)
            with sp.Fori(EDGE_AT, NT) as t:
                put(t)

            def spread_slots(g, b):
                if not isinstance(g, int) or g >= 2:
                    sp.wait_ge(s_onehot, g - 1)
                sp.dma_start(db[:, b, :], slots_d.rearrange("(g r) c -> g (r c)", r=RPG)[bass.ds(g, 1), :]
                             .broadcast_to((P, GE))).then_inc(s_slots[b], 16)
            sp.wait_ge(s_flag, 1)
            general = sp.value_load(flag[0:1, 0:1], min_val=0, max_val=1)
            sp.wait_ge(s_sl_st, 16)
            with sp.If(general == 0):
                for g in range(NB):
                    spread_slots(g, g % 2)
                with sp.Fori(1, NG // NB) as i:
                    for u in range(NB):
                        spread_slots(NB * i + u, u % 2)
            with sp.Else():
                sp.dma_start(dst_d.rearrange("(r i) c -> r (i c)", i=4), edf[:, :]).then_inc(x_dst, 16)
                sp.wait_ge(x_dst, 16)
                with sp.Fori(0, 2 * NT) as n:
                    with sp.Fori(0, NCH) as k:
                        sp.wait_ge(x_go, n * NCH + k + 1)
                        sp.dma_start(xdst, dst_d[bass.ds(k, 1), :].broadcast_to((P, P))).then_inc(x_db, 16)

            def store(t, b, n):
                sp.wait_ge(s_result, t + 1)
                sp.dma_start(out[bass.ds(t * P, n), :], y[0:n, b, :]).then_inc(s_stored[b], 16)
            with sp.Fori(0, NT // 2) as i:
                for u in range(2):
                    store(2 * i + u, u, P)
            store(NT - 1, 0, LAST)
            sp.wait_ge(s_stored[0], 16 * ((NT + 1) // 2))
            sp.wait_ge(s_stored[1], 16 * (NT // 2))

        @block.gpsimd
        def _(pool):
            pool.memset(xs[:, NT - 1, :], 0.0).then_inc(s_pool, 1)
            pool.memset(ident[:, :], 0.0).then_inc(s_pool, 1)
            pool.iota(lane_i[:, :], pattern=[[0, 1]], base=0, channel_multiplier=1).then_inc(s_pool, 1)
            pool.iota(cols_i[:, :], pattern=[[1, P]], base=0, channel_multiplier=0).then_inc(s_pool, 1)
            pool.iota(thr_i[:, :], pattern=[[P, NG // 2 + 1], [0, 2]], base=P * (1 - TPI * TL), channel_multiplier=0).then_inc(s_thr, 1)
            pool.wait_ge(s_pool, 4)
            pool.wait_ge(s_thr, 1)
            pool.affine_select(out=ident[:, :], in_=ident[:, :], compare_op=ALU.not_equal, fill=1.0, base=0,
                               pattern=[[-1, P]], channel_multiplier=1).then_inc(s_const, 1)
            pool.tensor_copy(lane[:, :], lane_i[:, :]).then_inc(s_const, 1)
            pool.tensor_copy(cols[:, :], cols_i[:, :]).then_inc(s_const, 1)
            pool.memset(ones[:, :], 1.0).then_inc(s_const, 1)
            pool.memset(onesb[:, :], 1.0).then_inc(s_const, 1)
            pool.memset(acc[:, NT, :], 0.0).then_inc(s_const, 1)
            pool.memset(ab3[:, NT, :, :], 0.0).then_inc(s_const, 1)
            pool.memset(blb[:, :], 0.0).then_inc(s_const, 1)
            pool.wait_ge(s_table, 16 * NT)

            def gather(g, b):
                if not isinstance(g, int) or g >= NB:
                    pool.wait_ge(s_sums, g - NB + 1)
                pool.wait_ge(s_picked, g + 1)
                pool.sem_inc(s_turn, 1)
                for c in range(CPG):
                    pool.indirect_dma_start(
                        gt[:, b, c, :], None, table,
                        bass.IndirectOffsetOnAxis(idxg[:, b, c:c + 1], 0)).then_inc(s_gathered[b], 16)
            for g in range(NB):
                gather(g, g)
            pool.wait_ge(s_flag, 1)
            general = pool.value_load(flag[0:1, 0:1], min_val=0, max_val=1)
            with pool.If(general == 0):
                with pool.Fori(1, NG // NB) as i:
                    for u in range(NB):
                        gather(NB * i + u, u)
            with pool.Else():
                for b in range(NB):
                    pool.wait_ge(s_gathered[b], 16 * CPG)
                with pool.Fori(0, 2 * NT) as n:
                    with pool.Fori(0, NG) as m:
                        for u in range(CPG):
                            pool.wait_ge(x_ix, n * NCH + CPG * m + u + 1)
                            pool.sem_inc(x_turn, 1)
                            pool.indirect_dma_start(xrow, None, table, bass.IndirectOffsetOnAxis(idxg[:, 0, 0:1], 0)).then_inc(x_gat[u], 16)
                            pool.wait_ge(x_gat[u], 16 * (n * NG + m + 1))
                            pool.sem_inc(x_got, 1)

        @block.scalar
        def _(act):
            act.dma_start(Wg[:, :, 0:D], W.rearrange("(k p) n -> p k n", p=P)).then_inc(s_gat_load, 16)
            act.dma_start(attb[:, 0, :], att_src.rearrange("(a h) c -> a (h c)", a=1).broadcast_to((P, D))).then_inc(s_gat_load, 16)
            act.wait_ge(s_pad, 2)
            act.dma_start(ed[0:FULL, :], dst[0:FULL * ROW].rearrange("(r c) -> r c", c=ROW)).then_inc(s_dst_load, 16)
            act.dma_start(ed[FULL:FULL + 1, 0:REST], dst[FULL * ROW:E].rearrange("(r c) -> r c", r=1)).then_inc(s_dst_load, 16)
            act.dma_start(es[0:FULL, :], src[0:FULL * ROW].rearrange("(r c) -> r c", c=ROW)).then_inc(s_src_load, 16)
            act.dma_start(es[FULL:FULL + 1, 0:REST], src[FULL * ROW:E].rearrange("(r c) -> r c", r=1)).then_inc(s_src_load, 16)
            act.dma_start(gb[:, :], gbias.rearrange("(a n) -> a n", a=1).broadcast_to((P, D))).then_inc(s_wb, 16)
            act.dma_start(bo[:, :], b_out.rearrange("(a n) -> a n", a=1).broadcast_to((P, D))).then_inc(s_wb, 16)

            def deviation(i):
                act.wait_ge(s_var, i + 1)
                act.activation(rstd[:, tiles_of(i)], mv[:, tiles_of(i), 1], ACT.Sqrt).then_inc(s_sd, 1)

            def evac_xT(t, b):
                act.wait_ge(s_xnT, t + 1)
                act.copy(xT[:, b, :], pT[b][:, 0:D]).then_inc(s_xTc, 1)

            def take(t, b):
                act.wait_ge(s_xp, t + 1)
                act.copy(flat(acc[:, bass.ds(t, 1), :]), bank[5 + b][:, 0:AW]).then_inc(s_xpc, 1)
            deviation(0)
            evac_xT(0, 0)
            for i in range(XL):
                with act.Fori(max(0, first_of[i] - 4) // 2, (first_of[i + 1] - 4) // 2 if i < XL - 1 else NT // 2) as k:
                    for u in range(2):
                        evac_xT(2 * k + u + 1, 1 - u)
                        take(2 * k + u, u)
                if i + 1 < XL:
                    deviation(i + 1)
            take(NT - 1, 0)
            act.wait_ge(s_idx, 1)
            act.copy(idxg[:, :, :].rearrange("p b c -> p (b c)"), idx[:, 0:NB * CPG]).then_inc(s_picked, NB)
            act.wait_ge(s_ea, 1)
            act.activation(ab[:, :, :], uv[:, :, :], ACT.Exp).then_inc(s_ex, 1)
            act.activation(wself, su[:, :, :], ACT.Exp).then_inc(s_ex, 1)
            for k in range(2):
                act.wait_ge(s_wxT, k + 1)
                act.copy(WxT[:, :, k * P:(k + 1) * P], bank[k][:, :].rearrange("p (j n) -> p j n", j=4)).then_inc(s_wxTc, 1)

            def half_a(t):
                act.wait_ge(s_rd, t + 1)
                for h in range(H):
                    last = act.activation(ELU[:, h * C:(h + 1) * C], flat(acc[:, bass.ds(t, 1), h * C:(h + 1) * C]), ACT.Copy, scale=rden[:, h:h + 1])
                last.then_inc(s_zz, 1)

            def elu(t):
                act.wait_ge(s_z, t + 1)
                act.activation(zr[:, :], z[:, :], ACT.Relu, scale=-1.0).then_inc(s_r, 1)
                act.wait_ge(s_r, t + 1)
                act.activation(ELU[:, 0:D], zr[:, :], ACT.Exp, scale=-1.0).then_inc(s_e, 1)

            def root(t, n):
                act.wait_ge(s_var2, t + 1)
                act.activation(sdf[:, 0:n], mvf[:, 0:n, 1], ACT.Sqrt).then_inc(s_sd2, 1)

            def turn(t):
                act.wait_ge(s_n2T, t + 1)
                act.copy(xTf[:, :], TR[:, 0:D]).then_inc(s_n2c, 1)

            def exps(t, LOGIT=LOGIT):
                act.wait_ge(s_logit_max, t + 1)
                for h in range(FH):
                    s = slice(h * G, (h + 1) * G)
                    last = act.activation(LOGIT[:, s], LOGIT[:, s], ACT.Exp, bias=mx[:, h:h + 1], accum_out=sm[:, h:h + 1])
                last.then_inc(s_logit_exp, 1)

            def close(t, n=P, TR=TR):
                act.wait_ge(s_swT, t + 1)
                for j in range(4):
                    last = act.activation(swT[:, j, bass.ds(t * P, n)], TR[:, j * P:j * P + n], ACT.Copy,
                                          accum_out=flat(nrt[:, bass.ds(t, 1), j:j + 1]))
                last.then_inc(s_swc, 1)

            def pick(g, u):
                act.copy(idxg[:, u, :], idx[:, bass.ds(g * CPG, CPG)]).then_inc(s_picked, 1)

            def rates(i, u):
                g, b = NB * i + u, u % 2
                if not (isinstance(i, int) and g < 2):
                    act.wait_ge(s_we, g - 1)
                act.wait_ge(s_gathered[u], 16 * CPG * (i + 1))
                act.activation(ee[:, b, :, 0:H], gt[:, u, :, D:D + H], ACT.Exp, bias=nG[:, 0:1])
                act.activation(ee[:, b, :, H:2 * H], gt[:, u, :, D:D + H], ACT.Exp, bias=nG[:, 1:2], scale=0.2).then_inc(s_rates, 1)

            def scale(i, u):
                g = NB * i + u
                act.wait_ge(s_weights, g + 1)
                for c in range(CPG - ACH, CPG):
                    for h in range(H):
                        r = gt[:, u, c, h * C:(h + 1) * C]
                        last = act.activation(r, r, ACT.Copy, scale=gt[:, u, c, D + h:D + h + 1])
                last.then_inc(s_scaled_act, 1)

            def iteration(i):
                for u in range(NB):
                    t = TPI * (i - TL) + u // 2
                    more = not (isinstance(i, int) and i == NI - 1 and u == NB - 1)
                    if not isinstance(i, int) or i < NI - 1:
                        pick(NB * (i + 1) + u, u)
                    if u % 2 == 0:
                        if runs(t):
                            half_a(t)
                        scale(i, u)
                        if more:
                            rates(i + (u + 1) // NB, (u + 1) % NB)
                        if runs(t - 3):
                            close(t - 3)
                        if runs(t):
                            elu(t)
                    else:
                        if runs(t - 2):
                            turn(t - 2)
                        scale(i, u)
                        if more:
                            rates(i + (u + 1) // NB, (u + 1) % NB)
                        if runs(t - 2):
                            exps(t - 2)
                        if u == NB - 1 and runs(t):
                            root(t, 2)

            act.wait_ge(s_flag, 1)
            general = act.value_load(flag[0:1, 0:1], min_val=0, max_val=1)
            with act.If(general == 0):
                rates(0, 0)
                for i in range(TL + 2):
                    iteration(i)
                with act.Fori(TL + 2, NI - 1) as i:
                    iteration(i)
                iteration(NI - 1)
                t = IN_LOOP
                half_a(t)
                turn(t - 2)
                elu(t)
                close(t - 3, TR=LOOK)
                exps(t - 2, logits_of(t - 2))
                turn(t - 1)
                half_a(t + 1)
                elu(t + 1)
                exps(t - 1, logits_of(t - 1))
                half_a(t + 2)
                close(t - 2, TR=LOOK)
                elu(t + 2)
                close(t - 1, TR=LOOK)
                root(t + 2, 3)
                turn(t)
                turn(t + 1)
                exps(t, logits_of(t))
                close(t, TR=LOOK)
                exps(t + 1, logits_of(t + 1))
                turn(t + 2)
                exps(t + 2, logits_of(t + 2))
                close(t + 1, TR=LOOK)
                close(t + 2, LAST, TR=LOOK)
            with act.Else():
                act.wait_ge(s_gathered[0], 16 * CPG)
                def pick1(q, k):
                    act.wait_ge(x_go, q + 1)
                    act.copy(idxg[:, 0, 0:1], idx_of(k)).then_inc(x_ix, 1)
                with act.Fori(0, NT) as j:
                    with act.Fori(0, NCH) as k:
                        pick1(2 * NCH * j + k, k)
                    act.wait_ge(x_self, j + 1)
                    act.activation(xw[:, :], xs1[:, :], ACT.Exp).then_inc(x_selfe, 1)
                    with act.Fori(0, NCH) as k:
                        pick1(2 * NCH * j + NCH + k, k)
                        act.wait_ge(x_arg, NCH * j + k + 1)
                        act.activation(xw[:, :], xs1[:, :], ACT.Exp).then_inc(x_exp, 1)

                def tiles(t, n, rows=P):
                    for k in range(n):
                        half_a(t + k)
                        elu(t + k)
                    root(t + n - 1, n)
                    for k in range(n):
                        turn(t + k)
                        exps(t + k)
                        close(t + k, rows)
                tiles(0, 2)
                with act.Fori(1, NT // 2) as i:
                    tiles(2 * i, 2)
                tiles(NT - 1, 1, LAST)

            act.wait_ge(s_tokn, 1)
            act.wait_ge(s_tokens, NT)
            for j in range(2, 4):
                last = act.activation(tokn[:, j, 0:D], TOK[j], ACT.Copy, scale=nrm[:, 1, j:j + 1])
            last.then_inc(s_att_act, 1)
            act.wait_ge(s_att_pe, 1)
            act.copy(tokT[:, 0, :], bank[4][:, :]).then_inc(s_att_act, 1)
            act.wait_ge(s_att_pe, 3)
            act.copy(nrow, bank[7][0:1, :]).then_inc(s_att_act, 1)
            act.wait_ge(s_att_pe, 4)
            act.copy(stT[:, 0:HG // 2], bank[0][0:G, 0:HG // 2]).then_inc(s_att_act, 1)
            act.wait_ge(s_att_pe, 6)
            act.copy(qkv[:, 0, :], bank[1][0:G, :]).then_inc(s_att_act, 1)
            act.wait_ge(s_att_pe, 8)
            act.copy(qkv[:, 2, :], bank[6][0:G, :]).then_inc(s_att_act, 1)
            for i in range(4):
                act.wait_ge(s_att_pe, 10 + i)
                act.copy(vwo[:, 2 * i:2 * i + 2, :], bank[VWO[i]][0:G, :].rearrange("p (h n) -> p h n", h=2)).then_inc(s_att_act, 1)
                if i == 0:
                    act.wait_ge(s_att_dve, 4)
                    act.activation(at_e[:, :], at_s[:, :], ACT.Exp, scale=float(G) ** -0.5).then_inc(s_att_act, 1)
            def weights_of(t, b, n=P):
                act.copy(swb[:, b, :, 0:n], swT[:, :, bass.ds(t * P, n)]).then_inc(s_swb, 1)
            for t in range(2):
                weights_of(t, t)
            act.wait_ge(s_att_dve, 6)
            act.wait_ge(s_att_pe, 17)
            for j in range(2, 4):
                last = act.activation(Z[:, j, :], bank[0][:, (j % 2) * D:(j % 2 + 1) * D], ACT.Copy, scale=rz[:, j:j + 1])
            last.then_inc(s_att_act, 1)

            with act.Fori(1, NT // 2) as i:
                for u in range(2):
                    act.wait_ge(s_product, 2 * i + u - 1)
                    weights_of(2 * i + u, u)
            act.wait_ge(s_product, NT - 2)
            weights_of(NT - 1, 0, LAST)

        @block.tensor
        def _(pe):
            mm_ = nc.tensor.matmul
            def turn(t, b):
                pe.wait_ge(s_normed, t + 1)
                if not isinstance(t, int) or t >= 2:
                    pe.wait_ge(s_xTc, t - 1)
                for k in range(2):
                    last = nc.tensor.transpose(pT[b % 2][:, k * P:(k + 1) * P], xns[b][:, k * P:(k + 1) * P], ident[:, :])
                last.then_inc(s_xnT, 1)

            def proj(t, b):
                pe.wait_ge(s_xTc, t + 1)
                if not isinstance(t, int) or t >= 2:
                    pe.wait_ge(s_xpc, t - 1)
                for k in range(2):
                    last = mm_(bank[5 + b][:, 0:AW], xT[:, b, k * P:(k + 1) * P], Wg[:, k, :], start=(k == 0), stop=(k == 1))
                last.then_inc(s_xp, 1)

            def keep_busy(n, bank=WP):
                for _ in range(n):
                    mm_(bank[:, :], onesb[:, :], blb[:, :], start=True, stop=True)

            pe.wait_ge(s_const, 8)
            keep_busy(26, bank[0])
            turn(0, 0)
            turn(1, 1)
            pe.wait_ge(s_watt, 2)
            proj(0, 0)
            for t in range(1, 4):
                turn(t + 1, (t + 1) % 4)
                proj(t, t % 2)
            with pe.Fori(1, EDGE_AT // 4) as i:
                for u in range(4):
                    turn(4 * i + u + 1, (u + 1) % 4)
                    proj(4 * i + u, u % 2)
            pe.wait_ge(s_ef, 5)
            for i in range(4):
                nc.tensor.transpose(bank[0][:, i * ROWS:(i + 1) * ROWS], esf[:, i * P:(i + 1) * P], ident[0:ROWS, 0:ROWS])
                last = nc.tensor.transpose(bank[1][:, i * ROWS:(i + 1) * ROWS], emf[:, i * P:(i + 1) * P], ident[0:ROWS, 0:ROWS])
            last.then_inc(s_eT, 1)
            for i in range(2):
                last = nc.tensor.transpose(bank[2][0:1, i * ROWS:(i + 1) * ROWS], mm[:, i:i + 1], ident[0:ROWS, 0:ROWS])
            last.then_inc(s_eT, 1)
            with pe.Fori(EDGE_AT // 4, NT // 4) as i:
                for u in range(4):
                    turn(4 * i + u + 1, (u + 1) % 4)
                    proj(4 * i + u, u % 2)
            proj(NT - 1, 0)
            pe.wait_ge(s_gm, 1)
            mm_(bank[3][:, 0:NG], ones[0:1, :], gmf[:, :], start=True, stop=True).then_inc(s_gmT, 1)

            pe.wait_ge(s_r2, 1)
            nc.tensor.transpose(bank[5][0:2, 0:P], r2[:, :], ident[:, :]).then_inc(s_r2T, 1)
            pe.wait_ge(s_dg, 1)
            mm_(bank[6][:, 0:2], ones[0:2, :], dg2[:, :], start=True, stop=True).then_inc(s_G, 1)

            pe.wait_ge(s_edge, 1)
            pe.wait_ge(s_ffn_load, 16 * 12)
            for k in range(2):
                for j in range(4):
                    last = nc.tensor.transpose(bank[k][:, j * P:(j + 1) * P], Wx[:, k, j * P:(j + 1) * P], ident[:, :])
                last.then_inc(s_wxT, 1)
            pe.wait_ge(s_wxTc, 2)
            for k in range(2):
                for h in range(FH):
                    o = G * (h % 2)
                    j = h // 2
                    last = mm_(bank[2 + k + 2 * (h % 2)][:, j * G:(j + 1) * G], WxT[o:o + G, h // 2, k * P:(k + 1) * P], Ws2[o:o + G, :],
                               start=True, stop=True)
                last.then_inc(s_wl, 1)
            for h in range(FH):
                last = mm_(bank[0][0:1, h * G:(h + 1) * G], bxT[:, h:h + 1], Ws2[0:G, :], start=True, stop=True)
            last.then_inc(s_wl, 1)


            def lookup(i, u):
                g, b = NB * i + u, u % 2
                pe.wait_ge(s_onehot, g + 1)
                pe.wait_ge(s_tsl, g + 1)
                if not (isinstance(i, int) and g == 0):
                    pe.wait_ge(s_abe, g)
                for c in range(CPG):
                    last = mm_(LOOK[:, c * 24:(c + 1) * 24], ot[:, b, c * P:(c + 1) * P], tsl[:, b, :], start=True, stop=True)
                last.then_inc(s_lookup, 1)

            def sums(i, u):
                g, b = NB * i + u, u % 2
                pe.wait_ge(s_onehot_e, g + 1)
                pe.wait_ge(s_scaled, g + 1)
                pe.wait_ge(s_scaled_act, g + 1)
                if not (isinstance(i, int) and g == 0):
                    pe.wait_ge(s_merged, g)
                for c in range(CPG):
                    last = mm_(SUMS[:, 0:D + H], oh[:, b, c, :], gt[:, u, c, 0:D + H], start=(c == 0), stop=(c == CPG - 1))
                last.then_inc(s_sums, 1)

            def half_b(t, b, LOGIT=LOGIT, own_bank=False):
                pe.wait_ge(s_n2, t + 1)
                if not own_bank and not (isinstance(t, int) and t == 0):
                    pe.wait_ge(s_swc, t)
                for k in range(2):
                    last = nc.tensor.transpose(TR[:, k * P:(k + 1) * P], xn[:, b, k * P:(k + 1) * P], ident[:, :])
                last.then_inc(s_n2T, 1)
                mm_(LOGIT[:, :], onesb[:, :], blb[:, :], start=True, stop=False)
                pe.wait_ge(s_n2c, t + 1)
                for k in range(2):
                    last = mm_(LOGIT[:, :], xTf[:, k * P:(k + 1) * P], Wl[:, k, :], start=False, stop=(k == 1))
                last.then_inc(s_logits, 1)

            def close(t, b, n=P, TR=TR):
                pe.wait_ge(s_slice_w, t + 1)
                if TR is LOOK:
                    pe.wait_ge(s_swc, t)
                for j in range(4):
                    last = nc.tensor.transpose(TR[:, j * P:(j + 1) * P], sw[:, j * P:(j + 1) * P], ident[:, :])
                last.then_inc(s_swT, 1)
                for j in range(4):
                    last = mm_(TOK[j], sw[0:n, j * P:(j + 1) * P], xn[0:n, b, :], start=(isinstance(t, int) and t == 0 and j % 2 == 0),
                               stop=(isinstance(t, int) and t == NT - 1), skip_group_check=True)
                last.then_inc(s_tokens, 1)

            def iteration(i):
                for u in range(NB):
                    if not (isinstance(i, int) and i == NI - 1 and u == NB - 1):
                        lookup(i + (u + 1) // NB, (u + 1) % NB)
                    t = TPI * (i - TL) + u // 2
                    if u % 2 == 0 and runs(t - 3):
                        close(t - 3, (u // 2 + 1) % 2)
                    if u % 2 == 1 and runs(t - 2):
                        half_b(t - 2, u // 2)
                    sums(i, u)

            pe.wait_ge(s_flag, 1)
            general = pe.value_load(flag[0:1, 0:1], min_val=0, max_val=1)
            with pe.If(general == 0):
                lookup(0, 0)
                for i in range(TL + 2):
                    iteration(i)
                with pe.Fori(TL + 2, NI - 1) as i:
                    iteration(i)
                iteration(NI - 1)
                pe.wait_ge(s_abe, NG)
                close(IN_LOOP - 3, 1, TR=LOOK)
                half_b(IN_LOOP - 2, 0, logits_of(IN_LOOP - 2), True)
                pe.wait_ge(s_merged, NG)
                half_b(IN_LOOP - 1, 1, logits_of(IN_LOOP - 1), True)
                keep_busy(2)
                close(IN_LOOP - 2, 0, TR=LOOK)
                keep_busy(10)
                close(IN_LOOP - 1, 1, TR=LOOK)
                keep_busy(4)
                half_b(IN_LOOP, 0, logits_of(IN_LOOP), True)
                for t in range(IN_LOOP, NT):
                    if t + 1 < NT:
                        half_b(t + 1, (t + 1) % 2, logits_of(t + 1), True)
                    keep_busy(2)
                    close(t, t % 2, P if t < NT - 1 else LAST, TR=LOOK)
            with pe.Else():
                with pe.Fori(0, NT) as j:
                    with pe.Fori(0, NCH) as k:
                        pe.wait_ge(x_diag, NCH * j + k + 1)
                        mm_(bank[0][:, 0:H * P], ones[:, :], xdiag, start=True, stop=True).then_inc(x_bc, 1)
                    pe.wait_ge(x_self, j + 1)
                    pe.sem_inc(x_turn_p, 1)
                    with pe.Fori(0, NCH) as k:
                        pe.wait_ge(x_hot, NCH * j + k + 1)
                        mm_(bank[1][:, 0:2 * H], xhot, xtbl[:, :], start=True, stop=True)
                        nc.tensor.transpose(bank[2][:, 0:P], xhot, ident[:, :]).then_inc(x_lk, 1)
                        pe.wait_ge(x_rows, NCH * j + k + 1)
                        mm_(bank[3][:, 0:D + H], xhotT, xrow[:, 0:D + H], start=True, stop=True).then_inc(x_sum, 1)

                def tile(t, b, n=P):
                    half_b(t, b)
                    close(t, b, n)
                for t in range(2):
                    tile(t, t)
                with pe.Fori(1, NT // 2) as i:
                    for u in range(2):
                        tile(2 * i + u, u)
                tile(NT - 1, 0, LAST)

            keep_busy(6)
            pe.wait_ge(s_tokn, 2)
            pe.wait_ge(s_att_act, 1)
            pe.wait_ge(s_swc, NT)
            for k in range(2):
                for j in range(4):
                    last = nc.tensor.transpose(bank[4 + k][:, j * P:(j + 1) * P], tokn[:, j, k * P:(k + 1) * P], ident[:, :])
                last.then_inc(s_att_pe, 1)
            for j in range(4):
                last = nc.tensor.transpose(bank[7][0:1, j * P:(j + 1) * P], tokn[:, j, D:D + 1], ident[:, :])
            last.then_inc(s_att_pe, 1)
            pe.wait_ge(s_att_act, 3)
            pe.wait_ge(s_att_dve, 1)
            for h in range(FH):
                s = slice(h * G, (h + 1) * G)
                o = slice((h % 4) * G, (h % 4 + 1) * G)
                for k in range(2):
                    mm_(bank[3 * (h // 4)][0:G, o], Wf[:, k, s], tokT[:, k, s], start=(k == 0), stop=False)
                last = mm_(bank[3 * (h // 4)][0:G, o], bf[:, s], nrow[:, s], start=False, stop=True)
                if h % 4 == 3:
                    last.then_inc(s_att_pe, 1)
            pe.wait_ge(s_att_act, 4)
            pe.wait_ge(s_att_dve, 2)
            for i, k in enumerate((1, 2, 6)):
                mm_(bank[k][0:G, :], Wq[:, i, :], stT, start=True, stop=True).then_inc(s_att_pe, 1)
            pe.wait_ge(s_att_act, 5)
            pe.wait_ge(s_att_dve, 3)
            for h in range(FH):
                s = slice(h * G, (h + 1) * G)
                last = mm_(bank[0][0:G, s], qkv[:, 0, s], qkv[:, 1, s], start=True, stop=True)
            last.then_inc(s_att_pe, 1)
            pe.wait_ge(s_att_act, 6)
            for h in range(FH):
                last = mm_(bank[VWO[h // 2]][0:G, (h % 2) * D:(h % 2 + 1) * D], qkv[:, 2, h * G:(h + 1) * G], Wo[:, h, :], start=True, stop=True)
                if h % 2 == 1:
                    last.then_inc(s_att_pe, 1)
            pe.wait_ge(s_att_act, 8)
            for h in range(FH):
                s = slice(h * G, (h + 1) * G)
                last = nc.tensor.transpose(bank[1][0:G, s], at_e[:, s], ident[0:G, 0:G])
            last.then_inc(s_att_pe, 1)
            pe.wait_ge(s_att_dve, 5)
            for h in range(FH):
                o, j = G * (h % 2), h // 2
                last = mm_(bank[2][o:o + G, j:j + 1], at_T[:, h * G:(h + 1) * G], ones[0:G, 0:1], start=True, stop=True)
            last.then_inc(s_att_pe, 1)
            pe.wait_ge(s_att_act, 11)
            for h in range(FH):
                o, j = G * (h % 2), h // 2
                last = mm_(bank[6 - 6 * (j // 2)][o:o + G, (j % 2) * D:(j % 2 + 1) * D], at_T[:, h * G:(h + 1) * G], vwo[:, h, :],
                           start=True, stop=True)
                if h % 4 == 3:
                    last.then_inc(s_att_pe, 1)

            def ffn2(t, b, n=P):
                pe.wait_ge(s_swb, t + 1)
                if not isinstance(t, int) or t >= 2:
                    pe.wait_ge(s_result, t - 1)
                for j in range(4):
                    last = mm_(bank[b][0:n, 0:D], swb[:, b, j, 0:n], Z[:, j, :], start=(j == 0), stop=(j == 3))
                last.then_inc(s_product, 1)
            pe.wait_ge(s_att_dve, 7)
            pe.wait_ge(s_att_act, 12)
            for t in range(2):
                ffn2(t, t)
            with pe.Fori(1, NT // 2) as i:
                for u in range(2):
                    ffn2(2 * i + u, u)
            ffn2(NT - 1, 0, LAST)

        @block.vector
        def _(v):
            own = Chain(v, s_dv)
            v.memset(ed[PAD_BASE:ROWS, :], N).then_inc(s_pad, 1)
            v.memset(es[PAD_BASE:ROWS, :], 0).then_inc(s_pad, 1)
            def attention_weights():
                v.wait_ge(s_gat_load, 16 * 3)
                for i in range(2):
                    for k in range(2):
                        own.add(v.tensor_tensor(watt[:, k, :], Wg[:, k, 0:D], attb[:, i, :], ALU.mult))
                    own.wait()
                    v.tensor_reduce(Wg[:, :, D + i * H:D + (i + 1) * H],
                                    watt[:, :, :].rearrange("p k (h c) -> p k h c", c=C), X, ALU.add).then_inc(s_watt, 1)
                    v.wait_ge(s_watt, i + 1)

            def moments(i):
                tiles = range(NT)[tiles_of(i)]
                v.wait_ge(s_x_load[i], 16)
                for t in tiles:
                    own.add(v.bn_stats(st[:, t, :], xs[:, t, :]))
                own.wait()
                for t in tiles:
                    own.add(v.bn_aggr(mv[:, t, :], st[:, t, :]))
                own.wait()
                v.tensor_scalar(mv[:, tiles_of(i), 1], mv[:, tiles_of(i), 1], EPS, None, ALU.add).then_inc(s_var, 1)

            def inverse(i):
                v.wait_ge(s_sd, i + 1)
                own.add(v.reciprocal(rstd[:, tiles_of(i)], rstd[:, tiles_of(i)]))
                own.wait()

            def norm(t, b):
                if t >= 4:
                    v.wait_ge(s_xnT, t - 3)
                v.tensor_scalar(xns[b], xs[:, t, :], mv[:, t, 0:1], rstd[:, t:t + 1], ALU.subtract, ALU.mult).then_inc(s_normed, 1)

            def edge_rows():
                v.wait_ge(s_dst_load, 32)
                own.add(v.tensor_scalar(emi[:, :], ed[:, :], P - 1, None, ALU.bitwise_and))
                own.add(v.tensor_copy(edf[:, :], ed[:, :]))
                v.wait_ge(s_src_load, 32)
                v.tensor_copy(esf[:, :], es[:, :]).then_inc(s_ef, 1)
                own.wait()
                v.tensor_copy(emf[:, :], emi[:, :]).then_inc(s_ef, 1)
                v.tensor_copy(emb[:, :], emi[:, :]).then_inc(s_ef, 1)
                v.tensor_reduce(mm[:, 0:1], edf[:, :], X, ALU.min).then_inc(s_ef, 1)
                v.tensor_reduce(mm[:, 1:2], edf[:, :], X, ALU.max).then_inc(s_ef, 1)

            def edge_chunks():
                v.wait_ge(s_const, 8)
                v.wait_ge(s_thr, 1)
                own.add(v.tensor_copy(thr[:, :], thr_i[:, :]))
                v.wait_ge(s_eT, 1)
                own.add(v.tensor_copy(idx[:, :].rearrange("p (q i) -> p q i", i=4), bank[0][:, 0:4 * ROWS].rearrange("p (i q) -> p q i", i=4)))
                own.add(v.tensor_copy(slot[:, :].rearrange("p (q i) -> p q i", i=4), bank[1][:, 0:4 * ROWS].rearrange("p (i q) -> p q i", i=4)))
                v.wait_ge(s_eT, 2)
                own.add(v.tensor_reduce(gmm[:, 0, :], bank[2][0:1, 0:ROWS].rearrange("p (g r) -> p g r", r=RPG), X, ALU.min))
                own.add(v.tensor_reduce(gmm[:, 1, :], bank[2][0:1, ROWS:2 * ROWS].rearrange("p (g r) -> p g r", r=RPG), X, ALU.max))
                own.wait()
                own.add(v.tensor_copy(gi[:, :], gmm[:, 0, :]))
                own.add(v.tensor_tensor(gmf[:, :], thr[:, 1:NG + 1], gmm[:, 0, :], ALU.subtract))
                own.add(v.tensor_tensor(gmm[:, 1, :], gmm[:, 1, :], gmm[:, 0, :], ALU.subtract))
                own.wait()
                own.add(v.tensor_reduce(flagf[:, 0:1], gmm[:, 1, :], X, ALU.max))
                own.add(v.tensor_reduce(flagf[:, 3:4], gmf[:, :], X, ALU.max))
                own.add(v.tensor_scalar(gblk[:, :], gi[:, :], 7, None, ALU.arith_shift_right))
                own.add(v.tensor_scalar(gmi[:, :], gi[:, :], P - 1, None, ALU.bitwise_and))
                own.wait()
                v.tensor_copy(gmf[:, :], gmi[:, :]).then_inc(s_gm, 1)
                v.sem_inc(s_idx, 1)

            moments(0)
            attention_weights()
            inverse(0)
            for t in range(NT):
                norm(t, t % 4)
                for i in range(1, XL):
                    if t == max(first_of[i] - 5, 3):
                        moments(i)
                    if t == first_of[i] - 1:
                        inverse(i)
                if t == EDGE_AT:
                    edge_rows()
                if t == NT - 5:
                    edge_chunks()
            v.wait_ge(s_xpc, NT)
            a_src = acc[:, 0:NT, D:D + H]
            a_dst = acc[:, 0:NT, D + H:D + 2 * H]
            own.add(v.tensor_reduce(r2[:, 0:1], a_src, XY, ALU.max))
            v.tensor_reduce(r2[:, 1:2], a_src, XY, ALU.min, negate=True).then_inc(s_r2, 1)
            own.wait()
            own.add(v.tensor_tensor(su[:, :, :], a_src, a_dst, ALU.add))
            own.wait()
            v.wait_ge(s_r2T, 1)
            own.add(v.tensor_reduce(g2[:, :], bank[5][0:2, 0:P], X, ALU.max))
            own.wait()
            v.tensor_scalar(dg2[:, :], ident[0:2, 0:2], g2[:, :], None, ALU.mult).then_inc(s_dg, 1)
            v.wait_ge(s_G, 1)
            own.add(v.tensor_copy(Gb[:, :], bank[6][:, 0:2]))
            own.add(v.scalar_tensor_tensor(su[:, :, :], su[:, :, :], 0.2, su[:, :, :], ALU.mult, ALU.max))
            own.wait()
            own.add(v.tensor_scalar(nG[:, 0:1], Gb[:, 0:1], -1.0, None, ALU.mult))
            own.add(v.tensor_scalar(nG[:, 1:2], Gb[:, 0:1], -0.2, None, ALU.mult))
            own.add(v.tensor_tensor(spr[:, :], Gb[0:1, 0:1], Gb[0:1, 1:2], ALU.add))
            own.add(v.tensor_scalar(uu[:, :, :], a_dst, Gb[:, 0:1], None, ALU.add))
            own.add(v.tensor_scalar(uv[:, :, 0:H], a_dst, Gb[:, 0:1], None, ALU.add))
            own.add(v.tensor_scalar(flagf[:, 0:1], flagf[:, 0:1], P - 0.5, None, ALU.is_gt))
            own.add(v.tensor_scalar(flagf[:, 3:4], flagf[:, 3:4], 0.0, None, ALU.is_gt))
            own.wait()
            own.add(v.tensor_scalar(flagf[:, 1:2], spr[:, :], SPREAD, None, ALU.is_gt))
            own.add(v.tensor_tensor(flagf[:, 2:3], flagf[:, 0:1], flagf[:, 3:4], ALU.max))
            own.wait()
            v.tensor_tensor(flag[:, :], flagf[:, 1:2], flagf[:, 2:3], ALU.max).then_inc(s_flag, 1)
            own.add(v.scalar_tensor_tensor(uu[:, :, :], uu[:, :, :], 0.2, uu[:, :, :], ALU.mult, ALU.max))
            own.wait()
            own.add(v.scalar_tensor_tensor(uv[:, :, H:2 * H], uv[:, :, 0:H], 0.2, uu[:, :, :], ALU.mult, ALU.subtract))
            own.add(v.tensor_tensor(su[:, :, :], su[:, :, :], uu[:, :, :], ALU.subtract))
            own.wait()
            v.tensor_tensor(uv[:, :, 0:H], uv[:, :, 0:H], uu[:, :, :], ALU.subtract).then_inc(s_ea, 1)
            v.wait_ge(s_gmT, 1)
            own.add(v.tensor_scalar(mhi[:, :], bank[3][:, 0:NG], lane[:, :], None, ALU.is_le))
            own.add(v.tensor_scalar(mlo[:, :], bank[3][:, 0:NG], lane[:, :], None, ALU.is_gt))
            own.wait()
            v.sem_inc(s_edge, 1)

            def slice_weights(own):
                v.wait_ge(s_wb, 32)
                v.wait_ge(s_ffn_load, 16 * 12)
                own.add(v.tensor_scalar(tmp8[:, :], tmp8[:, :], 0.1, 5.0, ALU.max, ALU.min))
                own.wait()
                own.add(v.reciprocal(itemp[:, :], tmp8[:, :]))
                own.wait()
                v.wait_ge(s_wl, 2)
                it2 = itemp[:, :].rearrange("p (j o) -> p o j", o=2)
                for k in range(2):
                    for o in range(2):
                        last = v.tensor_tensor(Wl[:, k, :].rearrange("p (j o g) -> p o j g", o=2, g=G)[:, o],
                                               bank[2 + k + 2 * o][:, 0:HG // 2].rearrange("p (j g) -> p j g", g=G),
                                               it2[:, o].unsqueeze(2).broadcast_to((P, FH // 2, G)), ALU.mult)
                    last.then_inc(s_wlc, 1)
                v.wait_ge(s_wl, 3)
                own.add(v.tensor_tensor(by_head(bl[:, :]), by_head(bank[0][0:1, :]), bsl[:, :].unsqueeze(1).broadcast_to((1, FH, G)), ALU.add))
                own.wait()
                own.add(v.tensor_tensor(by_head(bl[:, :]), by_head(bl[:, :]), over_slices(itemp[0:1, :]), ALU.mult))
                own.wait()
                for i in range(3):
                    r = 32 * i
                    own.add(v.tensor_copy(blb[r:r + 1, :], bl[:, :]))
                    own.wait()
                    if i < 2:
                        own.add(v.tensor_copy(blr[:, :], blb[r:r + 1, :]))
                        own.wait()
                        own.add(v.tensor_tensor(bl[:, :], bl[:, :], blr[:, :], ALU.subtract))
                        own.wait()
                v.sem_inc(s_wlc, 1)

            def a1(t):
                v.reciprocal(rden[:, :], flat(acc[:, bass.ds(t, 1), D:D + H])).then_inc(s_rd, 1)

            def a2(t):
                v.wait_ge(s_zz, t + 1)
                v.tensor_tensor(z[:, :], ELU[:, 0:D], gb[:, :], ALU.add).then_inc(s_z, 1)

            def a3(t, k, step):
                o = Own(v, s_ownA, t * 4 + step)
                xt = flat(xs[:, bass.ds(t, 1), :])
                if step == 0:
                    v.wait_ge(s_e, t + 1)
                    o.add(v.scalar_tensor_tensor(ELU[:, 0:D], z[:, :], 0.0, ELU[:, 0:D], ALU.max, ALU.add))
                    return
                o.wait()
                if step == 1:
                    o.add(v.scalar_tensor_tensor(xt, ELU[:, 0:D], -1.0, xt, ALU.add, ALU.add))
                if step == 2:
                    v.sem_inc(s_turn_v, 1)
                    o.add(v.bn_stats(stf[:, :], xt))
                if step == 3:
                    v.sem_inc(s_turn_v, 1)
                    o.add(v.bn_aggr(mvf[:, k, :], stf[:, :]))
                if step == 4:
                    v.tensor_scalar(mvf[:, k, 1:2], mvf[:, k, 1:2], EPS, None, ALU.add).then_inc(s_var2, 1)

            def b0(p, n):
                v.wait_ge(s_sd2, p + 1)
                v.reciprocal(sdf[:, 0:n], sdf[:, 0:n]).then_inc(s_rs, 1)
                v.wait_ge(s_rs, p + 1)

            def b1(t, b, k):
                if not isinstance(t, int) or t >= 2:
                    v.wait_ge(s_tokens, t - 1)
                v.tensor_scalar(xn[:, b, :], flat(xs[:, bass.ds(t, 1), :]), mvf[:, k, 0:1], sdf[:, k:k + 1],
                                ALU.subtract, ALU.mult).then_inc(s_n2, 1)

            def b2(t, LOGIT=LOGIT):
                v.wait_ge(s_logits, t + 1)
                v.tensor_reduce(mx[:, :], by_head(LOGIT[:, :]), X, ALU.max, negate=True).then_inc(s_logit_max, 1)

            def b3(t, LOGIT=LOGIT):
                o = Own(v, s_ownB, t)
                v.wait_ge(s_logit_exp, t + 1)
                o.add(v.reciprocal(sm[:, :], sm[:, :]))
                o.wait()
                if not (isinstance(t, int) and t == 0):
                    v.wait_ge(s_tokens, t)
                v.tensor_tensor(by_head(sw[:, :]), by_head(LOGIT[:, :]), over_slices(sm[:, :]), ALU.mult).then_inc(s_slice_w, 1)

            def quick():
                mine = Chain(v, s_quick)
                v.wait_ge(s_ex, 2)
                mine.add(v.tensor_copy(ab3[:, 0:NT, :, 0], ab[:, :, :]))
                mine.wait()
                mine.add(v.tensor_tensor(abr[:, :, :], ab[:, :, :], ab3[:, 0:NT, :, 0], ALU.subtract))
                mine.wait()
                mine.add(v.tensor_copy(ab3[:, 0:NT, :, 1], abr[:, :, :]))
                mine.wait()
                mine.add(v.tensor_tensor(abr[:, :, :], abr[:, :, :], ab3[:, 0:NT, :, 1], ALU.subtract))
                mine.wait()
                mine.add(v.tensor_copy(ab3[:, 0:NT, :, 2], abr[:, :, :]))
                v.wait_ge(s_table, 16 * NT)
                mine.add(v.tensor_copy(a_src, wself))
                xp4 = acc[:, 0:NT, 0:D].rearrange("p t (h c) -> p t h c", c=C)
                for t in range(NT):
                    mine.add(v.tensor_tensor(xp4[:, t], xp4[:, t], wself[:, t].unsqueeze(2).broadcast_to((P, H, C)), ALU.mult))
                mine.wait()
                slice_weights(mine)

                block_of = {}

                def hot(i, u):
                    g, b = NB * i + u, u % 2
                    first = isinstance(i, int) and g < 2
                    blk = v.value_load(gblk[0:1, bass.ds(g, 1)], min_val=0, max_val=NT - 1)
                    block_of[u] = blk
                    v.wait_ge(s_slots[b], 16 * (NB // 2 * i + u // 2 + 1))
                    if not first:
                        v.wait_ge(s_lookup, g - 1)
                    v.tensor_scalar(tsa[:, b, :], abs3(blk), mhi[:, bass.ds(g, 1)], None, ALU.mult).then_inc(s_ta, 1)
                    v.tensor_scalar(ot[:, b, :], db[:, b, :], lane[:, :], None, ALU.is_equal).then_inc(s_onehot, 1)
                    v.wait_ge(s_ta, g + 1)
                    v.scalar_tensor_tensor(tsl[:, b, :], abs3(blk + 1), mlo[:, bass.ds(g, 1)], tsa[:, b, :],
                                           ALU.mult, ALU.add).then_inc(s_tsl, 1)

                def hot2(i, u):
                    g, b = NB * i + u, u % 2
                    if not (isinstance(i, int) and g < 2):
                        v.wait_ge(s_sums, g - 1)
                    v.tensor_tensor(oh[:, b, :, :], cols[:, :].unsqueeze(1).broadcast_to((P, CPG, P)),
                                    slot[:, bass.ds(g * CPG, CPG)].unsqueeze(2).broadcast_to((P, CPG, P)), ALU.is_equal).then_inc(s_onehot_e, 1)

                def weigh(i, u, t=None):
                    g, b = NB * i + u, u % 2
                    v.wait_ge(s_lookup, g + 1)
                    v.tensor_reduce(abe[:, b, :, :], LOOK[:, 0:CPG * 24].rearrange("p (c e k) -> p c e k", c=CPG, k=3), X, ALU.add).then_inc(s_abe, 1)
                    v.wait_ge(s_rates, g + 1)
                    v.wait_ge(s_abe, g + 1)
                    v.tensor_tensor(we[:, b, :, :], abe[:, b, :, :], ee[:, b, :, :], ALU.mult).then_inc(s_we, 1)
                    v.wait_ge(s_we, g + 1)
                    wp = WP[:, b * 32:b * 32 + CPG * H].rearrange("p (c h) -> p c h", h=H)
                    v.tensor_tensor(gt[:, u, :, D:D + H], we[:, b, :, 0:H], we[:, b, :, H:2 * H], ALU.max).then_inc(s_weights, 1)
                    v.tensor_tensor(wp, we[:, b, :, 0:H], we[:, b, :, H:2 * H], ALU.max).then_inc(s_wp, 1)
                    v.wait_ge(s_wp, g + 1)
                    for c in range(CPG - ACH):
                        r = gt[:, u, c, 0:D].rearrange("p (h k) -> p h k", k=C)
                        last = v.tensor_tensor(r, r, wp[:, c, :].unsqueeze(2).broadcast_to((P, H, C)), ALU.mult)
                        if c == CPG - ACH - 1:
                            last.then_inc(s_scaled, 1)
                        if t is not None:
                            a3(t, u // 2, c)

                def merge(i, u, blk=None):
                    g, b = NB * i + u, u % 2
                    if blk is None:
                        blk = v.value_load(gblk[0:1, bass.ds(g, 1)], min_val=0, max_val=NT - 1)
                    v.wait_ge(s_sums, g + 1)
                    if not (isinstance(i, int) and g == 0):
                        v.wait_ge(s_merged, g)
                    for m, k in ((mhi, 0), (mlo, 1)):
                        a = flat(acc[:, bass.ds(blk + k, 1), 0:D + H])
                        last = v.scalar_tensor_tensor(a, SUMS[:, 0:D + H], m[:, bass.ds(g, 1)], a, ALU.mult, ALU.add)
                    last.then_inc(s_merged, 1)

                def iteration(i):
                    for u in range(NB):
                        more = not (isinstance(i, int) and i == NI - 1 and u == NB - 1)
                        t = TPI * (i - TL) + u // 2
                        k = u // 2
                        if u % 2 == 0 and runs(t):
                            a1(t)
                        if more:
                            hot(i + (u + 1) // NB, (u + 1) % NB)
                        if u % 2 == 0 and runs(t - 3):
                            b3(t - 3)
                        weigh(i, u, t if u % 2 == 1 and runs(t) else None)
                        if u % 2 == 0 and runs(t):
                            a2(t)
                        if u > 0 or not (isinstance(i, int) and i == 0):
                            merge(i - (u == 0), (u - 1) % NB, block_of[u - 1] if u >= 2 else None)
                        if u % 2 == 0 and runs(t - 2):
                            if k == 0:
                                b0(i - TL - 1, 2)
                            b1(t - 2, k, k)
                        if more:
                            hot2(i + (u + 1) // NB, (u + 1) % NB)
                        if u % 2 == 1 and runs(t - 2):
                            b2(t - 2)
                hot(0, 0)
                hot2(0, 0)
                for i in range(TL + 2):
                    iteration(i)
                with v.Fori(TL + 2, NI - 1) as i:
                    iteration(i)
                iteration(NI - 1)
                t = IN_LOOP
                b3(t - 3)
                a1(t)
                b0(NI - TL - 1, 2)
                b1(t - 2, 0, 0)
                a2(t)
                merge(NI - 1, NB - 1)
                v.wait_ge(s_merged, NG)
                b2(t - 2, logits_of(t - 2))
                b1(t - 1, 1, 1)
                for step in range(5):
                    a3(t, 0, step)
                a1(t + 1)
                a2(t + 1)
                b3(t - 2, logits_of(t - 2))
                b2(t - 1, logits_of(t - 1))
                for step in range(5):
                    a3(t + 1, 1, step)
                a1(t + 2)
                a2(t + 2)
                b3(t - 1, logits_of(t - 1))
                for step in range(5):
                    a3(t + 2, 2, step)
                b0(NI - TL, 3)
                b1(t, 0, 0)
                b1(t + 1, 1, 1)
                b2(t, logits_of(t))
                b3(t, logits_of(t))
                b2(t + 1, logits_of(t + 1))
                b1(t + 2, 0, 2)
                b3(t + 1, logits_of(t + 1))
                b2(t + 2, logits_of(t + 2))
                b3(t + 2, logits_of(t + 2))

            def general_path():
                K1, K2, KB = 4, 9, 11
                PB = (K1 + K2) * NCH + KB
                xown = Own(v, x_own, 0)
                slice_weights(Chain(v, x_prep))

                def at(base, n):
                    xown.base, xown.k = base, 0

                v.wait_ge(s_table, 16 * NT)
                v.tensor_copy(xnode[:, :], lane[:, :]).then_inc(x_own, 1)
                v.sem_inc(x_go, 1)

                def arrive(q):
                    v.wait_ge(x_got, q + 1)
                    v.wait_ge(x_db, 16 * (q + 1))
                    return v.tensor_scalar(xhot, xdst, xnode[:, :], None, ALU.is_equal)

                def leaky(a):
                    xown.add(v.tensor_scalar(xs2[:, :], a, 0.2, None, ALU.mult))
                    xown.wait()
                    xown.add(v.tensor_tensor(a, a, xs2[:, :], ALU.max))
                    xown.wait()

                with v.Fori(0, NT) as j:
                    acc_j = flat(acc[:, bass.ds(j, 1), :])
                    a_s = acc_j[:, D:D + H]
                    B0 = j * PB + 1
                    at(B0, 2)
                    xown.wait()
                    xown.add(v.tensor_copy(xmax[:, :], a_s))
                    xown.add(v.tensor_copy(xtbl[:, 0:H], acc_j[:, D + H:D + 2 * H]))
                    xown.wait()
                    v.sem_inc(x_turn_v, 1)
                    with v.Fori(0, NCH) as k:
                        q = 2 * NCH * j + k
                        at(B0 + 2 + K1 * k, K1)
                        v.wait_ge(x_go, q + 1)
                        xown.add(arrive(q))
                        for h in range(H):
                            last = v.tensor_scalar(xdiag[:, h, :], ident[:, :], xrow[:, D + h:D + h + 1], None, ALU.mult)
                        last.then_inc(x_diag, 1)
                        xown.wait()
                        xown.add(v.tensor_scalar(xpen, xhot, -1.0, BIG, ALU.add, ALU.mult))
                        xown.wait()
                        v.wait_ge(x_bc, NCH * j + k + 1)
                        xown.add(v.tensor_tensor(xtmp, bank[0][:, 0:H * P].rearrange("p (h e) -> p h e", h=H),
                                                 xpen.unsqueeze(1).broadcast_to((P, H, P)), ALU.add))
                        xown.wait()
                        xown.add(v.tensor_reduce(xred[:, :], xtmp, X, ALU.max))
                        xown.wait()
                        v.tensor_tensor(xmax[:, :], xmax[:, :], xred[:, :], ALU.max).then_inc(x_go, 1)
                        assert xown.k == K1
                    v.wait_ge(x_go, 2 * NCH * j + NCH + 1)
                    at(B0 + 2 + K1 * NCH, KB - 2)
                    xown.add(v.tensor_tensor(xtbl[:, H:2 * H], xmax[:, :], xtbl[:, 0:H], ALU.add))
                    xown.add(v.tensor_tensor(xs1[:, :], a_s, xtbl[:, 0:H], ALU.add))
                    xown.wait()
                    leaky(xtbl[:, H:2 * H])
                    leaky(xs1[:, :])
                    v.tensor_tensor(xs1[:, :], xs1[:, :], xtbl[:, H:2 * H], ALU.subtract).then_inc(x_self, 1)
                    v.wait_ge(x_selfe, j + 1)
                    for h in range(H):
                        last = v.tensor_scalar(acc_j[:, h * C:(h + 1) * C], acc_j[:, h * C:(h + 1) * C], xw[:, h:h + 1], None, ALU.mult)
                    xown.add(last)
                    xown.add(v.tensor_copy(acc_j[:, D:D + H], xw[:, :]))
                    xown.wait()
                    v.sem_inc(x_turn_v, 1)
                    with v.Fori(0, NCH) as k:
                        q = 2 * NCH * j + NCH + k
                        at(B0 + 2 + K1 * NCH + 8 + K2 * k, K2)
                        v.wait_ge(x_go, q + 1)
                        arrive(q).then_inc(x_hot, 1)
                        v.wait_ge(x_lk, NCH * j + k + 1)
                        xown.add(v.tensor_copy(xhotT, bank[2][:, 0:P]))
                        xown.add(v.tensor_tensor(xs1[:, :], xrow[:, D:D + H], bank[1][:, 0:H], ALU.add))
                        xown.wait()
                        leaky(xs1[:, :])
                        xown.add(v.tensor_tensor(xs1[:, :], xs1[:, :], bank[1][:, H:2 * H], ALU.subtract))
                        xown.wait()
                        v.tensor_scalar(xs1[:, :], xs1[:, :], 0.0, None, ALU.min).then_inc(x_arg, 1)
                        v.wait_ge(x_exp, NCH * j + k + 1)
                        for h in range(H):
                            xown.add(v.tensor_scalar(xrow[:, h * C:(h + 1) * C], xrow[:, h * C:(h + 1) * C], xw[:, h:h + 1], None, ALU.mult))
                        v.tensor_copy(xrow[:, D:D + H], xw[:, :]).then_inc(x_rows, 1)
                        v.wait_ge(x_sum, NCH * j + k + 1)
                        v.tensor_tensor(acc_j[:, 0:D + H], acc_j[:, 0:D + H], bank[3][:, 0:D + H], ALU.add).then_inc(x_go, 1)
                        assert xown.k == K2
                    v.wait_ge(x_go, 2 * NCH * (j + 1) + 1)
                    at(B0 + 2 + K1 * NCH + 8 + K2 * NCH, 1)
                    xown.add(v.tensor_scalar(xnode[:, :], xnode[:, :], float(P), None, ALU.add))

            v.wait_ge(s_gm, 1)
            v.wait_ge(s_flag, 1)
            general = v.value_load(flag[0:1, 0:1], min_val=0, max_val=1)
            with v.If(general == 0):
                quick()
            with v.Else():
                general_path()

                def tiles(p, n):
                    for k in range(n):
                        a1(2 * p + k)
                        a2(2 * p + k)
                        for step in range(5):
                            a3(2 * p + k, k, step)
                    b0(p, n)
                    for k in range(n):
                        b1(2 * p + k, k, k)
                        b2(2 * p + k)
                        b3(2 * p + k)
                tiles(0, 2)
                with v.Fori(1, NT // 2) as i:
                    tiles(i, 2)
                tiles(NT // 2, 1)

            v.wait_ge(s_swc, NT)
            own.add(v.tensor_reduce(nrm[:, 0, :], nrt[:, :, :].rearrange("p t j -> p j t"), X, ALU.add))
            own.wait()
            own.add(v.tensor_scalar(nrm[:, 1, :], nrm[:, 0, :], 1e-5, None, ALU.add))
            own.wait()
            own.add(v.reciprocal(nrm[:, 1, :], nrm[:, 1, :]))
            own.wait()
            v.tensor_tensor(tokn[:, :, D], nrm[:, 0, :], nrm[:, 1, :], ALU.mult).then_inc(s_tokn, 1)
            v.wait_ge(s_tokens, NT)
            for j in range(2):
                last = v.tensor_scalar(tokn[:, j, 0:D], TOK[j], nrm[:, 1, j:j + 1], None, ALU.mult)
            last.then_inc(s_tokn, 1)
            v.wait_ge(s_att_pe, 2)
            v.tensor_copy(tokT[:, 1, :], bank[5][:, :]).then_inc(s_att_dve, 1)
            v.wait_ge(s_att_pe, 5)
            v.tensor_copy(stT[:, HG // 2:HG], bank[3][0:G, 0:HG // 2]).then_inc(s_att_dve, 1)
            v.wait_ge(s_att_pe, 7)
            v.tensor_copy(qkv[:, 1, :], bank[2][0:G, :]).then_inc(s_att_dve, 1)
            v.wait_ge(s_att_pe, 9)
            own.add(v.tensor_reduce(amx[:, :], by_head(bank[0][0:G, :]), X, ALU.max))
            own.wait()
            v.tensor_tensor(by_head(at_s[:, :]), by_head(bank[0][0:G, :]), over_slices(amx[:, :]), ALU.subtract).then_inc(s_att_dve, 1)
            v.wait_ge(s_att_pe, 14)
            v.tensor_copy(at_T[:, :], bank[1][0:G, :]).then_inc(s_att_dve, 1)
            v.wait_ge(s_att_pe, 15)
            v.reciprocal(rz[:, :], bank[2][:, 0:4]).then_inc(s_att_dve, 1)
            v.wait_ge(s_att_dve, 6)
            v.wait_ge(s_att_pe, 16)
            v.scalar_tensor_tensor(Z[0:G, 0, :], bank[6][0:G, 0:D], rz[0:G, 0:1], bo[0:G, :], ALU.mult, ALU.add)
            v.tensor_scalar(Z[G:P, 0, :], bank[6][G:P, 0:D], rz[G:P, 0:1], None, ALU.mult)
            v.tensor_scalar(Z[:, 1, :], bank[6][:, D:2 * D], rz[:, 1:2], None, ALU.mult).then_inc(s_att_dve, 1)

            def ffn2(t, b, earlier, n=P):
                v.wait_ge(s_product, t + 1)
                if not isinstance(t, int) or t >= 2:
                    v.wait_ge(s_stored[b], 16 * earlier)
                v.tensor_tensor(y[0:n, b, :], bank[b][0:n, 0:D], flat(xs[0:n, bass.ds(t, 1), :]), ALU.add).then_inc(s_result, 1)

            for t in range(2):
                ffn2(t, t, 0)
            with v.Fori(1, NT // 2) as i:
                for u in range(2):
                    ffn2(2 * i + u, u, i)
            ffn2(NT - 1, 0, NT // 2, LAST)


_INS = ['x', 'src', 'dst', 'L0_gnn_W', 'L0_gnn_att_src', 'L0_gnn_att_dst', 'L0_gnn_bias', 'L0_ffn_W_fx', 'L0_ffn_b_fx',
        'L0_ffn_W_x', 'L0_ffn_b_x', 'L0_ffn_W_slice', 'L0_ffn_b_slice', 'L0_ffn_W_q', 'L0_ffn_W_k', 'L0_ffn_W_v',
        'L0_ffn_W_out', 'L0_ffn_b_out', 'L0_ffn_temperature']


def kernel(**inputs):
    import numpy as _np
    import concourse.bacc as _bacc
    from concourse import mybir as _mybir
    from concourse.bass_utils import run_bass_kernel_spmd as _run

    nc = _bacc.Bacc("TRN2", target_bir_lowering=False, num_devices=1)
    arrays, args = {}, []
    for name in _INS:
        a = _np.ascontiguousarray(inputs[name])
        arrays[f"in_{name}_dram"] = a
        args.append(nc.dram_tensor(f"in_{name}_dram", a.shape, _mybir.dt.from_np(a.dtype), kind="ExternalInput").ap())
    x = inputs['x']
    args.append(nc.dram_tensor("out_0_dram", tuple(x.shape), _mybir.dt.float32, kind="ExternalOutput").ap())
    build(nc, *args)
    r = _run(nc, [arrays], core_ids=[0])
    return r.results[0]["out_0_dram"]
```
